# Optimizing a Trainium2 kernel written in Bass

```python
import numpy as np
import jax
import jax.numpy as jnp

def _softmax(x, axis=-1):
    return jax.nn.softmax(x, axis=axis)

def _gelu(x):
    return jax.nn.gelu(x, approximate=True)

def _silu(x):
    return jax.nn.silu(x)

def _sigmoid(x):
    return jax.nn.sigmoid(x)

def _layernorm(x, axis=-1, eps=1e-05):
    m = jnp.mean(x, axis=axis, keepdims=True)
    v = jnp.var(x, axis=axis, keepdims=True)
    return (x - m) / jnp.sqrt(v + eps)

def _scatter_add(tgt, idx, src, axis=0):
    return tgt.at[idx].add(src)

def _segment_sum(src, seg, n):
    return jax.ops.segment_sum(src, seg, n)
kernel_name = 'mk_vit_tower_d2_tok_img768_r4_6b2b8d'

def setup_inputs(seed: int=0):
    np.random.seed(seed)
    _w = jnp.asarray

    def _rec_inputs():
        import jax
        import jax.numpy as jnp
        _rk = jax.random.key(seed)
        x = -0.000356955 + 1 * jax.random.normal(jax.random.fold_in(_rk, 1), (8, 3, 128, 128), jnp.float32)
        return x
    x = _rec_inputs()

    def _L0_tok_setup():
        import jax, jax.numpy as jnp
        import numpy as np
        PATCH = 16
        EMBED = 192
        IN_DIM = PATCH * PATCH * 3

        def extract_patches(x, p):
            B, C, H, Wd = x.shape
            h, w = (H // p, Wd // p)
            xr = x.reshape(B, C, h, p, w, p)
            xr = xr.transpose(0, 2, 4, 3, 5, 1)
            return xr.reshape(B, h * w, p * p * C)
        key = jax.random.key(seed)
        kx, kw, kb = jax.random.split(key, 3)
        x = jax.random.normal(kx, (128, 3, 224, 224), dtype=jnp.float32)
        bound = 1.0 / np.sqrt(IN_DIM)
        W = jax.random.uniform(kw, (EMBED, IN_DIM), jnp.float32, -bound, bound)
        b = jax.random.uniform(kb, (EMBED,), jnp.float32, -bound, bound)
        return {'x': x, 'W': W, 'b': b}
    _L0_tok_all = _L0_tok_setup()
    _L0_tok_in = {k: v for k, v in _L0_tok_all.items() if k in ('W', 'b')}
    del _L0_tok_all

    def _L0_attn_setup():
        import math
        import jax, jax.numpy as jnp
        import numpy as np
        H, D_MODEL, D_K, D_V, SEQ, BATCH = (12, 192, 64, 64, 512, 4)
        key = jax.random.key(seed)
        k1, k2, k3, k4, k5 = jax.random.split(key, 5)
        s = math.sqrt(0.02)
        return {'residual': jax.random.normal(k1, (BATCH, SEQ, D_MODEL), dtype=jnp.float32), 'W_Q': jax.random.normal(k2, (H, D_MODEL, D_K), dtype=jnp.float32) * s, 'W_K': jax.random.normal(k3, (H, D_MODEL, D_K), dtype=jnp.float32) * s, 'W_V': jax.random.normal(k4, (H, D_MODEL, D_V), dtype=jnp.float32) * s, 'W_O': jax.random.normal(k5, (H * D_V, D_MODEL), dtype=jnp.float32) * s}
    _L0_attn_all = _L0_attn_setup()
    _L0_attn_in = {k: v for k, v in _L0_attn_all.items() if k in ('W_Q', 'W_K', 'W_V', 'W_O')}
    del _L0_attn_all

    def _L0_ffn_setup():
        import jax, jax.numpy as jnp
        import numpy as np
        B, T, C = (4, 512, 192)
        E, K = (8, 2)

        def _mlp(x, wfc, wproj):
            h = jnp.square(jax.nn.relu(x @ wfc))
            return h @ wproj
        key = jax.random.key(seed)
        ks = jax.random.split(key, 6)
        s = 0.02
        return {'x': jax.random.normal(ks[0], (B, T, C), jnp.float32), 'w_fc_sh': jax.random.normal(ks[1], (C, C), jnp.float32) * s, 'w_proj_sh': jax.random.normal(ks[2], (C, C), jnp.float32) * s, 'w1': jax.random.normal(ks[3], (E, C, C), jnp.float32) * s, 'w2': jax.random.normal(ks[4], (E, C, C), jnp.float32) * s, 'router_w': jax.random.normal(ks[5], (E, C), jnp.float32) * s, 'balance_bias': jnp.zeros((E,), jnp.float32)}
    _L0_ffn_all = _L0_ffn_setup()
    _L0_ffn_in = {k: v for k, v in _L0_ffn_all.items() if k in ('w_fc_sh', 'w_proj_sh', 'w1', 'w2', 'router_w', 'balance_bias')}
    del _L0_ffn_all

    def _L1_attn_setup():
        import jax, jax.numpy as jnp
        import numpy as np
        DIM, D_STATE, D_CONV, EXPAND = (192, 16, 4, 2)
        D_INNER = EXPAND * DIM
        DT_RANK = (DIM + 15) // 16
        B_SZ, L_SZ = (4, 1024)

        def _causal_depthwise_conv(x, w, b):
            k = w.shape[-1]
            xp = jnp.pad(x, ((0, 0), (0, 0), (k - 1, 0)))
            y = jax.lax.conv_general_dilated(xp, w, window_strides=(1,), padding='VALID', dimension_numbers=('NCH', 'OIH', 'NCH'), feature_group_count=x.shape[1])
            return y + b[None, :, None]

        def _selective_scan(u, dt, A, B, C, D):
            b, d, l = u.shape
            n = A.shape[1]

            def step(h, inp):
                u_t, dt_t, B_t, C_t = inp
                dA = jnp.exp(dt_t[..., None] * A)
                h = h * dA + dt_t[..., None] * B_t[:, None, :] * u_t[..., None]
                y = jnp.einsum('bdn,bn->bd', h, C_t)
                return (h, y)
            h0 = jnp.zeros((b, d, n), u.dtype)
            xs = (jnp.moveaxis(u, 2, 0), jnp.moveaxis(dt, 2, 0), jnp.moveaxis(B, 2, 0), jnp.moveaxis(C, 2, 0))
            _, ys = jax.lax.scan(step, h0, xs)
            y = jnp.moveaxis(ys, 0, 2)
            return y + u * D[None, :, None]

        def _one_direction(xz, conv_w, conv_b, x_proj_w, dt_w, dt_b, A_log, D):
            d_inner = xz.shape[1] // 2
            xin, z = (xz[:, :d_inner], xz[:, d_inner:])
            xc = jax.nn.silu(_causal_depthwise_conv(xin, conv_w, conv_b))
            x_dbl = jnp.einsum('bdl,cd->bcl', xc, x_proj_w)
            dt_r = x_dbl[:, :DT_RANK]
            Bm = x_dbl[:, DT_RANK:DT_RANK + D_STATE]
            Cm = x_dbl[:, DT_RANK + D_STATE:]
            dt = jax.nn.softplus(jnp.einsum('brl,dr->bdl', dt_r, dt_w) + dt_b[None, :, None])
            A = -jnp.exp(A_log)
            y = _selective_scan(xc, dt, A, Bm, Cm, D)
            return y * jax.nn.silu(z)
        key = jax.random.key(seed)
        ks = jax.random.split(key, 20)
        s = 0.02
        d = {}
        d['x'] = jax.random.normal(ks[0], (B_SZ, L_SZ, DIM), jnp.float32)
        d['in_proj_w'] = jax.random.normal(ks[1], (2 * D_INNER, DIM), jnp.float32) * s
        d['out_proj_w'] = jax.random.normal(ks[2], (DIM, D_INNER), jnp.float32) * s
        d['conv1d_w'] = jax.random.normal(ks[3], (D_INNER, 1, D_CONV), jnp.float32) * s
        d['conv1d_bias'] = jax.random.normal(ks[4], (D_INNER,), jnp.float32) * s
        d['x_proj_w'] = jax.random.normal(ks[5], (DT_RANK + 2 * D_STATE, D_INNER), jnp.float32) * s
        d['dt_proj_w'] = jax.random.normal(ks[6], (D_INNER, DT_RANK), jnp.float32) * s
        d['dt_proj_bias'] = jax.random.normal(ks[7], (D_INNER,), jnp.float32) * 0.1 - 4.0
        d['A_log'] = jnp.log(jax.random.uniform(ks[8], (D_INNER, D_STATE), jnp.float32, 1.0, 16.0))
        d['D'] = jax.random.normal(ks[9], (D_INNER,), jnp.float32) * 0.1 + 1.0
        d['conv1d_w_b'] = jax.random.normal(ks[10], (D_INNER, 1, D_CONV), jnp.float32) * s
        d['conv1d_bias_b'] = jax.random.normal(ks[11], (D_INNER,), jnp.float32) * s
        d['x_proj_w_b'] = jax.random.normal(ks[12], (DT_RANK + 2 * D_STATE, D_INNER), jnp.float32) * s
        d['dt_proj_w_b'] = jax.random.normal(ks[13], (D_INNER, DT_RANK), jnp.float32) * s
        d['dt_proj_bias_b'] = jax.random.normal(ks[14], (D_INNER,), jnp.float32) * 0.1 - 4.0
        d['A_log_b'] = jnp.log(jax.random.uniform(ks[15], (D_INNER, D_STATE), jnp.float32, 1.0, 16.0))
        d['D_b'] = jax.random.normal(ks[16], (D_INNER,), jnp.float32) * 0.1 + 1.0
        return d
    _L1_attn_all = _L1_attn_setup()
    _L1_attn_in = {k: v for k, v in _L1_attn_all.items() if k in ('in_proj_w', 'out_proj_w', 'conv1d_w', 'conv1d_bias', 'x_proj_w', 'dt_proj_w', 'dt_proj_bias', 'A_log', 'D', 'conv1d_w_b', 'conv1d_bias_b', 'x_proj_w_b', 'dt_proj_w_b', 'dt_proj_bias_b', 'A_log_b', 'D_b')}
    del _L1_attn_all

    def _L1_ffn_setup():
        import jax, jax.numpy as jnp
        import numpy as np
        DIM = 192
        FF = 768
        E = 8
        K = 2
        H = 12
        HD = DIM // H
        LN_EPS = 1e-05

        def _layernorm(x, g, b):
            m = jnp.mean(x, axis=-1, keepdims=True)
            v = jnp.var(x, axis=-1, keepdims=True)
            return (x - m) * jax.lax.rsqrt(v + LN_EPS) * g + b

        def _attention(x, Wqkv, Wproj):
            B, T, D = x.shape
            qkv = (x @ Wqkv).reshape(B, T, 3, H, HD)
            q, k, v = (qkv[:, :, 0], qkv[:, :, 1], qkv[:, :, 2])
            scores = jnp.einsum('bqhd,bkhd->bhqk', q, k) * jnp.float32(HD) ** (-0.5)
            attn = jax.nn.softmax(scores, axis=-1)
            out = jnp.einsum('bhqk,bkhd->bqhd', attn, v).reshape(B, T, D)
            return out @ Wproj

        def _moe(x, Wrouter, W1, W2):
            B, T, D = x.shape
            xf = x.reshape(-1, D)
            N = xf.shape[0]
            logits = xf @ Wrouter
            topk_w, topk_idx = jax.lax.top_k(logits, K)
            topk_w = jax.nn.softmax(topk_w.astype(jnp.float32), axis=-1).astype(x.dtype)
            we = jnp.zeros((N, E), x.dtype).at[jnp.arange(N)[:, None], topk_idx].add(topk_w)

            def body(acc, expert):
                W1e, W2e, we_e = expert
                h = jax.nn.gelu(xf @ W1e, approximate=False)
                return (acc + we_e[:, None] * (h @ W2e), None)
            out, _ = jax.lax.scan(body, jnp.zeros_like(xf), (W1, W2, we.T))
            return out.reshape(B, T, D)
        key = jax.random.key(seed)
        ks = jax.random.split(key, 7)
        B, T = (4, 256)
        init = lambda k, shape, fan: jax.random.normal(k, shape, jnp.float32) * fan ** (-0.5)
        return {'x': jax.random.normal(ks[0], (B, T, DIM), jnp.float32), 'Wqkv': init(ks[1], (DIM, 3 * DIM), DIM), 'Wproj': init(ks[2], (DIM, DIM), DIM), 'Wrouter': init(ks[3], (DIM, E), DIM), 'W1': init(ks[4], (E, DIM, FF), DIM), 'W2': init(ks[5], (E, FF, DIM), FF), 'ln1_g': jnp.ones((DIM,), jnp.float32), 'ln1_b': jnp.zeros((DIM,), jnp.float32), 'ln2_g': jnp.ones((DIM,), jnp.float32), 'ln2_b': jnp.zeros((DIM,), jnp.float32)}
    _L1_ffn_all = _L1_ffn_setup()
    _L1_ffn_in = {k: v for k, v in _L1_ffn_all.items() if k in ('Wqkv', 'Wproj', 'Wrouter', 'W1', 'W2', 'ln1_g', 'ln1_b', 'ln2_g', 'ln2_b')}
    del _L1_ffn_all
    return {'x': x, 'L0_tok_W': _L0_tok_in['W'], 'L0_tok_b': _L0_tok_in['b'], 'L0_attn_W_Q': _L0_attn_in['W_Q'], 'L0_attn_W_K': _L0_attn_in['W_K'], 'L0_attn_W_V': _L0_attn_in['W_V'], 'L0_attn_W_O': _L0_attn_in['W_O'], 'L0_ffn_w_fc_sh': _L0_ffn_in['w_fc_sh'], 'L0_ffn_w_proj_sh': _L0_ffn_in['w_proj_sh'], 'L0_ffn_w1': _L0_ffn_in['w1'], 'L0_ffn_w2': _L0_ffn_in['w2'], 'L0_ffn_router_w': _L0_ffn_in['router_w'], 'L0_ffn_balance_bias': _L0_ffn_in['balance_bias'], 'L1_attn_in_proj_w': _L1_attn_in['in_proj_w'], 'L1_attn_out_proj_w': _L1_attn_in['out_proj_w'], 'L1_attn_conv1d_w': _L1_attn_in['conv1d_w'], 'L1_attn_conv1d_bias': _L1_attn_in['conv1d_bias'], 'L1_attn_x_proj_w': _L1_attn_in['x_proj_w'], 'L1_attn_dt_proj_w': _L1_attn_in['dt_proj_w'], 'L1_attn_dt_proj_bias': _L1_attn_in['dt_proj_bias'], 'L1_attn_A_log': _L1_attn_in['A_log'], 'L1_attn_D': _L1_attn_in['D'], 'L1_attn_conv1d_w_b': _L1_attn_in['conv1d_w_b'], 'L1_attn_conv1d_bias_b': _L1_attn_in['conv1d_bias_b'], 'L1_attn_x_proj_w_b': _L1_attn_in['x_proj_w_b'], 'L1_attn_dt_proj_w_b': _L1_attn_in['dt_proj_w_b'], 'L1_attn_dt_proj_bias_b': _L1_attn_in['dt_proj_bias_b'], 'L1_attn_A_log_b': _L1_attn_in['A_log_b'], 'L1_attn_D_b': _L1_attn_in['D_b'], 'L1_ffn_Wqkv': _L1_ffn_in['Wqkv'], 'L1_ffn_Wproj': _L1_ffn_in['Wproj'], 'L1_ffn_Wrouter': _L1_ffn_in['Wrouter'], 'L1_ffn_W1': _L1_ffn_in['W1'], 'L1_ffn_W2': _L1_ffn_in['W2'], 'L1_ffn_ln1_g': _L1_ffn_in['ln1_g'], 'L1_ffn_ln1_b': _L1_ffn_in['ln1_b'], 'L1_ffn_ln2_g': _L1_ffn_in['ln2_g'], 'L1_ffn_ln2_b': _L1_ffn_in['ln2_b']}

def reference(x, L0_tok_W, L0_tok_b, L0_attn_W_Q, L0_attn_W_K, L0_attn_W_V, L0_attn_W_O, L0_ffn_w_fc_sh, L0_ffn_w_proj_sh, L0_ffn_w1, L0_ffn_w2, L0_ffn_router_w, L0_ffn_balance_bias, L1_attn_in_proj_w, L1_attn_out_proj_w, L1_attn_conv1d_w, L1_attn_conv1d_bias, L1_attn_x_proj_w, L1_attn_dt_proj_w, L1_attn_dt_proj_bias, L1_attn_A_log, L1_attn_D, L1_attn_conv1d_w_b, L1_attn_conv1d_bias_b, L1_attn_x_proj_w_b, L1_attn_dt_proj_w_b, L1_attn_dt_proj_bias_b, L1_attn_A_log_b, L1_attn_D_b, L1_ffn_Wqkv, L1_ffn_Wproj, L1_ffn_Wrouter, L1_ffn_W1, L1_ffn_W2, L1_ffn_ln1_g, L1_ffn_ln1_b, L1_ffn_ln2_g, L1_ffn_ln2_b):
    import jax
    import jax.numpy as jnp

    def _L0_tok_ref(x, W, b):
        import jax, jax.numpy as jnp
        import numpy as np
        PATCH = 16
        EMBED = 192
        IN_DIM = PATCH * PATCH * 3

        def extract_patches(x, p):
            B, C, H, Wd = x.shape
            h, w = (H // p, Wd // p)
            xr = x.reshape(B, C, h, p, w, p)
            xr = xr.transpose(0, 2, 4, 3, 5, 1)
            return xr.reshape(B, h * w, p * p * C)
        patches = extract_patches(x, PATCH)
        return jnp.einsum('bnd,ed->bne', patches, W) + b

    def _L0_attn_ref(residual, W_Q, W_K, W_V, W_O):
        import math
        import jax, jax.numpy as jnp
        import numpy as np
        H, D_MODEL, D_K, D_V, SEQ, BATCH = (12, 192, 64, 64, 512, 4)
        B, S, _ = residual.shape
        Q = jnp.einsum('hmk,bsm->hbsk', W_Q, residual)
        K = jnp.einsum('hmk,bsm->hbsk', W_K, residual)
        V = jnp.einsum('hmv,bsm->hbsv', W_V, residual)
        QK = jnp.einsum('hbqk,hbsk->hbqs', Q, K)
        causal = jnp.triu(jnp.ones((S, S), dtype=bool), k=1)
        mask = jnp.where(causal, -jnp.inf, 0.0).astype(QK.dtype)
        soft = jax.nn.softmax((QK + mask) / math.sqrt(D_K), axis=-1)
        attn = jnp.einsum('hbqs,hbsv->hbqv', soft, V)
        multi_head = jnp.transpose(attn, (1, 2, 0, 3)).reshape(B, S, -1)
        return jnp.einsum('nd,bqn->bqd', W_O, multi_head)

    def _L0_ffn_ref(x, w_fc_sh, w_proj_sh, w1, w2, router_w, balance_bias):
        import jax, jax.numpy as jnp
        import numpy as np
        B, T, C = (4, 512, 192)
        E, K = (8, 2)

        def _mlp(x, wfc, wproj):
            h = jnp.square(jax.nn.relu(x @ wfc))
            return h @ wproj
        Bx, Tx, Cx = x.shape
        shared = _mlp(x, w_fc_sh, w_proj_sh)
        xf = x.reshape(-1, Cx)
        logits = xf.astype(jnp.float32) @ router_w.T
        scores = jax.nn.sigmoid(logits)
        _, idx = jax.lax.top_k(scores + balance_bias, K)
        tw = jnp.take_along_axis(scores, idx, axis=-1)
        tw = tw / (tw.sum(-1, keepdims=True) + 1e-20)
        combine = (jax.nn.one_hot(idx, E, dtype=tw.dtype) * tw[..., None]).sum(1)
        h = jnp.square(jax.nn.relu(jnp.einsum('nc,ech->neh', xf, w1)))
        y = jnp.einsum('neh,ehc->nec', h, w2)
        routed = jnp.einsum('nec,ne->nc', y, combine)
        return shared + routed.reshape(Bx, Tx, Cx)

    def _L1_attn_ref(x, in_proj_w, out_proj_w, conv1d_w, conv1d_bias, x_proj_w, dt_proj_w, dt_proj_bias, A_log, D, conv1d_w_b, conv1d_bias_b, x_proj_w_b, dt_proj_w_b, dt_proj_bias_b, A_log_b, D_b):
        import jax, jax.numpy as jnp
        import numpy as np
        DIM, D_STATE, D_CONV, EXPAND = (192, 16, 4, 2)
        D_INNER = EXPAND * DIM
        DT_RANK = (DIM + 15) // 16
        B_SZ, L_SZ = (4, 1024)

        def _causal_depthwise_conv(x, w, b):
            k = w.shape[-1]
            xp = jnp.pad(x, ((0, 0), (0, 0), (k - 1, 0)))
            y = jax.lax.conv_general_dilated(xp, w, window_strides=(1,), padding='VALID', dimension_numbers=('NCH', 'OIH', 'NCH'), feature_group_count=x.shape[1])
            return y + b[None, :, None]

        def _selective_scan(u, dt, A, B, C, D):
            b, d, l = u.shape
            n = A.shape[1]

            def step(h, inp):
                u_t, dt_t, B_t, C_t = inp
                dA = jnp.exp(dt_t[..., None] * A)
                h = h * dA + dt_t[..., None] * B_t[:, None, :] * u_t[..., None]
                y = jnp.einsum('bdn,bn->bd', h, C_t)
                return (h, y)
            h0 = jnp.zeros((b, d, n), u.dtype)
            xs = (jnp.moveaxis(u, 2, 0), jnp.moveaxis(dt, 2, 0), jnp.moveaxis(B, 2, 0), jnp.moveaxis(C, 2, 0))
            _, ys = jax.lax.scan(step, h0, xs)
            y = jnp.moveaxis(ys, 0, 2)
            return y + u * D[None, :, None]

        def _one_direction(xz, conv_w, conv_b, x_proj_w, dt_w, dt_b, A_log, D):
            d_inner = xz.shape[1] // 2
            xin, z = (xz[:, :d_inner], xz[:, d_inner:])
            xc = jax.nn.silu(_causal_depthwise_conv(xin, conv_w, conv_b))
            x_dbl = jnp.einsum('bdl,cd->bcl', xc, x_proj_w)
            dt_r = x_dbl[:, :DT_RANK]
            Bm = x_dbl[:, DT_RANK:DT_RANK + D_STATE]
            Cm = x_dbl[:, DT_RANK + D_STATE:]
            dt = jax.nn.softplus(jnp.einsum('brl,dr->bdl', dt_r, dt_w) + dt_b[None, :, None])
            A = -jnp.exp(A_log)
            y = _selective_scan(xc, dt, A, Bm, Cm, D)
            return y * jax.nn.silu(z)
        xz = jnp.einsum('bld,ed->bel', x, in_proj_w)
        out_f = _one_direction(xz, conv1d_w, conv1d_bias, x_proj_w, dt_proj_w, dt_proj_bias, A_log, D)
        out_r = _one_direction(xz[:, :, ::-1], conv1d_w_b, conv1d_bias_b, x_proj_w_b, dt_proj_w_b, dt_proj_bias_b, A_log_b, D_b)
        out = out_f + out_r[:, :, ::-1]
        return jnp.einsum('bdl,od->blo', out, out_proj_w)

    def _L1_ffn_ref(x, Wqkv, Wproj, Wrouter, W1, W2, ln1_g, ln1_b, ln2_g, ln2_b):
        import jax, jax.numpy as jnp
        import numpy as np
        DIM = 192
        FF = 768
        E = 8
        K = 2
        H = 12
        HD = DIM // H
        LN_EPS = 1e-05

        def _layernorm(x, g, b):
            m = jnp.mean(x, axis=-1, keepdims=True)
            v = jnp.var(x, axis=-1, keepdims=True)
            return (x - m) * jax.lax.rsqrt(v + LN_EPS) * g + b

        def _attention(x, Wqkv, Wproj):
            B, T, D = x.shape
            qkv = (x @ Wqkv).reshape(B, T, 3, H, HD)
            q, k, v = (qkv[:, :, 0], qkv[:, :, 1], qkv[:, :, 2])
            scores = jnp.einsum('bqhd,bkhd->bhqk', q, k) * jnp.float32(HD) ** (-0.5)
            attn = jax.nn.softmax(scores, axis=-1)
            out = jnp.einsum('bhqk,bkhd->bqhd', attn, v).reshape(B, T, D)
            return out @ Wproj

        def _moe(x, Wrouter, W1, W2):
            B, T, D = x.shape
            xf = x.reshape(-1, D)
            N = xf.shape[0]
            logits = xf @ Wrouter
            topk_w, topk_idx = jax.lax.top_k(logits, K)
            topk_w = jax.nn.softmax(topk_w.astype(jnp.float32), axis=-1).astype(x.dtype)
            we = jnp.zeros((N, E), x.dtype).at[jnp.arange(N)[:, None], topk_idx].add(topk_w)

            def body(acc, expert):
                W1e, W2e, we_e = expert
                h = jax.nn.gelu(xf @ W1e, approximate=False)
                return (acc + we_e[:, None] * (h @ W2e), None)
            out, _ = jax.lax.scan(body, jnp.zeros_like(xf), (W1, W2, we.T))
            return out.reshape(B, T, D)
        x = x + _attention(_layernorm(x, ln1_g, ln1_b), Wqkv, Wproj)
        x = x + _moe(_layernorm(x, ln2_g, ln2_b), Wrouter, W1, W2)
        return x
    h = _L0_tok_ref(x, L0_tok_W, L0_tok_b)
    h = h + _L0_attn_ref(_layernorm(h, axis=-1), L0_attn_W_Q, L0_attn_W_K, L0_attn_W_V, L0_attn_W_O)
    h = h + _L0_ffn_ref(_layernorm(h, axis=-1), L0_ffn_w_fc_sh, L0_ffn_w_proj_sh, L0_ffn_w1, L0_ffn_w2, L0_ffn_router_w, L0_ffn_balance_bias)
    h = h + _L1_attn_ref(_layernorm(h, axis=-1), L1_attn_in_proj_w, L1_attn_out_proj_w, L1_attn_conv1d_w, L1_attn_conv1d_bias, L1_attn_x_proj_w, L1_attn_dt_proj_w, L1_attn_dt_proj_bias, L1_attn_A_log, L1_attn_D, L1_attn_conv1d_w_b, L1_attn_conv1d_bias_b, L1_attn_x_proj_w_b, L1_attn_dt_proj_w_b, L1_attn_dt_proj_bias_b, L1_attn_A_log_b, L1_attn_D_b)
    h = h + _L1_ffn_ref(_layernorm(h, axis=-1), L1_ffn_Wqkv, L1_ffn_Wproj, L1_ffn_Wrouter, L1_ffn_W1, L1_ffn_W2, L1_ffn_ln1_g, L1_ffn_ln1_b, L1_ffn_ln2_g, L1_ffn_ln2_b)
    return h

_drawn_inputs = setup_inputs


def setup_inputs(seed=0):
    import zlib

    import numpy as np

    out = dict(_drawn_inputs(seed))
    spreads = {'L0_ffn_balance_bias': (0.0, 0.8),
     'L1_ffn_ln1_g': (1.0, 0.6),
     'L1_ffn_ln1_b': (0.0, 1.797),
     'L1_ffn_ln2_g': (1.0, 0.6),
     'L1_ffn_ln2_b': (0.0, 2.0)}
    factors = {'L0_ffn_w_fc_sh': 8.0,
     'L0_ffn_w_proj_sh': 8.0,
     'L0_ffn_w1': 8.0,
     'L0_ffn_w2': 8.0,
     'L0_ffn_router_w': 8.0,
     'L1_attn_in_proj_w': 8.0,
     'L1_attn_out_proj_w': 8.0,
     'L1_attn_conv1d_w': 8.0,
     'L1_attn_conv1d_bias': 8.0,
     'L1_attn_x_proj_w': 8.0,
     'L1_attn_dt_proj_w': 8.0,
     'L1_attn_dt_proj_bias': 8.0,
     'L1_attn_A_log': 8.0,
     'L1_attn_D': 8.0,
     'L1_attn_conv1d_w_b': 8.0,
     'L1_attn_conv1d_bias_b': 8.0,
     'L1_attn_x_proj_w_b': 8.0,
     'L1_attn_dt_proj_bias_b': 8.0,
     'L1_attn_A_log_b': 8.0,
     'L1_attn_D_b': 8.0,
     'L1_ffn_Wrouter': 3.616,
     'L1_ffn_W1': 3.494,
     'L1_ffn_W2': 3.087}
    for name, (base, spread) in spreads.items():
        noise = np.random.default_rng([zlib.crc32(name.encode()), seed]).standard_normal(out[name].shape)
        drawn = base * np.exp(spread * noise) if base else spread * noise
        out[name] = jnp.asarray(drawn.astype(out[name].dtype))
    for name, factor in factors.items():
        out[name] = (out[name] * factor).astype(out[name].dtype)
    return out
```

```python
import concourse.bass as bass
from concourse import mybir
from contextlib import ExitStack

BATCH, TOKENS_PER_IMAGE, DIM = 8, 64, 192
TOKENS = BATCH * TOKENS_PER_IMAGE
TILES = TOKENS // 128
PATCH_K = 768 // 128
HEADS = 12
PAIRS = HEADS // 2
LN_EPS = 1e-5
EXPERTS = 8
INNER, STATE, RANK, TAPS = 384, 16, 12, 4
CTILES = INNER // 128
UNITS = 2 * CTILES
STEP = 16
COMBOS = 8
PART_U = [c % 3 for c in range(COMBOS)]
PART_B = [c // 3 for c in range(COMBOS)]
MASKED = -1.0e30


def build_tower(nc, io, out):
    F32 = mybir.dt.float32
    BF16 = mybir.dt.bfloat16
    ALU = mybir.AluOpType
    ACT = mybir.ActivationFunctionType
    AX = mybir.AxisListType

    c_dram = nc.dram_tensor("c_scratch", (2, BATCH, STATE, 64), F32, kind="Internal").ap()
    u_dram = nc.dram_tensor("u_scratch", (UNITS, 3, 128, 512), BF16, kind="Internal").ap()

    ctx = ExitStack()
    with ctx:
        def sb(name, shape, dt=F32):
            return ctx.enter_context(nc.sbuf_tensor(name, shape, dt))

        def sem(name):
            return ctx.enter_context(nc.semaphore(name))

        PS = ctx.enter_context(nc.psum_tensor("PS", [128, 8, 512], F32))

        ident = sb("ident", [128, 128])
        h = sb("h", [128, TILES, DIM])
        xn = sb("xn", [128, TILES, 256])
        xta = sb("xta", [128, TOKENS])
        xtb = sb("xtb", [128, TOKENS])
        stats = sb("stats", [128, TILES, 6])
        moments = sb("moments", [128, TILES, 2])
        rstd = sb("rstd", [128, TILES])
        neg_half = sb("neg_half", [128, TILES])

        expert_ids = sb("expert_ids", [128, TILES, EXPERTS])

        ARENA = 49900
        arena = sb("arena", [128, ARENA])

        def carve(at, *shape, dt=F32):
            n = 1
            for s in shape:
                n *= s
            cols = n if dt == F32 else n // 2
            assert at[0] + cols <= at[1], (at, shape)
            v = arena[:, at[0]:at[0] + cols]
            at[0] += cols
            if dt != F32:
                v = v.bitcast(dt)
            names = "abcde"[:len(shape)]
            if len(shape) > 1:
                v = v.rearrange(f"p ({' '.join(names)}) -> p {' '.join(names)}",
                                **{names[i]: shape[i] for i in range(1, len(shape))})
            return v

        at = [0, ARENA]
        patches = carve(at, PATCH_K, TOKENS)
        tok_w = carve(at, PATCH_K, DIM)
        tok_b = carve(at, DIM)
        wqk = carve(at, PAIRS, 3, 128)
        wv = carve(at, 2, HEADS * 64)
        wo = carve(at, PAIRS, DIM)
        causal = carve(at, 64)
        vtok = carve(at, TILES, HEADS * 64)
        qT = carve(at, 2, TOKENS)
        kT = carve(at, 2, TOKENS)
        prob = carve(at, 2, TILES, 2, 64)
        rowmax = carve(at, 2, 8)
        rowsum = carve(at, 2, 8)
        probT = carve(at, TILES, 128)
        attnT = carve(at, PAIRS, TOKENS)

        fw1 = carve(at, 2, 3, 128)
        fw2 = carve(at, 2, 2, DIM)
        frelu = carve(at, 2, 2, TOKENS)
        fhid = carve(at, 2, 2, TOKENS)
        frw = carve(at, 2, EXPERTS)
        fbias = carve(at, EXPERTS)
        fscore = carve(at, TILES, EXPERTS)
        fpick = carve(at, TILES, EXPERTS)
        ftop = carve(at, TILES, 8)
        fidx = carve(at, TILES, 8).bitcast(mybir.dt.uint32)
        fidxf = carve(at, TILES, 2)
        fhot = carve(at, 2, TILES, EXPERTS)
        fsum = carve(at, TILES)
        fwt = carve(at, TILES, 1 + EXPERTS)

        at[0] = max(at[0], 29900)
        fresh = at[0]
        decay = carve(at, 2, 4, STATE, 64)
        mark = at[0]
        at = [fresh, mark]
        xpad = carve(at, CTILES, BATCH, 70)
        softx = carve(at, 2, TOKENS)
        softe = carve(at, 2, TOKENS)
        softw = carve(at, 2, TOKENS)
        softl = carve(at, 2, TOKENS)
        at = [mark, ARENA]
        m_in = carve(at, CTILES, 3, 128)
        m_xp = carve(at, 2, CTILES, 44)
        m_dtw = carve(at, 2, INNER)
        m_out = carve(at, CTILES, DIM)
        m_conv = carve(at, 2, CTILES, TAPS)
        m_convb = carve(at, 2, CTILES)
        m_dtb = carve(at, 2, CTILES)
        m_a = carve(at, 2, CTILES, STATE)
        m_d = carve(at, 2, CTILES)
        m_mask = carve(at, STEP)
        zgate = carve(at, CTILES, TOKENS)
        xc = carve(at, 2, CTILES, TOKENS)
        dts = carve(at, 2, CTILES, TOKENS)
        bts = carve(at, 2, TILES, STATE)
        at = [0, fresh]
        hbuf = carve(at, 2, 2, STATE, 64)
        mark = at[0]
        at = [0, mark]
        m_sel = carve(at, 8, 3, 128, dt=BF16)
        du = carve(at, 2, TOKENS)
        dr = carve(at, 2, TOKENS)
        at = [mark, fresh]
        bd = carve(at, 2, 32, STEP, STATE, dt=BF16)
        lw = carve(at, 2, 8, TILES, 128, dt=BF16)
        cb = carve(at, BATCH, STATE, 64)
        yf = carve(at, CTILES, TOKENS)
        xdbl = carve(at, 2, TOKENS)
        uparts = carve(at, 2, 3, TILES, 128, dt=BF16)
        bparts = carve(at, 2, 3, TILES, STATE, dt=BF16)
        bsel = carve(at, 2, TILES, 8, STATE, dt=BF16)
        yr = carve(at, 2, 256)

        QUADS = HEADS // 4
        HCHUNKS = 6
        at = [4096, 8192]
        q_wqk = carve(at, QUADS, 3, 128)
        q_wv = carve(at, 2, HEADS * 32)
        q_wo = carve(at, QUADS, DIM)
        gw1_0 = carve(at, 3, 3, 128)
        at = [8192, 16384]
        gw1 = [gw1_0, carve(at, 3, 3, 128)]
        gw2 = [carve(at, HCHUNKS, DIM) for _ in range(2)]
        ln_gb = [carve(at, DIM) for _ in range(4)]
        grw = carve(at, 2, EXPERTS)
        at = [16384, fresh]
        q_v = carve(at, TILES, HEADS * 32)
        q_qT = carve(at, 2, TOKENS)
        q_kT = carve(at, 2, TOKENS)
        q_prob = carve(at, 2, 4, 2, 2, 64)
        q_probT = carve(at, 4, 2, 128)
        q_attnT = carve(at, QUADS, TOKENS)
        q_max = carve(at, 2, 16)
        q_sum = carve(at, 2, 16)
        gtop = carve(at, TILES, 8)
        gidx = carve(at, TILES, 8).bitcast(mybir.dt.uint32)
        gidxf = carve(at, TILES, 2)
        glog = carve(at, TILES, EXPERTS)
        ghot = carve(at, 2, TILES, EXPERTS)
        gpair = carve(at, 2, TILES)
        gwt = carve(at, TILES, EXPERTS)
        at = [fresh, fresh + 8192]
        x4 = carve(at, TILES, DIM)
        x5 = carve(at, TILES, DIM)
        ghid = carve(at, 2, HCHUNKS, TOKENS)

        s_const = sem("const_loaded")
        s_tokw = sem("tok_weights_loaded")
        s_patch = [sem(f"patches_loaded{k}") for k in range(PATCH_K)]
        s_tok = sem("tok_done")
        s_h = sem("h_written")
        s_nh = sem("neg_half_set")
        s_w0 = sem("attn0_weights_loaded")
        s_out = sem("out_stored")
        s_st = sem("ln_stats")
        s_mo = sem("ln_moments")
        s_rs = sem("ln_rstd")
        s_xn = sem("ln_normed")
        s_xt = sem("ln_transposed")
        s_xta = sem("ln_xta")
        s_xtb = sem("ln_xtb")
        TURN = [0, 1, 2, None, 3, 4]

        a_v = sem("attn0_v_done")
        a_va = sem("attn0_v_copied_by_scalar")
        a_vd = sem("attn0_v_copied_by_vector")
        a_proj = sem("attn0_qk_done")
        a_q = sem("attn0_q_copied")
        a_k = sem("attn0_k_copied")
        a_s = sem("attn0_scores_done")
        a_mask = sem("attn0_masked")
        a_max = sem("attn0_max_done")
        a_sub = sem("attn0_shifted")
        a_exp = sem("attn0_exp_done")
        a_sum = sem("attn0_sum_done")
        a_rec = sem("attn0_recip_done")
        a_p = sem("attn0_probs_ready")
        a_pt = sem("attn0_probs_transposed")
        a_ptc = sem("attn0_probsT_copied")
        a_pv = sem("attn0_pv_done")
        a_oe = sem("attn0_even_copied")
        a_oo = sem("attn0_odd_copied")
        a_o = sem("attn0_out_done")

        f_w1 = [sem(f"moe0_w1_loaded{n}") for n in range(2)]
        f_w2 = [sem(f"moe0_w2_loaded{n}") for n in range(2)]
        f_rw = sem("moe0_router_loaded")
        f_lg = sem("moe0_logits_done")
        f_sig = sem("moe0_sigmoid_done")
        f_rt = sem("moe0_routing_steps")
        f_hid = sem("moe0_hidden_done")
        f_relu = sem("moe0_relu_done")
        f_sqa = sem("moe0_hidden_a_squared")
        f_sqb = sem("moe0_hidden_b_squared")
        f_y = sem("moe0_y_done")
        f_acc = sem("moe0_y_added")
        s_ids = sem("expert_ids_made")

        q_w = sem("attn1_weights_loaded")
        q_vd = sem("attn1_v_done")
        q_va = sem("attn1_v_copied_by_scalar")
        q_vv = sem("attn1_v_copied_by_vector")
        q_proj = sem("attn1_qk_done")
        q_q = sem("attn1_q_copied")
        q_k = sem("attn1_k_copied")
        q_s = sem("attn1_scores_done")
        q_mx = sem("attn1_max_done")
        q_sub = sem("attn1_shifted")
        q_exp = sem("attn1_exp_done")
        q_sm = sem("attn1_sum_done")
        q_rec = sem("attn1_recip_done")
        q_p = sem("attn1_probs_ready")
        q_pt = sem("attn1_probs_transposed")
        q_ptc = [sem(f"attn1_probsT_copied{n}") for n in range(2)]
        q_pv = sem("attn1_pv_done")
        q_oe = sem("attn1_even_copied")
        q_oo = sem("attn1_odd_copied")
        q_o = sem("attn1_out_done")
        s_x5 = sem("x5_written")
        s_hx = sem("x5_added_to_h")
        s_aff = [sem(f"ln{n}_affine_steps") for n in range(4, 6)]
        g_w1 = [sem(f"moe1_w1_loaded{n}") for n in range(2)]
        g_w2 = [sem(f"moe1_w2_loaded{n}") for n in range(2)]
        g_gb = sem("norm_gains_loaded")
        g_lg = sem("moe1_logits_done")
        g_rt = sem("moe1_routing_steps")
        g_d = sem("moe1_top_difference")
        g_e = sem("moe1_top_exp")
        g_hid = sem("moe1_hidden_done")
        g_act = sem("moe1_gelu_done")
        g_y = sem("moe1_y_done")
        g_acc = sem("moe1_y_added")

        m_w = sem("ssm_weights_loaded")
        m_sell = sem("ssm_selector_loaded")
        m_pad = sem("ssm_pads_zeroed")
        m_xz = sem("ssm_xz_done")
        m_x = sem("ssm_x_copied")
        m_z = sem("ssm_z_gated")
        m_cv = sem("ssm_conv_taps")
        m_silu = sem("ssm_conv_silu")
        m_xd = sem("ssm_xdbl_done")
        m_xdc = sem("ssm_xdbl_copied")
        m_cst = sem("ssm_c_stored")
        m_cld = [sem(f"ssm_c_loaded{q}") for q in range(4)]
        m_bt = sem("ssm_b_transposed")
        m_bs = sem("ssm_b_split_steps")
        m_bsl = sem("ssm_b_selected")
        m_bsc = sem("ssm_b_selected_copied")
        m_bd = sem("ssm_b_blocks")
        m_dt = sem("ssm_dt_raw_done")
        m_sx = sem("ssm_softplus_x")
        m_sab = sem("ssm_softplus_abs")
        m_se = sem("ssm_softplus_exp")
        m_sw = sem("ssm_softplus_w")
        m_sr = sem("ssm_softplus_rest")
        m_sm = sem("ssm_softplus_max")
        m_sl = sem("ssm_softplus_ln")
        m_s1 = sem("ssm_softplus_sum")
        m_dts = sem("ssm_dt_ready")
        m_du = sem("ssm_dtu_ready")
        m_dut = sem("ssm_dtu_transposed")
        m_p1 = sem("ssm_dtu_part1")
        m_r1 = sem("ssm_dtu_rest")
        m_p2 = sem("ssm_dtu_part2")
        m_p3 = sem("ssm_dtu_part3")
        m_ust = [sem(f"ssm_dtu_stored{n}") for n in range(2)]
        m_lw = sem("ssm_dtu_loaded")
        m_ea = sem("ssm_a_exp")
        m_na = sem("ssm_a_negated")
        m_zero = sem("ssm_decay_starts_zeroed")
        m_dec = sem("ssm_decay_ready")
        m_b = sem("ssm_inputs_formed")
        m_scan = sem("ssm_scanned")
        m_mul = sem("ssm_times_c")
        m_y = sem("ssm_y_summed")
        m_post = sem("ssm_y_taken")
        m_yr = sem("ssm_yr_made")
        m_sum = sem("ssm_directions_added")
        m_g = sem("ssm_gated")
        m_o = sem("ssm_out_done")

        block = ctx.enter_context(nc.Block())

        @block.sync
        def _(sp):
            sp.dma_start(tok_w, io["tok_w"]).then_inc(s_tokw, 16)
            for k in range(PATCH_K):
                sp.dma_start(patches[:, k, :], io["patches"][:, k, :]).then_inc(s_patch[k], 16)
            sp.dma_start(wv, io["a0_wv"]).then_inc(s_w0, 16)
            sp.dma_start(wqk, io["a0_wqk"]).then_inc(s_w0, 16)
            sp.dma_start(wo, io["a0_wo"]).then_inc(s_w0, 16)
            sp.dma_start(frw, io["m0_router"]).then_inc(f_rw, 16)
            sp.dma_start(fbias, io["m0_bias"].partition_broadcast(128)).then_inc(f_rw, 16)
            for e in range(1 + EXPERTS):
                if e >= 2:
                    sp.wait_ge(f_hid, e - 1)
                sp.dma_start(fw1[:, e % 2], io["m0_w1"][e]).then_inc(f_w1[e % 2], 16)
                if e >= 2:
                    sp.wait_ge(f_y, e - 1)
                sp.dma_start(fw2[:, e % 2], io["m0_w2"][e]).then_inc(f_w2[e % 2], 16)
            for n, (to, name) in enumerate(((m_in, "m_in"), (m_xp, "m_xp"), (m_dtw[0:RANK], "m_dtw"), (m_out, "m_out"),
                                            (m_conv, "m_conv"), (m_convb, "m_convb"), (m_dtb, "m_dtb"),
                                            (m_a, "m_a"), (m_d, "m_d"), (m_mask, "m_mask"))):
                sp.dma_start(to, io[name]).then_inc(m_w, 16)
            sp.wait_ge(s_xn, 8 * 3)
            sp.dma_start(m_sel.bitcast(mybir.dt.uint16), io["m_sel"]).then_inc(m_sell, 16)
            for d in range(2):
                sp.wait_ge(m_xdc, d + 1)
                sp.dma_start(c_dram[d].rearrange("b n t -> n b t"),
                             xdbl[RANK + STATE:44, d, :].rearrange("n (b t) -> n b t", t=64)).then_inc(m_cst, 16)

            def load_c(d, q):
                if d == 1:
                    sp.wait_ge(m_mul, 8 * (CTILES - 1) + 2 * q + 2)
                sp.dma_start(cb[:, 2 * q:2 * q + 2].rearrange("p b n t -> p (b n t)"),
                             c_dram[d, 2 * q:2 * q + 2].rearrange("b n t -> (b n t)").partition_broadcast(128)
                             ).then_inc(m_cld[q], 16)

            def load_u(u):
                if u >= 2:
                    sp.wait_ge(m_b, 8 * (u - 1))
                if u >= 1:
                    sp.wait_ge(m_lw, 16 * COMBOS * u)
                sp.wait_ge(m_ust[u % 2], 48 * (u // 2 + 1))
                rows = u_dram[u].rearrange("i (g t) x -> i t g x", t=STEP)
                for c in range(COMBOS):
                    sp.dma_start(lw[c * STEP:(c + 1) * STEP, u % 2].rearrange("p g t d -> p g (t d)"),
                                 rows[PART_U[c]]).then_inc(m_lw, 16)

            def store_u(u):
                for i in range(3):
                    sp.wait_ge((m_p1, m_p2, m_p3)[i], u + 1)
                    sp.dma_start(u_dram[u, i], uparts[:, u % 2, i].rearrange("p t d -> p (t d)")).then_inc(m_ust[u % 2], 16)

            sp.wait_ge(m_cst, 32)
            for q in range(4):
                load_c(0, q)
            store_u(0)
            load_u(0)
            store_u(1)
            load_u(1)
            for u in range(2, UNITS):
                store_u(u)
            for u in range(2, UNITS):
                load_u(u)
                if u == 3:
                    for q in range(4):
                        load_c(1, q)
            sp.dma_start(q_wqk, io["a1_wqk"]).then_inc(q_w, 16)
            sp.dma_start(q_wv, io["a1_wv"]).then_inc(q_w, 16)
            sp.dma_start(q_wo, io["a1_wo"]).then_inc(q_w, 16)
            sp.dma_start(gw1[0], io["m1_w1"][0]).then_inc(g_w1[0], 16)
            sp.wait_ge(m_b, 8 * UNITS)
            for n, name in enumerate(("ln1_g", "ln1_b", "ln2_g", "ln2_b")):
                sp.dma_start(ln_gb[n], io[name].partition_broadcast(128)).then_inc(g_gb, 16)
            sp.dma_start(grw, io["m1_router"]).then_inc(g_gb, 16)
            for e in range(EXPERTS):
                if e >= 1:
                    if e >= 2:
                        sp.wait_ge(g_hid, 3 * (e - 1))
                    sp.dma_start(gw1[e % 2], io["m1_w1"][e]).then_inc(g_w1[e % 2], 16)
                if e >= 2:
                    sp.wait_ge(g_y, e - 1)
                sp.dma_start(gw2[e % 2], io["m1_w2"][e]).then_inc(g_w2[e % 2], 16)
            sp.wait_ge(g_acc, 8 + TILES * EXPERTS)
            sp.dma_start(out.rearrange("(t p) d -> p t d", p=128), h[:]).then_inc(s_out, 16)
            sp.wait_ge(s_out, 16)

        @block.gpsimd
        def _(pool):
            pool.memset(neg_half[:], -0.5).then_inc(s_nh, 1)
            pool.wait_ge(s_nh, 1)

            def ln_pool(n):
                pool.wait_ge(s_mo, TILES * (n + 1))
                pool.tensor_scalar(rstd[:], moments[:, :, 1], LN_EPS, None, ALU.add).then_inc(s_rs, 1)
                pool.wait_ge(s_rs, 2 * n + 1)
                pool.tensor_tensor(rstd[:], rstd[:], neg_half[:], ALU.pow).then_inc(s_rs, 1)

            pool.iota(expert_ids[:], [[0, TILES], [1, EXPERTS]], channel_multiplier=0,
                      allow_small_or_imprecise_dtypes=True).then_inc(s_ids, 1)
            pool.memset(fwt[:, :, 0:1], 1.0).then_inc(s_ids, 1)
            ln_pool(0)
            ln_pool(1)
            pool.memset(xpad, 0.0).then_inc(m_pad, 1)
            ln_pool(2)

            for u in range(UNITS):
                p = u % 2
                pool.wait_ge(m_sl, u + 1)
                pool.wait_ge(m_sr, u + 1)
                pool.tensor_tensor(softl[:, p], softl[:, p], softe[:, p], ALU.subtract).then_inc(m_s1, 1)
                pool.wait_ge(m_s1, u + 1)
                pool.wait_ge(m_sm, u + 1)
                pool.tensor_tensor(dts[:, u // 3, u % 3, :], softl[:, p], softx[:, p], ALU.add).then_inc(m_dts, 1)

            pool.wait_ge(m_dts, UNITS)
            pool.memset(decay[:, :, :, :, 0:1].rearrange("p a b n o -> p (a b n) o"), 0.0).then_inc(m_zero, 1)

            for B in range(8 * UNITS):
                u, b = B // 8, B % 8
                hb = hbuf[:, (b // 2) % 2, b % 2].rearrange("p n t -> p (n t)")
                if b % 2 == 0:
                    pool.wait_ge(m_cld[b // 2], 16 * (u // 3 + 1))
                pool.wait_ge(m_scan, B + 1)
                pool.tensor_tensor(hb, hb, cb[:, b].rearrange("p n t -> p (n t)"), ALU.mult).then_inc(m_mul, 1)
            ln_pool(3)
            ln_pool(4)
            ln_pool(5)
            for t in range(TILES):
                pool.wait_ge(s_x5, t + 1)
                pool.tensor_tensor(h[:, t, :], h[:, t, :], x5[:, t, :], ALU.add).then_inc(s_hx, 1)

        @block.scalar
        def _(act):
            act.dma_start(ident[:], io["ident"]).then_inc(s_const, 16)
            act.dma_start(causal, io["causal"]).then_inc(s_const, 16)
            act.dma_start(tok_b, io["tok_b"].partition_broadcast(128)).then_inc(s_const, 16)

            def ln_act(n, bank):
                act.wait_ge(s_xt, TILES * (TURN[n] + 1))
                act.activation(xta[:], PS[:, bank, :], ACT.Copy).then_inc(s_xta, 1)

            ln_act(0, 6)
            for r in range(2):
                act.wait_ge(a_v, r + 1)
                act.activation(vtok[:, 2 * r, :].rearrange("p (a n) -> p a n", a=2),
                               PS[:, 4 * r:4 * r + 2, 0:384], ACT.Copy).then_inc(a_va, 1)

            def q_copy(j):
                act.wait_ge(a_proj, j + 1)
                if j >= 2:
                    act.wait_ge(a_s, j - 1)
                act.activation(qT[:, j % 2, :], PS[:, 0, :], ACT.Copy).then_inc(a_q, 1)

            def exps(j):
                act.wait_ge(a_sub, j + 1)
                v = prob[:, j % 2].rearrange("p t a k -> p (t a k)")
                act.activation(v, v, ACT.Exp, scale=0.125).then_inc(a_exp, 1)

            def probT_copy(j):
                act.wait_ge(a_pt, j + 1)
                act.activation(probT.rearrange("p t n -> p (t n)"), PS[:, 4, :], ACT.Copy).then_inc(a_ptc, 1)

            def even_copy(j):
                act.wait_ge(a_pv, j + 1)
                act.activation(attnT[:, j, :].rearrange("p (t a q) -> p a t q", a=2, q=64)[:, 0],
                               PS[:, 5, 0:256].rearrange("p (t q) -> p t q", q=64), ACT.Copy).then_inc(a_oe, 1)

            q_copy(0)
            q_copy(1)
            exps(0)
            for j in range(PAIRS):
                if j + 2 < PAIRS:
                    q_copy(j + 2)
                probT_copy(j)
                if j + 1 < PAIRS:
                    exps(j + 1)
                even_copy(j)

            ln_act(1, 6)
            act.sem_inc(f_relu, 2)
            act.wait_ge(f_lg, 1)
            act.activation(fscore.rearrange("p t e -> p (t e)"), PS[:, 6, 0:TILES * EXPERTS],
                           ACT.Sigmoid).then_inc(f_sig, 1)

            def moe0_relu(e, p):
                act.wait_ge(f_hid, e + 1)
                for i in range(2):
                    act.activation(frelu[:, p, i, :], PS[:, 2 * p + i, :], ACT.Relu).then_inc(f_relu, 1)
                act.wait_ge(f_relu, 2 * e + 4)
                act.activation(fhid[:, p, 1, :], frelu[:, p, 1, :], ACT.Square).then_inc(f_sqb, 1)

            moe0_relu(0, 0)
            with act.Fori(0, EXPERTS // 2) as i:
                moe0_relu(2 * i + 1, 1)
                moe0_relu(2 * i + 2, 0)

            ln_act(2, 6)
            for c in range(CTILES):
                k = 2 * (c % 2)
                act.wait_ge(m_xz, c + 1)
                if c == 0:
                    act.wait_ge(m_pad, 1)
                act.activation(xpad[:, c, :, 3:67], PS[:, k, :].rearrange("p (b t) -> p b t", t=64),
                               ACT.Copy).then_inc(m_x, 1)
                act.activation(zgate[:, c], PS[:, k + 1, :], ACT.Silu).then_inc(m_z, 1)
            for u in range(UNITS):
                act.wait_ge(m_cv, 12 * (u // 3) + 9 + u % 3 + 1)
                act.activation(xc[:, u // 3, u % 3], xc[:, u // 3, u % 3], ACT.Silu).then_inc(m_silu, 1)
                if u % 3 == 2:
                    act.wait_ge(m_xd, u // 3 + 1)
                    act.activation(xdbl[0:44, u // 3, :], PS[0:44, 4 + u // 3, :], ACT.Copy).then_inc(m_xdc, 1)
            act.wait_ge(m_w, 160)
            act.activation(m_a.rearrange("p d c n -> p (d c n)"), m_a.rearrange("p d c n -> p (d c n)"),
                           ACT.Exp).then_inc(m_ea, 1)

            def softplus_exp(u):
                p = u % 2
                act.wait_ge(m_dt, u + 1)
                if u >= 2:
                    act.wait_ge(m_dts, u - 1)
                act.activation(softx[:, p], PS[:, 6 + p, :], ACT.Identity,
                               bias=m_dtb[:, u // 3, u % 3:u % 3 + 1]).then_inc(m_sx, 1)
                act.wait_ge(m_sx, u + 1)
                act.activation(softe[:, p], softx[:, p], ACT.Abs).then_inc(m_sab, 1)
                act.wait_ge(m_sab, u + 1)
                act.activation(softe[:, p], softe[:, p], ACT.Exp, scale=-1.0).then_inc(m_se, 1)

            def softplus_ln(u):
                act.wait_ge(m_sw, u + 1)
                act.activation(softl[:, u % 2], softw[:, u % 2], ACT.Ln).then_inc(m_sl, 1)

            def part1(u):
                act.wait_ge(m_dut, u + 1)
                if u >= 2:
                    act.wait_ge(m_ust[u % 2], 48 * (u // 2))
                act.activation(uparts[:, u % 2, 0].rearrange("p t d -> p (t d)"), PS[:, 2 + u % 2, :],
                               ACT.Copy).then_inc(m_p1, 1)

            def part2(u):
                act.wait_ge(m_r1, u + 1)
                act.activation(uparts[:, u % 2, 1].rearrange("p t d -> p (t d)"), dr[:, u % 2],
                               ACT.Copy).then_inc(m_p2, 1)

            for n in range(UNITS + 4):
                if n < UNITS:
                    softplus_exp(n)
                if 0 <= n - 1 < UNITS:
                    softplus_ln(n - 1)
                if n in (1, 2):
                    act.wait_ge(m_bsl, n)
                    act.activation(bsel[:, n - 1].rearrange("p t g n -> p g t n"),
                                   PS[:, 3 + n, :].rearrange("p (g t n) -> p g t n", g=8, n=STATE),
                                   ACT.Copy).then_inc(m_bsc, 1)
                if 0 <= n - 2 < UNITS:
                    part1(n - 2)
                if 0 <= n - 3 < UNITS:
                    part2(n - 3)

            act.wait_ge(m_zero, 1)
            act.wait_ge(m_na, 1)
            for u in range(UNITS):
                for half in range(2):
                    if u >= 1:
                        act.wait_ge(m_scan, 8 * (u - 1) + 4 * half + 4)
                    for n in range(STATE):
                        i = act.activation(decay[:, half, :, n, 1:64],
                                           dts[:, u // 3, u % 3, 256 * half:256 * half + 256]
                                           .rearrange("p (b t) -> p b t", t=64)[:, :, 1:64],
                                           ACT.Exp, scale=m_a[:, u // 3, u % 3, n:n + 1])
                    i.then_inc(m_dec, 1)

            ln_act(4, 6)
            act.wait_ge(q_vd, 1)
            act.activation(q_v[:, 0:2, :], PS[:, 2:4, 0:384], ACT.Copy).then_inc(q_va, 1)

            def quad_q_copy(j):
                act.wait_ge(q_proj, j + 1)
                act.activation(q_qT[:, j % 2, :], PS[:, 0, :], ACT.Copy).then_inc(q_q, 1)

            def quad_exps(j):
                act.wait_ge(q_sub, j + 1)
                v = q_prob[:, j % 2].rearrange("p m t a k -> p (m t a k)")
                act.activation(v, v, ACT.Exp, scale=0.25).then_inc(q_exp, 1)

            def quad_probT_copy(j):
                act.wait_ge(q_pt, 1 + 2 * j)
                act.activation(q_probT[:, 0:2].rearrange("p m t n -> p (m t n)"), PS[:, 6, :],
                               ACT.Copy).then_inc(q_ptc[0], 1)

            def quad_even_copy(j):
                act.wait_ge(q_pv, j + 1)
                act.activation(q_attnT[:, j, :].rearrange("p (t a q) -> p a t q", a=2, q=64)[:, 0],
                               PS[:, 0, 0:256].rearrange("p (t q) -> p t q", q=64), ACT.Copy).then_inc(q_oe, 1)

            quad_q_copy(0)
            quad_q_copy(1)
            quad_exps(0)
            for j in range(QUADS):
                quad_probT_copy(j)
                if j + 1 < QUADS:
                    quad_exps(j + 1)
                quad_even_copy(j)
                if j + 2 < QUADS:
                    quad_q_copy(j + 2)
            ln_act(5, 6)
            act.wait_ge(g_d, 1)
            act.activation(gpair[:, 1], gpair[:, 1], ACT.Exp).then_inc(g_e, 1)

            def moe1_gelu(e, p):
                for m in range(3):
                    act.wait_ge(g_hid, 3 * e + m + 1)
                    for i in range(2):
                        act.activation(ghid[:, p, 2 * m + i, :], PS[:, 2 * ((3 * p + m) % 2) + i, :],
                                       ACT.Gelu).then_inc(g_act, 1)

            moe1_gelu(0, 0)
            with act.Fori(0, EXPERTS // 2 - 1) as i:
                moe1_gelu(2 * i + 1, 1)
                moe1_gelu(2 * i + 2, 0)
            moe1_gelu(EXPERTS - 1, 1)

        @block.vector
        def _(dve):
            dve.wait_ge(s_const, 48)
            for t in range(TILES):
                dve.wait_ge(s_tok, t + 1)
                dve.tensor_tensor(h[:, t, :], PS[:, t, 0:DIM], tok_b, ALU.add).then_inc(s_h, 1)

            def ln_moments(n, src, src_sem, src_count, each=1):
                for t in range(TILES):
                    dve.wait_ge(src_sem, src_count + each * (t + 1))
                    dve.bn_stats(stats[:, t, :], src[:, t, :]).then_inc(s_st, 1)
                for t in range(TILES):
                    dve.wait_ge(s_st, TILES * n + t + 1)
                    dve.bn_aggr(moments[:, t, :], stats[:, t, :]).then_inc(s_mo, 1)
                dve.wait_ge(s_rs, 2 * n + 2)

            def xtb_copy(n, bank):
                dve.wait_ge(s_xt, TILES * (TURN[n] + 1))
                dve.tensor_copy(xtb[:], PS[:, bank, :]).then_inc(s_xtb, 1)

            def ln_vector(n, src, src_sem, src_count, bank):
                ln_moments(n, src, src_sem, src_count)
                for t in range(TILES):
                    for to, cols in ((slice(0, DIM), slice(0, DIM)), (slice(DIM, 256), slice(128, DIM))):
                        dve.tensor_scalar(xn[:, t, to], src[:, t, cols], moments[:, t, 0:1], rstd[:, t:t + 1],
                                          ALU.subtract, ALU.mult).then_inc(s_xn, 1)
                xtb_copy(n, bank)

            def ln_plain(n, src, src_sem, src_count, to):
                ln_moments(n, src, src_sem, src_count)
                for t in range(TILES):
                    dve.tensor_scalar(to[:, t, 0:DIM], src[:, t, :], moments[:, t, 0:1], rstd[:, t:t + 1],
                                      ALU.subtract, ALU.mult).then_inc(s_xn, 2)

            def ln_affine(n, src, src_sem, src_count, each, bank):
                gamma, beta = ln_gb[2 * (n - 4)], ln_gb[2 * (n - 4) + 1]
                steps = s_aff[n - 4]
                dve.wait_ge(g_gb, 80)
                ln_moments(n, src, src_sem, src_count, each)
                for t in range(TILES):
                    dve.tensor_scalar(xn[:, t, 0:DIM], src[:, t, :], moments[:, t, 0:1], rstd[:, t:t + 1],
                                      ALU.subtract, ALU.mult).then_inc(steps, 1)
                dve.wait_ge(steps, TILES)
                dve.tensor_tensor(xn[:, :, 0:DIM], xn[:, :, 0:DIM],
                                  gamma.unsqueeze(1).to_broadcast([128, TILES, DIM]), ALU.mult).then_inc(steps, 1)
                dve.wait_ge(steps, TILES + 1)
                dve.tensor_tensor(xn[:, :, DIM:256], xn[:, :, 128:DIM],
                                  beta[:, 128:DIM].unsqueeze(1).to_broadcast([128, TILES, 64]),
                                  ALU.add).then_inc(steps, 1)
                dve.wait_ge(steps, TILES + 2)
                dve.tensor_tensor(xn[:, :, 0:DIM], xn[:, :, 0:DIM],
                                  beta.unsqueeze(1).to_broadcast([128, TILES, DIM]),
                                  ALU.add).then_inc(s_xn, 2 * TILES)
                xtb_copy(n, bank)

            ln_vector(0, h, s_h, 0, 7)
            for r in range(2):
                dve.wait_ge(a_v, r + 1)
                dve.tensor_copy(vtok[:, 2 * r + 1, :].rearrange("p (a n) -> p a n", a=2),
                                PS[:, 4 * r + 2:4 * r + 4, 0:384]).then_inc(a_vd, 1)

            def k_copy(j):
                dve.wait_ge(a_proj, j + 1)
                if j >= 2:
                    dve.wait_ge(a_s, j - 1)
                dve.tensor_copy(kT[:, j % 2, :], PS[:, 1, :]).then_inc(a_k, 1)

            def shift(j):
                b = j % 2
                dve.wait_ge(a_s, j + 1)
                if j >= 2:
                    dve.wait_ge(a_pt, j - 1)
                sc = prob[:, b]
                flat = sc.rearrange("p t a k -> p (t a) k")
                for a in range(2):
                    dve.tensor_tensor(sc[:, :, a], PS[:, 2 + a, 0:256].rearrange("p (t k) -> p t k", k=64),
                                      causal.unsqueeze(1).to_broadcast([128, 4, 64]),
                                      ALU.add).then_inc(a_mask, 1)
                dve.wait_ge(a_mask, 2 * j + 2)
                dve.tensor_reduce(rowmax[:, b, :], flat, AX.X, ALU.max).then_inc(a_max, 1)
                dve.wait_ge(a_max, j + 1)
                dve.tensor_tensor(flat, flat, rowmax[:, b, :].unsqueeze(2).to_broadcast([128, 8, 64]),
                                  ALU.subtract).then_inc(a_sub, 1)

            def normalise(j):
                b = j % 2
                flat = prob[:, b].rearrange("p t a k -> p (t a) k")
                dve.wait_ge(a_exp, j + 1)
                dve.tensor_reduce(rowsum[:, b, :], flat, AX.X, ALU.add).then_inc(a_sum, 1)
                dve.wait_ge(a_sum, j + 1)
                dve.reciprocal(rowsum[:, b, :], rowsum[:, b, :]).then_inc(a_rec, 1)
                dve.wait_ge(a_rec, j + 1)
                dve.tensor_tensor(flat, flat, rowsum[:, b, :].unsqueeze(2).to_broadcast([128, 8, 64]),
                                  ALU.mult).then_inc(a_p, 1)

            def odd_copy(j):
                dve.wait_ge(a_pv, j + 1)
                dve.tensor_copy(attnT[:, j, :].rearrange("p (t a q) -> p a t q", a=2, q=64)[:, 1],
                                PS[:, 6, 0:256].rearrange("p (t q) -> p t q", q=64)).then_inc(a_oo, 1)

            k_copy(0)
            k_copy(1)
            shift(0)
            for j in range(PAIRS):
                normalise(j)
                if j + 2 < PAIRS:
                    k_copy(j + 2)
                if j + 1 < PAIRS:
                    shift(j + 1)
                odd_copy(j)
            for t in range(TILES):
                dve.wait_ge(a_o, t + 1)
                dve.tensor_tensor(h[:, t, :], h[:, t, :], PS[:, t, 0:DIM], ALU.add).then_inc(s_h, 1)

            ln_vector(1, h, s_h, 4, 7)
            dve.sem_inc(f_acc, 8)

            def moe0_square(e, p):
                dve.wait_ge(f_relu, 2 * e + 3)
                dve.tensor_tensor(fhid[:, p, 0, :], frelu[:, p, 0, :], frelu[:, p, 0, :],
                                  ALU.mult).then_inc(f_sqa, 1)

            def moe0_add(e, p):
                dve.wait_ge(f_y, e + 1)
                for t in range(TILES):
                    dve.wait_ge(f_acc, TILES * e + t + 5)
                    dve.scalar_tensor_tensor(h[:, t, :], PS[:, 4 + 2 * p + t % 2, (t // 2) * DIM:(t // 2 + 1) * DIM],
                                             fwt[:, t, bass.ds(e, 1)], h[:, t, :],
                                             ALU.mult, ALU.add).then_inc(f_acc, 1)

            steps = [0]

            def routing_step(ins):
                steps[0] += 1
                ins.then_inc(f_rt, 1)
                dve.wait_ge(f_rt, steps[0])

            dve.wait_ge(f_sig, 1)
            dve.wait_ge(f_rw, 32)
            dve.wait_ge(s_ids, 2)
            routing_step(dve.tensor_tensor(fpick, fscore, fbias.unsqueeze(1).to_broadcast([128, TILES, EXPERTS]),
                                           ALU.add))
            for t in range(TILES):
                routing_step(dve.max(ftop[:, t, :], fpick[:, t, :]))
                routing_step(dve.max_index(fidx[:, t, :], ftop[:, t, :], fpick[:, t, :]))
            routing_step(dve.tensor_copy(fidxf, fidx[:, :, 0:2]))
            for k in range(2):
                routing_step(dve.tensor_tensor(fhot[:, k], expert_ids[:],
                                               fidxf[:, :, k:k + 1].to_broadcast([128, TILES, EXPERTS]),
                                               ALU.is_equal))
            routing_step(dve.tensor_tensor(fhot[:, 0], fhot[:, 0], fhot[:, 1], ALU.add))
            routing_step(dve.tensor_tensor(fhot[:, 0], fhot[:, 0], fscore, ALU.mult))
            routing_step(dve.tensor_reduce(fsum, fhot[:, 0], AX.X, ALU.add))
            routing_step(dve.tensor_scalar(fsum, fsum, 1e-20, None, ALU.add))
            routing_step(dve.reciprocal(fsum, fsum))
            routing_step(dve.tensor_tensor(fwt[:, :, 1:1 + EXPERTS], fhot[:, 0],
                                           fsum.unsqueeze(2).to_broadcast([128, TILES, EXPERTS]), ALU.mult))
            moe0_square(0, 0)
            with dve.Fori(0, EXPERTS // 2) as i:
                for p in range(2):
                    moe0_square(2 * i + p + 1, 1 - p)
                    moe0_add(2 * i + p, p)
            moe0_add(EXPERTS, 0)

            ln_vector(2, h, f_acc, 8 + TILES * EXPERTS, 7)
            dve.wait_ge(m_w, 160)
            for d in range(2):
                for k in range(TAPS):
                    for c in range(CTILES):
                        taps = xpad[:, c, :, k:k + 64] if d == 0 else xpad[:, c, :, 69 - k:5 - k:-1]
                        acc = xc[:, d, c].rearrange("p (b t) -> p b t", t=64)
                        if k == 0:
                            if d == 0:
                                dve.wait_ge(m_x, c + 1)
                            dve.tensor_scalar(acc, taps, m_conv[:, d, c, 0:1], m_convb[:, d, c:c + 1],
                                              ALU.mult, ALU.add).then_inc(m_cv, 1)
                        else:
                            dve.wait_ge(m_cv, 12 * d + 3 * (k - 1) + c + 1)
                            dve.scalar_tensor_tensor(acc, taps, m_conv[:, d, c, k:k + 1], acc,
                                                     ALU.mult, ALU.add).then_inc(m_cv, 1)

            bsteps = [0]

            def split_step(ins):
                bsteps[0] += 1
                ins.then_inc(m_bs, 1)
                dve.wait_ge(m_bs, bsteps[0])

            for d in range(2):
                dve.wait_ge(m_bt, d + 1)
                raw = bts[:, d]
                part = [bparts[:, d, i] for i in range(3)]
                split_step(dve.tensor_copy(raw, PS[:, 4 + d, 0:TILES * 44]
                                           .rearrange("p (t r) -> p t r", r=44)[:, :, RANK:RANK + STATE]))
                split_step(dve.tensor_copy(part[0], raw))
                split_step(dve.tensor_tensor(raw, raw, part[0], ALU.subtract))
                split_step(dve.tensor_copy(part[1], raw))
                split_step(dve.tensor_tensor(part[2], raw, part[1], ALU.subtract))
            dve.wait_ge(m_ea, 1)
            dve.tensor_scalar(m_a.rearrange("p d c n -> p (d c n)"), m_a.rearrange("p d c n -> p (d c n)"),
                              -1.0, None, ALU.mult).then_inc(m_na, 1)

            def softplus_vector(u):
                p = u % 2
                dve.wait_ge(m_se, u + 1)
                dve.tensor_scalar(softw[:, p], softe[:, p], 1.0, None, ALU.add).then_inc(m_sw, 1)
                dve.tensor_scalar(softx[:, p], softx[:, p], 0.0, None, ALU.max).then_inc(m_sm, 1)
                dve.wait_ge(m_sw, u + 1)
                dve.scalar_tensor_tensor(softe[:, p], softw[:, p], 1.0, softe[:, p],
                                         ALU.subtract, ALU.subtract).then_inc(m_sr, 1)

            def dtu(u):
                dve.wait_ge(m_dts, u + 1)
                dve.wait_ge(m_silu, u + 1)
                if u >= 2:
                    dve.wait_ge(m_dut, u - 1)
                dve.tensor_tensor(du[:, u % 2], dts[:, u // 3, u % 3], xc[:, u // 3, u % 3],
                                  ALU.mult).then_inc(m_du, 1)

            def rest1(u):
                dve.wait_ge(m_p1, u + 1)
                dve.tensor_tensor(dr[:, u % 2], PS[:, 2 + u % 2, :],
                                  uparts[:, u % 2, 0].rearrange("p t d -> p (t d)"), ALU.subtract).then_inc(m_r1, 1)

            def part3(u):
                dve.wait_ge(m_p2, u + 1)
                dve.tensor_tensor(uparts[:, u % 2, 2].rearrange("p t d -> p (t d)"), dr[:, u % 2],
                                  uparts[:, u % 2, 1].rearrange("p t d -> p (t d)"), ALU.subtract).then_inc(m_p3, 1)

            def b_blocks(d):
                dve.wait_ge(m_bsc, d + 1)
                for t in range(STEP):
                    dve.tensor_scalar(bd[:, d, :, t, :], bsel[:, d].rearrange("p t g n -> p (t g) n"),
                                      m_mask[:, t:t + 1], None, ALU.mult).then_inc(m_bd, 1)

            dve.wait_ge(m_sell, 16)
            for n in range(UNITS + 4):
                if n < UNITS:
                    softplus_vector(n)
                if 0 <= n - 1 < UNITS:
                    dtu(n - 1)
                if 0 <= n - 2 < UNITS:
                    rest1(n - 2)
                if 0 <= n - 3 < UNITS:
                    part3(n - 3)
                if n in (2, 4):
                    b_blocks(n // 2 - 1)

            def take_y(u, half):
                d, c = u // 3, u % 3
                cols = slice(256 * half, 256 * half + 256)
                dve.wait_ge(m_y, 4 * u + 2 * half + 2)
                to = yf[:, c, cols] if d == 0 else yr[:, half]
                dve.scalar_tensor_tensor(to, xc[:, d, c, cols], m_d[:, d, c:c + 1],
                                         PS[:, 4 + half, 0:256], ALU.mult, ALU.add).then_inc(m_post, 1)
                if d == 1:
                    n = 2 * c + half + 1
                    dve.wait_ge(m_post, 2 * u + half + 1)
                    f = yf[:, c, cols].rearrange("p (b t) -> p b t", t=64)
                    dve.tensor_tensor(f, f, yr[:, half].rearrange("p (b t) -> p b t", t=64)[:, :, ::-1],
                                      ALU.add).then_inc(m_sum, 1)
                    dve.wait_ge(m_sum, n)
                    dve.tensor_tensor(zgate[:, c, cols], yf[:, c, cols], zgate[:, c, cols],
                                      ALU.mult).then_inc(m_g, 1)

            for B in range(8 * UNITS):
                u, b = B // 8, B % 8
                chunk = B // 2
                dve.wait_ge(m_b, B + 1)
                if b % 4 == 0:
                    dve.wait_ge(m_dec, 2 * u + b // 4 + 1)
                if b % 2 == 0 and chunk >= 2:
                    dve.wait_ge(m_y, chunk - 1)
                dve.tensor_tensor_scan(hbuf[:, chunk % 2, b % 2].rearrange("p n t -> p (n t)"),
                                       decay[:, b // 4, b % 4].rearrange("p n t -> p (n t)"),
                                       PS[:, 2 * (b % 2):2 * (b % 2) + 2, :].rearrange("p k x -> p (k x)"),
                                       0.0, ALU.mult, ALU.add).then_inc(m_scan, 1)
                if b % 4 == 2 and chunk >= 3:
                    half_no = (chunk - 3) // 2
                    take_y(half_no // 2, half_no % 2)
            take_y(UNITS - 1, 1)
            for t in range(TILES):
                dve.wait_ge(m_o, t + 1)
                dve.tensor_tensor(h[:, t, :], h[:, t, :], PS[:, t, 0:DIM], ALU.add).then_inc(s_h, 1)

            ln_plain(3, h, s_h, 8, x4)
            ln_affine(4, x4, s_xn, 8 * 3, 2, 7)
            dve.wait_ge(q_vd, 2)
            dve.tensor_copy(q_v[:, 2:4, :], PS[:, 4:6, 0:384]).then_inc(q_vv, 1)

            def quad_k_copy(j):
                dve.wait_ge(q_proj, j + 1)
                dve.tensor_copy(q_kT[:, j % 2, :], PS[:, 1, :]).then_inc(q_k, 1)

            def quad_shift(j):
                b = j % 2
                dve.wait_ge(q_s, j + 1)
                sc = PS[:, 2:6, 0:256].rearrange("p m (x k) -> p m x k", k=64)
                mx = q_max[:, b].rearrange("p (m x) -> p m x", m=4)
                dve.tensor_reduce(mx, sc, AX.X, ALU.max).then_inc(q_mx, 1)
                dve.wait_ge(q_mx, j + 1)
                dve.tensor_tensor(q_prob[:, b].rearrange("p m t a k -> p m (t a) k"), sc,
                                  mx.unsqueeze(3).to_broadcast([128, 4, 4, 64]), ALU.subtract).then_inc(q_sub, 1)

            def quad_normalise(j):
                b = j % 2
                flat = q_prob[:, b].rearrange("p m t a k -> p (m t a) k")
                dve.wait_ge(q_exp, j + 1)
                dve.tensor_reduce(q_sum[:, b], flat, AX.X, ALU.add).then_inc(q_sm, 1)
                dve.wait_ge(q_sm, j + 1)
                dve.reciprocal(q_sum[:, b], q_sum[:, b]).then_inc(q_rec, 1)
                dve.wait_ge(q_rec, j + 1)
                dve.tensor_tensor(flat, flat, q_sum[:, b].unsqueeze(2).to_broadcast([128, 16, 64]),
                                  ALU.mult).then_inc(q_p, 1)

            def quad_probT_copy_b(j):
                dve.wait_ge(q_pt, 2 + 2 * j)
                dve.tensor_copy(q_probT[:, 2:4].rearrange("p m t n -> p (m t n)"), PS[:, 7, :]).then_inc(q_ptc[1], 1)

            def quad_odd_copy(j):
                dve.wait_ge(q_pv, j + 1)
                dve.tensor_copy(q_attnT[:, j, :].rearrange("p (t a q) -> p a t q", a=2, q=64)[:, 1],
                                PS[:, 1, 0:256].rearrange("p (t q) -> p t q", q=64)).then_inc(q_oo, 1)

            quad_k_copy(0)
            quad_k_copy(1)
            quad_shift(0)
            for j in range(QUADS):
                quad_normalise(j)
                quad_probT_copy_b(j)
                if j + 1 < QUADS:
                    quad_shift(j + 1)
                quad_odd_copy(j)
                if j + 2 < QUADS:
                    quad_k_copy(j + 2)
            for t in range(TILES):
                dve.wait_ge(q_o, t + 1)
                dve.tensor_tensor(x5[:, t, :], x4[:, t, :], PS[:, t, 0:DIM], ALU.add).then_inc(s_x5, 1)
            ln_affine(5, x5, s_x5, 0, 1, 7)
            dve.sem_inc(g_acc, 8)

            steps1 = [0]

            def routing1_step(ins):
                steps1[0] += 1
                ins.then_inc(g_rt, 1)
                dve.wait_ge(g_rt, steps1[0])

            dve.wait_ge(g_lg, 1)
            routing1_step(dve.tensor_copy(glog.rearrange("p t e -> p (t e)"), PS[:, 6, 0:TILES * EXPERTS]))
            for t in range(TILES):
                routing1_step(dve.max(gtop[:, t, :], glog[:, t, :]))
                routing1_step(dve.max_index(gidx[:, t, :], gtop[:, t, :], glog[:, t, :]))
            dve.tensor_tensor(gpair[:, 1], gtop[:, :, 1], gtop[:, :, 0], ALU.subtract).then_inc(g_d, 1)
            routing1_step(dve.tensor_copy(gidxf, gidx[:, :, 0:2]))
            dve.wait_ge(g_e, 1)
            routing1_step(dve.tensor_scalar(gpair[:, 0], gpair[:, 1], 1.0, None, ALU.add))
            routing1_step(dve.reciprocal(gpair[:, 0], gpair[:, 0]))
            routing1_step(dve.tensor_tensor(gpair[:, 1], gpair[:, 1], gpair[:, 0], ALU.mult))
            for k in range(2):
                routing1_step(dve.tensor_tensor(ghot[:, k], expert_ids[:],
                                                gidxf[:, :, k:k + 1].to_broadcast([128, TILES, EXPERTS]),
                                                ALU.is_equal))
                routing1_step(dve.tensor_tensor(ghot[:, k], ghot[:, k],
                                                gpair[:, k].unsqueeze(2).to_broadcast([128, TILES, EXPERTS]),
                                                ALU.mult))
            routing1_step(dve.tensor_tensor(gwt, ghot[:, 0], ghot[:, 1], ALU.add))
            dve.wait_ge(s_hx, TILES)

            def moe1_add(e, p):
                dve.wait_ge(g_y, e + 1)
                for t in range(TILES):
                    dve.wait_ge(g_acc, TILES * e + t + 5)
                    dve.scalar_tensor_tensor(h[:, t, :], PS[:, 4 + 2 * p + t % 2, (t // 2) * DIM:(t // 2 + 1) * DIM],
                                             gwt[:, t, bass.ds(e, 1)], h[:, t, :],
                                             ALU.mult, ALU.add).then_inc(g_acc, 1)

            with dve.Fori(0, EXPERTS // 2) as i:
                for p in range(2):
                    moe1_add(2 * i + p, p)

        @block.tensor
        def _(pe):
            pe.wait_ge(s_tokw, 16)
            for k in range(PATCH_K):
                pe.wait_ge(s_patch[k], 16)
                for t in range(TILES):
                    mm = pe.matmul(PS[:, t, 0:DIM], patches[:, k, t * 128:t * 128 + 128], tok_w[:, k, :],
                                   start=(k == 0), stop=(k == PATCH_K - 1))
                    if k == PATCH_K - 1:
                        mm.then_inc(s_tok, 1)
            pe.wait_ge(s_const, 48)

            def ln_tensor(n, bank_a, bank_b):
                for t in range(TILES):
                    cols = slice(t * 128, t * 128 + 128)
                    pe.wait_ge(s_xn, 8 * n + 2 * t + 2)
                    pe.transpose(PS[:, bank_a, cols], xn[:, t, 0:128], ident[:])
                    pe.transpose(PS[:, bank_b, cols], xn[:, t, 128:256], ident[:]).then_inc(s_xt, 1)

            ln_tensor(0, 6, 7)
            pe.wait_ge(s_w0, 48)
            pe.wait_ge(s_xta, 1)
            pe.wait_ge(s_xtb, 1)
            pe.wait_ge(s_h, 4)
            for r in range(2):
                for half in range(2):
                    ncol = slice(half * 384, half * 384 + 384)
                    banks = [PS[:, 4 * r + half, 0:384], PS[:, 4 * r + 2 + half, 0:384]]
                    for i, t in enumerate((2 * r, 2 * r + 1)):
                        pe.matmul(banks[i], xta[:, t * 128:t * 128 + 128], wv[:, 0, ncol], start=True, stop=False)
                    for i, t in enumerate((2 * r, 2 * r + 1)):
                        rows = slice(64 * i, 64 * i + 64)
                        mm = pe.matmul(banks[i], xtb[rows, t * 128:t * 128 + 128], wv[rows, 1, ncol],
                                       start=False, stop=True)
                mm.then_inc(a_v, 1)

            def project(j):
                if j >= 1:
                    pe.wait_ge(a_q, j)
                    pe.wait_ge(a_k, j)
                else:
                    pe.wait_ge(a_va, 1)
                    pe.wait_ge(a_vd, 1)
                for i in range(2):
                    pe.matmul(PS[:, i, :], wqk[:, j, i, :], xta[:], start=True, stop=False)
                for i in range(2):
                    rows = slice(64 * i, 64 * i + 64)
                    mm = pe.matmul(PS[:, i, :], wqk[rows, j, 2, :], xtb[rows, :], start=False, stop=True)
                mm.then_inc(a_proj, 1)

            def scores(j):
                b = j % 2
                pe.wait_ge(a_q, j + 1)
                pe.wait_ge(a_k, j + 1)
                if j >= 1:
                    pe.wait_ge(a_mask, 2 * j)
                for swap in range(2):
                    for t in range(TILES):
                        for i in ((0, 1), (1, 0))[swap]:
                            a = (i + swap) % 2
                            rows = slice(64 * i, 64 * i + 64)
                            img = 2 * t + a
                            cols = slice(img * 64, img * 64 + 64)
                            mm = pe.matmul(PS[rows, 2 + a, t * 64:t * 64 + 64], qT[rows, b, cols],
                                           kT[rows, b, cols], start=True, stop=True)
                mm.then_inc(a_s, 1)

            def transpose_probs(j):
                pe.wait_ge(a_p, j + 1)
                if j >= 1:
                    pe.wait_ge(a_ptc, j)
                for t in range(TILES):
                    mm = pe.transpose(PS[:, 4, t * 128:t * 128 + 128], prob[:, j % 2, t].rearrange("p a k -> p (a k)"), ident[:])
                mm.then_inc(a_pt, 1)

            def weigh(j):
                pe.wait_ge(a_ptc, j + 1)
                if j >= 1:
                    pe.wait_ge(a_oe, j)
                    pe.wait_ge(a_oo, j)
                for i in range(2):
                    for t in range(TILES):
                        for a in range(2):
                            rows = slice(64 * a, 64 * a + 64)
                            outp = slice(64 * i, 64 * i + 64)
                            mm = pe.matmul(PS[outp, 5 + a, t * 64:t * 64 + 64],
                                           vtok[rows, t, (2 * j + i) * 64:(2 * j + i) * 64 + 64],
                                           probT[rows, t, i * 64:i * 64 + 64], start=True, stop=True)
                mm.then_inc(a_pv, 1)

            project(0)
            pe.wait_ge(a_va, 2)
            pe.wait_ge(a_vd, 2)
            project(1)
            scores(0)
            for j in range(PAIRS):
                if j + 2 < PAIRS:
                    project(j + 2)
                transpose_probs(j)
                if j + 1 < PAIRS:
                    scores(j + 1)
                weigh(j)
            pe.wait_ge(a_oe, PAIRS)
            pe.wait_ge(a_oo, PAIRS)
            for t in range(TILES):
                for j in range(PAIRS):
                    mm = pe.matmul(PS[:, t, 0:DIM], attnT[:, j, t * 128:t * 128 + 128], wo[:, j, :],
                                   start=(j == 0), stop=(j == PAIRS - 1))
                mm.then_inc(a_o, 1)

            ln_tensor(1, 6, 7)
            pe.wait_ge(f_rw, 32)
            pe.wait_ge(s_xta, 2)
            pe.wait_ge(s_xtb, 2)
            for t in range(TILES):
                cols = slice(t * 128, t * 128 + 128)
                lg = PS[:, 6, t * EXPERTS:(t + 1) * EXPERTS]
                pe.matmul(lg, xta[:, cols], frw[:, 0, :], start=True, stop=False)
                mm = pe.matmul(lg, xtb[0:64, cols], frw[0:64, 1, :], start=False, stop=True)
            mm.then_inc(f_lg, 1)

            def moe0_up(p, loads, relus):
                pe.wait_ge(f_w1[p], 16 * loads)
                pe.wait_ge(f_relu, relus)
                for i in range(2):
                    pe.matmul(PS[:, 2 * p + i, :], fw1[:, p, i, :], xta[:], start=True, stop=False)
                for i in range(2):
                    rows = slice(64 * i, 64 * i + 64)
                    mm = pe.matmul(PS[:, 2 * p + i, :], fw1[rows, p, 2, :], xtb[rows, :], start=False, stop=True)
                mm.then_inc(f_hid, 1)

            def moe0_down(e, p, loads):
                pe.wait_ge(f_w2[p], 16 * loads)
                pe.wait_ge(f_sqa, e + 1)
                pe.wait_ge(f_sqb, e + 1)
                pe.wait_ge(f_acc, TILES * e + 4)
                for r in range(2):
                    to = [PS[:, 4 + 2 * p + i, r * DIM:(r + 1) * DIM] for i in range(2)]
                    for i in range(2):
                        cols = slice((2 * r + i) * 128, (2 * r + i + 1) * 128)
                        pe.matmul(to[i], fhid[:, p, 0, cols], fw2[:, p, 0, :], start=True, stop=False)
                    for i in range(2):
                        cols = slice((2 * r + i) * 128, (2 * r + i + 1) * 128)
                        rows = slice(64 * i, 64 * i + 64)
                        mm = pe.matmul(to[i], fhid[rows, p, 1, cols], fw2[rows, p, 1, :], start=False, stop=True)
                mm.then_inc(f_y, 1)

            moe0_up(0, 1, 2)
            pe.wait_ge(f_sig, 1)
            with pe.Fori(0, EXPERTS // 2) as i:
                for p in range(2):
                    moe0_up(1 - p, i + p + 1, 4 * i + 2 * p + 2)
                    moe0_down(2 * i + p, p, i + 1)
            moe0_down(EXPERTS, 0, EXPERTS // 2 + 1)

            ln_tensor(2, 6, 7)
            pe.wait_ge(m_w, 160)
            pe.wait_ge(s_xta, 3)
            pe.wait_ge(s_xtb, 3)
            for c in range(CTILES):
                k = 2 * (c % 2)
                if c >= 2:
                    pe.wait_ge(m_x, c - 1)
                    pe.wait_ge(m_z, c - 1)
                for i in range(2):
                    pe.matmul(PS[:, k + i, :], m_in[:, c, i, :], xta[:], start=True, stop=False)
                for i in range(2):
                    rows = slice(64 * i, 64 * i + 64)
                    mm = pe.matmul(PS[:, k + i, :], m_in[rows, c, 2, :], xtb[rows, :], start=False, stop=True)
                mm.then_inc(m_xz, 1)

            def x_dbl(d):
                for c in range(CTILES):
                    pe.wait_ge(m_silu, 3 * d + c + 1)
                    mm = pe.matmul(PS[0:44, 4 + d, :], m_xp[:, d, c, :], xc[:, d, c], start=(c == 0),
                                   stop=(c == CTILES - 1))
                mm.then_inc(m_xd, 1)
                pe.wait_ge(m_xdc, d + 1)
                for t in range(TILES):
                    mm = pe.transpose(PS[:, 4 + d, t * 44:t * 44 + 44], xdbl[0:44, d, t * 128:t * 128 + 128],
                                      ident[0:44, 0:44])
                mm.then_inc(m_bt, 1)

            def raw_dt(u):
                d, c = u // 3, u % 3
                if u >= 2:
                    pe.wait_ge(m_sx, u - 1)
                pe.matmul(PS[:, 6 + u % 2, :], m_dtw[0:RANK, d, c * 128:c * 128 + 128], xdbl[0:RANK, d, :],
                          start=True, stop=True).then_inc(m_dt, 1)

            def select_b(d):
                pe.wait_ge(m_bs, 5 * d + 5)
                pe.wait_ge(m_sell, 16)
                for g in range(8):
                    for j in range(3):
                        mm = pe.matmul(PS[:, 4 + d, g * 64:g * 64 + 64], m_sel[:, g, j, :],
                                       bparts[:, d, j].rearrange("p t n -> p (t n)"), start=(j == 0), stop=(j == 2))
                mm.then_inc(m_bsl, 1)

            def transpose_dtu(u):
                pe.wait_ge(m_du, u + 1)
                if u >= 2:
                    pe.wait_ge(m_r1, u - 1)
                for t in range(TILES):
                    mm = pe.transpose(PS[:, 2 + u % 2, t * 128:t * 128 + 128], du[:, u % 2, t * 128:t * 128 + 128],
                                      ident[:])
                mm.then_inc(m_dut, 1)

            x_dbl(0)
            raw_dt(0)
            raw_dt(1)
            select_b(0)
            x_dbl(1)
            raw_dt(2)
            select_b(1)
            transpose_dtu(0)
            for u in range(3, UNITS):
                raw_dt(u)
                transpose_dtu(u - 2)
            transpose_dtu(UNITS - 2)
            transpose_dtu(UNITS - 1)

            def form_inputs(B):
                u, b = B // 8, B % 8
                if b == 0:
                    pe.wait_ge(m_lw, 16 * COMBOS * (u + 1))
                    pe.wait_ge(m_bd, STEP * (u // 3 + 1))
                if B >= 2:
                    pe.wait_ge(m_scan, B - 1)
                for s in range(4):
                    for nh in range(2):
                        to = PS[:, 2 * (b % 2) + nh, :].rearrange("p (n t) -> p t n", t=64)
                        mm = pe.matmul(to[:, s * STEP:(s + 1) * STEP, :],
                                       lw[:, u % 2, (b % 2) * 4 + s, b // 2, :],
                                       bd[:, u // 3, b * 4 + s, :, nh * 8:nh * 8 + 8], start=True, stop=True)
                mm.then_inc(m_b, 1)

            def sum_states(v):
                u, q = v // 4, v % 4
                pe.wait_ge(m_mul, 2 * v + 2)
                if q % 2 == 0 and u >= 1:
                    pe.wait_ge(m_post, 2 * (u - 1) + q // 2 + 1)
                to = PS[:, 4 + q // 2, (q % 2) * 128:(q % 2) * 128 + 128]
                for n in range(STATE):
                    mm = pe.matmul(to, ident[:], hbuf[:, v % 2, :, n, :], start=(n == 0), stop=(n == STATE - 1))
                mm.then_inc(m_y, 1)

            pe.wait_ge(m_r1, UNITS)
            pe.wait_ge(m_bsc, 2)
            form_inputs(0)
            form_inputs(1)
            for v in range(4 * UNITS):
                if v + 1 < 4 * UNITS:
                    form_inputs(2 * v + 2)
                    form_inputs(2 * v + 3)
                sum_states(v)
            pe.wait_ge(m_scan, 8 * UNITS)
            pe.wait_ge(m_g, 2 * CTILES)
            for t in range(TILES):
                for c in range(CTILES):
                    mm = pe.matmul(PS[:, t, 0:DIM], zgate[:, c, t * 128:t * 128 + 128], m_out[:, c, :],
                                   start=(c == 0), stop=(c == CTILES - 1))
                mm.then_inc(m_o, 1)

            ln_tensor(4, 6, 7)
            pe.wait_ge(q_w, 48)
            pe.wait_ge(s_xta, 4)
            pe.wait_ge(s_xtb, 4)
            for r in range(2):
                banks = [PS[:, 2 + 2 * r + i, 0:384] for i in range(2)]
                for i in range(2):
                    t = 2 * r + i
                    pe.matmul(banks[i], xta[:, t * 128:t * 128 + 128], q_wv[:, 0, :], start=True, stop=False)
                for i in range(2):
                    t = 2 * r + i
                    rows = slice(64 * i, 64 * i + 64)
                    mm = pe.matmul(banks[i], xtb[rows, t * 128:t * 128 + 128], q_wv[rows, 1, :],
                                   start=False, stop=True)
                mm.then_inc(q_vd, 1)

            def quad_project(j):
                if j >= 1:
                    pe.wait_ge(q_q, j)
                    pe.wait_ge(q_k, j)
                if j >= 2:
                    pe.wait_ge(q_oe, j - 1)
                    pe.wait_ge(q_oo, j - 1)
                for i in range(2):
                    pe.matmul(PS[:, i, :], q_wqk[:, j, i, :], xta[:], start=True, stop=False)
                for i in range(2):
                    rows = slice(64 * i, 64 * i + 64)
                    mm = pe.matmul(PS[:, i, :], q_wqk[rows, j, 2, :], xtb[rows, :], start=False, stop=True)
                mm.then_inc(q_proj, 1)

            def quad_scores(j):
                b = j % 2
                pe.wait_ge(q_q, j + 1)
                pe.wait_ge(q_k, j + 1)
                if j >= 1:
                    pe.wait_ge(q_sub, j)
                for swap in range(2):
                    for t2 in range(2):
                        for a in range(2):
                            for hd in ((0, 1, 2, 3), (1, 0, 3, 2))[swap]:
                                side, hp = hd % 2, hd // 2
                                par = (side + swap) % 2
                                img = 2 * (2 * t2 + par) + a
                                rows = slice(32 * hd, 32 * hd + 32)
                                cols = slice(img * 64, img * 64 + 64)
                                x = (t2 * 2 + a) * 64
                                mm = pe.matmul(PS[64 * side:64 * side + 64, 2 + 2 * hp + par, x:x + 64],
                                               q_qT[rows, b, cols], q_kT[rows, b, cols], start=True, stop=True,
                                               tile_position=(32 * hd, 64 * side))
                mm.then_inc(q_s, 1)

            def quad_transpose_probs(j):
                pe.wait_ge(q_p, j + 1)
                if j >= 1:
                    pe.wait_ge(q_ptc[0], j)
                    pe.wait_ge(q_ptc[1], j)
                for m in range(4):
                    for t2 in range(2):
                        x = ((m % 2) * 2 + t2) * 128
                        mm = pe.transpose(PS[:, 6 + m // 2, x:x + 128],
                                          q_prob[:, j % 2, m, t2].rearrange("p a k -> p (a k)"), ident[:])
                    if m % 2:
                        mm.then_inc(q_pt, 1)

            def quad_weigh(j):
                pe.wait_ge(q_ptc[0], j + 1)
                pe.wait_ge(q_ptc[1], j + 1)
                pe.wait_ge(q_q, min(j + 2, QUADS))
                pe.wait_ge(q_k, min(j + 2, QUADS))
                if j >= 1:
                    pe.wait_ge(q_oe, j)
                    pe.wait_ge(q_oo, j)
                for hd in range(4):
                    side, hp = hd % 2, hd // 2
                    for t in range(TILES):
                        for a in range(2):
                            rows = slice(64 * a, 64 * a + 64)
                            hcol = (4 * j + hd) * 32
                            mm = pe.matmul(PS[32 * hd:32 * hd + 32, a, t * 64:t * 64 + 64],
                                           q_v[rows, t, hcol:hcol + 32],
                                           q_probT[rows, 2 * hp + t % 2, t // 2, side * 64:side * 64 + 64],
                                           start=True, stop=True, tile_position=(64 * a, 32 * hd))
                mm.then_inc(q_pv, 1)

            quad_project(0)
            pe.wait_ge(q_va, 1)
            pe.wait_ge(q_vv, 1)
            quad_project(1)
            quad_scores(0)
            for j in range(QUADS):
                quad_transpose_probs(j)
                if j + 1 < QUADS:
                    quad_scores(j + 1)
                quad_weigh(j)
                if j + 2 < QUADS:
                    quad_project(j + 2)
            pe.wait_ge(q_oe, QUADS)
            pe.wait_ge(q_oo, QUADS)
            for t in range(TILES):
                for j in range(QUADS):
                    mm = pe.matmul(PS[:, t, 0:DIM], q_attnT[:, j, t * 128:t * 128 + 128], q_wo[:, j, :],
                                   start=(j == 0), stop=(j == QUADS - 1))
                mm.then_inc(q_o, 1)

            ln_tensor(5, 6, 7)
            pe.wait_ge(g_gb, 80)
            pe.wait_ge(s_xta, 5)
            pe.wait_ge(s_xtb, 5)
            for t in range(TILES):
                cols = slice(t * 128, t * 128 + 128)
                lg = PS[:, 6, t * EXPERTS:(t + 1) * EXPERTS]
                pe.matmul(lg, xta[:, cols], grw[:, 0, :], start=True, stop=False)
                mm = pe.matmul(lg, xtb[0:64, cols], grw[0:64, 1, :], start=False, stop=True)
            mm.then_inc(g_lg, 1)

            def moe1_up(e, p, loads, first=False):
                pe.wait_ge(g_w1[p], 16 * loads)
                for m in range(3):
                    k = 2 * ((3 * p + m) % 2)
                    if not first or m == 2:
                        pe.wait_ge(g_act, 2 * (3 * e + m - 1))
                    for i in range(2):
                        pe.matmul(PS[:, k + i, :], gw1[p][:, m, i, :], xta[:], start=True, stop=False)
                    for i in range(2):
                        rows = slice(64 * i, 64 * i + 64)
                        mm = pe.matmul(PS[:, k + i, :], gw1[p][rows, m, 2, :], xtb[rows, :], start=False, stop=True)
                    mm.then_inc(g_hid, 1)

            def moe1_down(e, p, loads):
                pe.wait_ge(g_w2[p], 16 * loads)
                pe.wait_ge(g_act, 6 * e + 6)
                pe.wait_ge(g_acc, TILES * e + 4)
                for t in range(TILES):
                    for k in range(HCHUNKS):
                        mm = pe.matmul(PS[:, 4 + 2 * p + t % 2, (t // 2) * DIM:(t // 2 + 1) * DIM],
                                       ghid[:, p, k, t * 128:t * 128 + 128], gw2[p][:, k, :],
                                       start=(k == 0), stop=(k == HCHUNKS - 1))
                mm.then_inc(g_y, 1)

            moe1_up(0, 0, 1, first=True)
            pe.wait_ge(g_rt, 1)
            with pe.Fori(0, EXPERTS // 2 - 1) as i:
                for p in range(2):
                    moe1_up(2 * i + p + 1, 1 - p, i + p + 1)
                    moe1_down(2 * i + p, p, i + 1)
            moe1_up(EXPERTS - 1, 1, EXPERTS // 2)
            moe1_down(EXPERTS - 2, 0, EXPERTS // 2)
            moe1_down(EXPERTS - 1, 1, EXPERTS // 2)


def lay_out(i):
    import numpy as np
    f = lambda a: np.ascontiguousarray(a)
    chunked = lambda a: f(a.reshape(-1, 128, a.shape[-1]).transpose(1, 0, 2))
    twice = lambda a: np.concatenate([a, a], 0)

    x = i["x"].reshape(8, 3, 8, 16, 8, 16)
    a = {"ident": np.eye(128, dtype=np.float32)}
    a["patches"] = chunked(x.transpose(1, 3, 5, 0, 2, 4).reshape(768, 512))
    a["tok_w"] = chunked(i["L0_tok_W"].reshape(192, 16, 16, 3).transpose(3, 1, 2, 0).reshape(768, 192))
    a["tok_b"] = f(i["L0_tok_b"])
    q = np.arange(128)[:, None] % 64
    a["causal"] = np.where(np.arange(64)[None, :] > q, np.float32(MASKED), np.float32(0)).astype(np.float32)

    pair = lambda w: w.reshape(6, 2, 192, 64).transpose(2, 0, 1, 3).reshape(192, 6, 128)
    wq, wk = pair(i["L0_attn_W_Q"]), pair(i["L0_attn_W_K"])
    a["a0_wqk"] = f(np.stack([wq[:128], wk[:128], np.concatenate([wq[128:], wk[128:]], 0)], 2))
    wv = i["L0_attn_W_V"].transpose(1, 0, 2).reshape(192, 768)
    a["a0_wv"] = f(np.stack([wv[:128], twice(wv[128:])], 1))
    a["a0_wo"] = chunked(i["L0_attn_W_O"])

    moe0_1 = lambda w: np.stack([w[:128, :128], np.concatenate([w[:128, 128:]] * 2, 1),
                                 np.concatenate([w[128:, :128], np.concatenate([w[128:, 128:]] * 2, 1)], 0)], 1)
    moe0_2 = lambda w: np.stack([w[:128], twice(w[128:])], 1)
    a["m0_w1"] = f(np.stack([moe0_1(w) for w in [i["L0_ffn_w_fc_sh"], *i["L0_ffn_w1"]]], 0))
    a["m0_w2"] = f(np.stack([moe0_2(w) for w in [i["L0_ffn_w_proj_sh"], *i["L0_ffn_w2"]]], 0))
    a["m0_router"] = f(moe0_2(i["L0_ffn_router_w"].T))
    a["m0_bias"] = f(i["L0_ffn_balance_bias"])

    w = i["L1_attn_in_proj_w"].T
    wx, wz = w[:, :384].reshape(192, 3, 128), w[:, 384:].reshape(192, 3, 128)
    a["m_in"] = f(np.stack([wx[:128], wz[:128], np.concatenate([wx[128:], wz[128:]], 0)], 2))
    both = lambda name: np.stack([i["L1_attn_" + name], i["L1_attn_" + name + "_b"]], 0)
    per_channel = lambda v: f(v.reshape(2, 3, 128, -1).transpose(2, 0, 1, 3))
    a["m_xp"] = per_channel(both("x_proj_w").transpose(0, 2, 1))
    a["m_dtw"] = f(np.stack([i["L1_attn_dt_proj_w"], i["L1_attn_dt_proj_w_b"]], 0).transpose(2, 0, 1))
    a["m_out"] = chunked(i["L1_attn_out_proj_w"].T)
    a["m_conv"] = per_channel(both("conv1d_w"))
    a["m_convb"] = per_channel(both("conv1d_bias"))[..., 0]
    a["m_dtb"] = per_channel(both("dt_proj_bias"))[..., 0]
    a["m_a"] = per_channel(both("A_log"))
    a["m_d"] = per_channel(both("D"))[..., 0]
    row = np.arange(128)
    a["m_mask"] = (row[:, None] % STEP == np.arange(STEP)[None, :]).astype(np.float32)
    sel = np.zeros((128, 8, 3, 128), np.uint16)
    for c in range(COMBOS):
        for g in range(8):
            for t in range(STEP):
                sel[g * STEP + t, g, PART_B[c], c * STEP + t] = 1
    a["m_sel"] = sel * np.uint16(0x3F80)

    w = i["L1_ffn_Wqkv"].reshape(192, 3, 12, 16)
    w = np.concatenate([w, np.zeros_like(w)], 3).reshape(192, 3, 384)
    wq, wk, wv = w[:, 0].reshape(192, 3, 128), w[:, 1].reshape(192, 3, 128), w[:, 2]
    a["a1_wqk"] = f(np.stack([wq[:128], wk[:128], np.concatenate([wq[128:], wk[128:]], 0)], 2))
    a["a1_wv"] = f(np.stack([wv[:128], twice(wv[128:])], 1))
    w = i["L1_ffn_Wproj"].reshape(12, 16, 192)
    a["a1_wo"] = chunked(np.concatenate([w, np.zeros_like(w)], 1).reshape(384, 192))
    w = i["L1_ffn_W1"].reshape(8, 192, 3, 2, 128)
    a["m1_w1"] = f(np.stack([w[:, :128, :, 0], w[:, :128, :, 1],
                             np.concatenate([w[:, 128:, :, 0], w[:, 128:, :, 1]], 1)], 3))
    a["m1_w2"] = f(i["L1_ffn_W2"].reshape(8, 6, 128, 192).transpose(0, 2, 1, 3))
    a["m1_router"] = f(moe0_2(i["L1_ffn_Wrouter"]))
    for n in ("ln1_g", "ln1_b", "ln2_g", "ln2_b"):
        a[n] = f(i["L1_ffn_" + n])
    return a


def kernel(**inputs):
    import numpy as np
    import concourse.bacc as bacc
    from concourse.bass_utils import run_bass_kernel_spmd

    arrays = lay_out({k: np.asarray(v) for k, v in inputs.items()})
    nc = bacc.Bacc("TRN2", target_bir_lowering=False, num_devices=1)
    io = {n: nc.dram_tensor(f"in_{n}", a.shape, mybir.dt.from_np(a.dtype), kind="ExternalInput").ap()
          for n, a in arrays.items()}
    out = nc.dram_tensor("out", (TOKENS, DIM), mybir.dt.float32, kind="ExternalOutput").ap()
    build_tower(nc, io, out)
    got = run_bass_kernel_spmd(nc, [{f"in_{n}": a for n, a in arrays.items()}], core_ids=[0])
    return got.results[0]["out"].reshape(BATCH, TOKENS_PER_IMAGE, DIM)
```

```python
import concourse.bass as bass
from concourse import mybir
from contextlib import ExitStack

BATCH, TOKENS_PER_IMAGE, DIM = 8, 64, 192
TOKENS = BATCH * TOKENS_PER_IMAGE
TILES = TOKENS // 128
PATCH_K = 768 // 128
HEADS = 12
PAIRS = HEADS // 2
LN_EPS = 1e-5
EXPERTS = 8
INNER, STATE, RANK, TAPS = 384, 16, 12, 4
CTILES = INNER // 128
UNITS = 2 * CTILES
STEP = 16
COMBOS = 8
PART_U = [c % 3 for c in range(COMBOS)]
PART_B = [c // 3 for c in range(COMBOS)]
MASKED = -1.0e30


def build_tower(nc, io, out):
    F32 = mybir.dt.float32
    F32R = mybir.dt.float32r
    BF16 = mybir.dt.bfloat16
    ALU = mybir.AluOpType
    ACT = mybir.ActivationFunctionType
    AX = mybir.AxisListType

    c_dram = nc.dram_tensor("c_scratch", (2, BATCH, STATE, 64), F32, kind="Internal").ap()
    u_dram = nc.dram_tensor("u_scratch", (UNITS, 3, 128, 512), BF16, kind="Internal").ap()

    ctx = ExitStack()
    with ctx:
        def sb(name, shape, dt=F32):
            return ctx.enter_context(nc.sbuf_tensor(name, shape, dt))

        def sem(name):
            return ctx.enter_context(nc.semaphore(name))

        PS = ctx.enter_context(nc.psum_tensor("PS", [128, 8, 512], F32))

        ident = sb("ident", [128, 128])
        h = sb("h", [128, TILES, DIM])
        xn = sb("xn", [128, TILES, 256])
        xta = sb("xta", [128, TOKENS])
        xtb = sb("xtb", [128, TOKENS])
        stats = sb("stats", [128, TILES, 6])
        moments = sb("moments", [128, TILES, 2])
        rstd = sb("rstd", [128, TILES])
        neg_half = sb("neg_half", [128, TILES])

        expert_ids = sb("expert_ids", [128, TILES, EXPERTS])

        ARENA = 49900
        arena_at = -(-nc.sbuf_base // 32) * 32
        arena = sb("arena", [128, ARENA])

        def carve(at, *shape, dt=F32):
            n = 1
            for s in shape:
                n *= s
            cols = n // 2 if dt == BF16 else n
            if dt == F32R:
                at[0] = -(-at[0] // 8) * 8
            assert at[0] + cols <= at[1], (at, shape)
            if dt == F32R:
                v = nc.alloc_sbuf_tensor_at(f"parts_at_{at[0]}", [128, cols], F32R, offset=arena_at + 4 * at[0])[:]
            else:
                v = arena[:, at[0]:at[0] + cols]
            at[0] += cols
            if dt == BF16:
                v = v.bitcast(dt)
            names = "abcde"[:len(shape)]
            if len(shape) > 1:
                v = v.rearrange(f"p ({' '.join(names)}) -> p {' '.join(names)}",
                                **{names[i]: shape[i] for i in range(1, len(shape))})
            return v

        SPLIT_X = 25128
        at = [SPLIT_X, SPLIT_X + 4 * TOKENS]
        xh = carve(at, 2, TOKENS, dt=F32R)
        xl = carve(at, 2, TOKENS, dt=F32R)

        at = [0, ARENA]
        patches = carve(at, PATCH_K, TOKENS)
        tok_w = carve(at, PATCH_K, DIM)
        tok_b = carve(at, DIM)
        wqk = carve(at, PAIRS, 3, 128)
        wv = carve(at, 2, HEADS * 64)
        wo = carve(at, PAIRS, DIM)
        causal = carve(at, 64)
        vtok = carve(at, TILES, HEADS * 64)
        qT = carve(at, 2, TOKENS)
        kT = carve(at, 2, TOKENS)
        prob = carve(at, 2, TILES, 2, 64)
        rowmax = carve(at, 2, 8)
        rowsum = carve(at, 2, 8)
        probT = carve(at, TILES, 128)
        attnT = carve(at, PAIRS, TOKENS)

        frw = carve(at, 2, EXPERTS)
        fbias = carve(at, EXPERTS)
        fscore = carve(at, TILES, EXPERTS)
        fpick = carve(at, TILES, EXPERTS)
        ftop = carve(at, TILES, 8)
        fidx = carve(at, TILES, 8).bitcast(mybir.dt.uint32)
        fidxf = carve(at, TILES, 2)
        fhot = carve(at, 2, TILES, EXPERTS)
        fsum = carve(at, TILES)
        fwt = carve(at, TILES, 1 + EXPERTS)

        at = [SPLIT_X + 4 * TOKENS, 29896 + 8192]
        fw1 = carve(at, 2, 2, 2, 128)
        fw1h = carve(at, 2, 2, 2, 128, dt=F32R)
        fw1l = carve(at, 2, 2, 128, dt=F32R)
        fw2 = carve(at, 2, 2, DIM)
        fw2h = carve(at, 2, 2, DIM, dt=F32R)
        fw2l = carve(at, 2, DIM, dt=F32R)
        frwh = carve(at, 2, EXPERTS, dt=F32R)
        frwl = carve(at, EXPERTS, dt=F32R)
        frelu = carve(at, 2, 2, TOKENS)
        fhh = carve(at, 2, 2, TOKENS, dt=F32R)
        fhl = carve(at, 2, 2, TOKENS, dt=F32R)

        at = [29896, ARENA]
        fresh = at[0]
        decay = carve(at, 2, 4, STATE, 64)
        mark = at[0]
        at = [fresh, mark]
        xpad = carve(at, CTILES, BATCH, 70)
        softx = carve(at, 2, CTILES, TOKENS)
        softe = carve(at, 2, CTILES, TOKENS)
        at = [mark, ARENA]
        m_in = carve(at, CTILES, 3, 128)
        m_xp = carve(at, 2, CTILES, 44)
        m_dtw = carve(at, 2, INNER)
        m_out = carve(at, CTILES, DIM)
        m_conv = carve(at, 2, CTILES, TAPS)
        m_convb = carve(at, 2, CTILES)
        m_dtb = carve(at, 2, CTILES)
        m_a = carve(at, 2, CTILES, STATE)
        m_d = carve(at, 2, CTILES)
        m_mask = carve(at, STEP)
        zgate = carve(at, CTILES, TOKENS)
        xc = carve(at, 2, CTILES, TOKENS)
        dts = carve(at, 2, CTILES, TOKENS)
        bts = carve(at, 2, TILES, STATE)
        at = [0, fresh]
        hbuf = [carve(at, 2, STATE, 64) for _ in range(2)]
        mark = at[0]
        at = [0, mark]
        du = carve(at, 2, CTILES, TOKENS)
        dr = carve(at, 2, TOKENS)
        at = [mark, fresh]
        bd = carve(at, 2, 32, STEP, STATE, dt=BF16)
        lw = carve(at, 2, 8, TILES, 128, dt=BF16)
        cb = carve(at, BATCH, STATE, 64)
        softw = [cb[:, 4 + 2 * d:6 + 2 * d].rearrange("p b n t -> p (b n t)")[:, 0:CTILES * TOKENS]
                 .rearrange("p (c t) -> p c t", c=CTILES) for d in range(2)]
        m_sel = carve([at[0], at[1]], 8, 3, 128, dt=BF16)
        yf = carve(at, CTILES, TOKENS)
        third = at[0]
        xdbl = carve(at, 2, TOKENS)
        uparts = [carve(at, 3, TILES, 128, dt=BF16) for _ in range(2)]
        hbuf.append(carve([third, at[0]], 2, STATE, 64))
        for lent in (lw[:, 1].rearrange("p g t d -> p (g t d)"),
                     cb[:, 2:4].rearrange("p b n t -> p (b n t)").bitcast(BF16)):
            for k in range(2):
                uparts.append(lent[:, k * 1536:(k + 1) * 1536].rearrange("p (i t d) -> p i t d", i=3, t=TILES))
        bparts = carve(at, 2, 3, TILES, STATE, dt=BF16)
        bsel = carve(at, 2, TILES, 8, STATE, dt=BF16)
        yr = carve(at, 2, 256)

        QUADS = HEADS // 4
        HCHUNKS = 6
        at = [4096, 8192]
        q_wqk = carve(at, QUADS, 3, 128)
        q_wv = carve(at, 2, HEADS * 32)
        q_wo = carve(at, QUADS, DIM)
        gw1_0 = carve(at, HCHUNKS, 2, 128)
        at = [8192, 16384]
        gw1 = [gw1_0, carve(at, HCHUNKS, 2, 128)]
        gw2 = [carve(at, HCHUNKS, DIM) for _ in range(2)]
        gw1h = [carve(at, HCHUNKS, 2, 128, dt=F32R) for _ in range(2)]
        ln_gb = [carve(at, DIM) for _ in range(4)]
        grw = carve(at, 2, EXPERTS)
        grwh = carve(at, 2, EXPERTS, dt=F32R)
        grwl = carve(at, EXPERTS, dt=F32R)
        at = [16384, SPLIT_X]
        q_v = carve(at, TILES, HEADS * 32)
        q_qT = carve(at, 2, TOKENS)
        q_kT = carve(at, 2, TOKENS)
        q_prob = carve(at, 2, 4, 2, 2, 64)
        q_probT = carve(at, 4, 2, 128)
        q_attnT = carve(at, QUADS, TOKENS)
        q_max = carve(at, 2, 16)
        q_sum = carve(at, 2, 16)
        gtop = carve(at, TILES, 8)
        gidx = carve(at, TILES, 8).bitcast(mybir.dt.uint32)
        gidxf = carve(at, TILES, 2)
        glog = carve(at, TILES, EXPERTS)
        ghot = carve(at, 2, TILES, EXPERTS)
        gpair = carve(at, 2, TILES)
        gwt = carve(at, TILES, EXPERTS)
        at = [fresh, fresh + 8192]
        x4 = carve(at, TILES, DIM)
        x5 = carve(at, TILES, DIM)
        gw2h = [carve(at, HCHUNKS, DIM, dt=F32R) for _ in range(2)]
        gw1l = [carve(at, HCHUNKS, 128, dt=F32R) for _ in range(2)]
        at = [fresh + 8192, ARENA]
        gw2l = [carve(at, HCHUNKS, DIM, dt=F32R) for _ in range(2)]
        ghh = [carve(at, HCHUNKS, TOKENS, dt=F32R) for _ in range(2)]
        at = [16384, SPLIT_X]
        ghl = [carve(at, HCHUNKS, TOKENS, dt=F32R)]
        ghl.append(carve(at, HCHUNKS, TOKENS, dt=F32R))
        at = [SPLIT_X + 4 * TOKENS, 29896]
        gact_a = carve(at, 4, TOKENS)
        at = [29896 + 8192 + 2 * HCHUNKS * DIM + 2 * HCHUNKS * TOKENS, ARENA]
        gact_b = carve(at, 2, TOKENS)
        gact = [gact_a[:, 0:2], gact_a[:, 2:4], gact_b]

        s_const = sem("const_loaded")
        s_tokw = sem("tok_weights_loaded")
        s_patch = [sem(f"patches_loaded{k}") for k in range(PATCH_K)]
        s_tok = sem("tok_done")
        s_h = sem("h_written")
        s_nh = sem("neg_half_set")
        s_w0 = sem("attn0_weights_loaded")
        s_out = sem("out_stored")
        s_st = sem("ln_stats")
        s_mo = sem("ln_moments")
        s_rs = sem("ln_rstd")
        s_xn = sem("ln_normed")
        s_xt = sem("ln_transposed")
        s_xta = sem("ln_xta")
        s_xtb = sem("ln_xtb")
        TURN = [0, 1, 2, None, 3, 4]

        a_v = sem("attn0_v_done")
        a_va = sem("attn0_v_copied_by_scalar")
        a_vd = sem("attn0_v_copied_by_vector")
        a_proj = sem("attn0_qk_done")
        a_q = sem("attn0_q_copied")
        a_k = sem("attn0_k_copied")
        a_s = sem("attn0_scores_done")
        a_sub = sem("attn0_masked_max_shifted")
        a_exp = sem("attn0_exp_done")
        a_p = sem("attn0_sum_recip_probs")
        a_pt = sem("attn0_probs_transposed")
        a_ptc = sem("attn0_probsT_copied")
        a_pv = sem("attn0_pv_done")
        a_oe = sem("attn0_even_copied")
        a_oo = sem("attn0_odd_copied")
        a_o = sem("attn0_out_done")

        f_w1 = [sem(f"moe0_w1_loaded{n}") for n in range(2)]
        f_w2 = [sem(f"moe0_w2_loaded{n}") for n in range(2)]
        f_rw = sem("moe0_router_loaded")
        f_rs = sem("moe0_router_split_steps")
        f_lg = sem("moe0_logits_done")
        f_sig = sem("moe0_sigmoid_done")
        f_rt = sem("moe0_routing_steps")
        f_hid = sem("moe0_hidden_done")
        f_relu = sem("moe0_relu_done")
        f_sq = sem("moe0_hidden_squared")
        f_h1 = sem("moe0_w1_upper_done")
        f_l1 = sem("moe0_w1_lower_done")
        f_h2 = sem("moe0_w2_upper_done")
        f_l2 = sem("moe0_w2_lower_done")
        f_hh = sem("moe0_hidden_upper_done")
        f_hl = sem("moe0_hidden_lower_done")
        f_y = sem("moe0_y_done")
        f_acc = sem("moe0_y_added")
        s_ids = sem("expert_ids_made")

        q_w = sem("attn1_weights_loaded")
        q_vd = sem("attn1_v_done")
        q_va = sem("attn1_v_copied_by_scalar")
        q_vv = sem("attn1_v_copied_by_vector")
        q_proj = sem("attn1_qk_done")
        q_q = sem("attn1_q_copied")
        q_k = sem("attn1_k_copied")
        q_s = sem("attn1_scores_done")
        q_sub = sem("attn1_max_shifted")
        q_exp = sem("attn1_exp_done")
        q_p = sem("attn1_sum_recip_probs")
        q_pt = sem("attn1_probs_transposed")
        q_ptc = [sem(f"attn1_probsT_copied{n}") for n in range(2)]
        q_pv = sem("attn1_pv_done")
        q_oe = sem("attn1_even_copied")
        q_oo = sem("attn1_odd_copied")
        q_o = sem("attn1_out_done")
        s_x5 = sem("x5_written")
        s_hx = sem("x5_added_to_h")
        s_aff = [sem(f"ln{n}_affine_steps") for n in range(4, 6)]
        g_w1 = [sem(f"moe1_w1_loaded{n}") for n in range(2)]
        g_w2 = [sem(f"moe1_w2_loaded{n}") for n in range(2)]
        g_gb = sem("norm_gains_loaded")
        g_rs = sem("moe1_router_split_steps")
        g_lg = sem("moe1_logits_done")
        g_rt = sem("moe1_routing_steps")
        g_d = sem("moe1_top_difference")
        g_e = sem("moe1_logits_copied_top_exp")
        g_hid = sem("moe1_hidden_done")
        g_act = sem("moe1_gelu_done")
        g_h1 = sem("moe1_w1_upper_done")
        g_l1 = sem("moe1_w1_lower_done")
        g_h2 = sem("moe1_w2_upper_done")
        g_l2 = sem("moe1_w2_lower_done")
        g_hh = sem("moe1_hidden_upper_done")
        g_hl = sem("moe1_hidden_lower_done")
        g_y = sem("moe1_y_done")
        g_acc = sem("moe1_y_added")

        m_w = sem("ssm_weights_loaded")
        m_sell = sem("ssm_selector_loaded")
        m_pad = sem("ssm_pads_zeroed")
        m_xz = sem("ssm_xz_done")
        m_x = sem("ssm_x_copied")
        m_z = sem("ssm_z_gated")
        m_cv = sem("ssm_conv_taps")
        m_silu = sem("ssm_conv_silu")
        m_xd = sem("ssm_xdbl_done")
        m_xdc = sem("ssm_xdbl_copied")
        m_cst = sem("ssm_c_stored")
        m_cld = [sem(f"ssm_c_loaded{q}") for q in range(4)]
        m_bt = sem("ssm_b_transposed")
        m_bs = sem("ssm_b_split_steps")
        m_bsl = sem("ssm_b_selected")
        m_bsc = sem("ssm_b_selected_copied")
        m_bd = sem("ssm_b_blocks")
        m_dt = sem("ssm_dt_raw_done")
        m_se = sem("ssm_softplus_x_abs_exp")
        m_sw = sem("ssm_softplus_w")
        m_sr = sem("ssm_softplus_rest")
        m_sm = sem("ssm_softplus_max_less_rest")
        m_sl = sem("ssm_softplus_ln")
        m_dts = sem("ssm_dt_ready")
        m_du = sem("ssm_dtu_ready")
        m_dut = sem("ssm_dtu_transposed")
        m_p1 = sem("ssm_dtu_part1")
        m_r1 = sem("ssm_dtu_rest")
        m_p2 = sem("ssm_dtu_part2")
        m_p3 = sem("ssm_dtu_part3")
        m_ust = [sem(f"ssm_dtu_stored{u}") for u in range(UNITS)]
        m_lw = sem("ssm_dtu_loaded")
        m_ea = sem("ssm_a_exp")
        m_na = sem("ssm_a_negated")
        m_zero = sem("ssm_decay_starts_zeroed")
        m_dec = sem("ssm_decay_ready")
        m_b = sem("ssm_inputs_formed")
        m_scan = sem("ssm_scanned")
        m_mul = sem("ssm_times_c_by_pool")
        m_fold = sem("ssm_times_c_and_folded")

        def by_pool(chunk):
            return 2 * (chunk + 1 - (chunk + 1) // 4)
        m_y = sem("ssm_y_summed")
        m_post = sem("ssm_y_taken")
        m_yr = sem("ssm_yr_made")
        m_sum = sem("ssm_directions_added")
        m_g = sem("ssm_gated")
        m_o = sem("ssm_out_done")

        block = ctx.enter_context(nc.Block())

        @block.sync
        def _(sp):
            sp.dma_start(tok_w, io["tok_w"]).then_inc(s_tokw, 16)
            for k in range(PATCH_K):
                sp.dma_start(patches[:, k, :], io["patches"][:, k, :]).then_inc(s_patch[k], 16)
            sp.dma_start(wv, io["a0_wv"]).then_inc(s_w0, 16)
            sp.dma_start(wqk, io["a0_wqk"]).then_inc(s_w0, 16)
            sp.dma_start(wo, io["a0_wo"]).then_inc(s_w0, 16)
            sp.dma_start(frw, io["m0_router"]).then_inc(f_rw, 16)
            sp.dma_start(fbias, io["m0_bias"].partition_broadcast(128)).then_inc(f_rw, 16)
            for e in range(1 + EXPERTS):
                if e >= 2:
                    sp.wait_ge(f_l1, 2 * (e - 1))
                sp.dma_start(fw1[:, e % 2], io["m0_w1"][e]).then_inc(f_w1[e % 2], 16)
                if e >= 2:
                    sp.wait_ge(f_l2, 2 * (e - 1))
                sp.dma_start(fw2[:, e % 2], io["m0_w2"][e]).then_inc(f_w2[e % 2], 16)
            for n, (to, name) in enumerate(((m_in, "m_in"), (m_xp, "m_xp"), (m_dtw[0:RANK], "m_dtw"), (m_out, "m_out"),
                                            (m_conv, "m_conv"), (m_convb, "m_convb"), (m_dtb, "m_dtb"),
                                            (m_a, "m_a"), (m_d, "m_d"), (m_mask, "m_mask"))):
                sp.dma_start(to, io[name]).then_inc(m_w, 16)
            sp.wait_ge(s_xn, 8 * 3)
            sp.dma_start(m_sel.bitcast(mybir.dt.uint16), io["m_sel"]).then_inc(m_sell, 16)
            for d in range(2):
                sp.wait_ge(m_xdc, d + 1)
                sp.dma_start(c_dram[d].rearrange("b n t -> n b t"),
                             xdbl[RANK + STATE:44, d, :].rearrange("n (b t) -> n b t", t=64)).then_inc(m_cst, 16)

            def load_c(d, q):
                if d == 1:
                    sp.wait_ge(m_mul, by_pool(4 * (CTILES - 1) + q))
                    sp.wait_ge(m_fold, 3 * (CTILES - 1 + q // 3))
                sp.dma_start(cb[:, 2 * q:2 * q + 2].rearrange("p b n t -> p (b n t)"),
                             c_dram[d, 2 * q:2 * q + 2].rearrange("b n t -> (b n t)").partition_broadcast(128)
                             ).then_inc(m_cld[q], 16)

            def load_u(u):
                if u >= 2:
                    sp.wait_ge(m_b, 8 * (u - 1))
                if u >= 1:
                    sp.wait_ge(m_lw, 16 * COMBOS * u)
                sp.wait_ge(m_ust[u], 48)
                rows = u_dram[u].rearrange("i (g t) x -> i t g x", t=STEP)
                for c in range(COMBOS):
                    sp.dma_start(lw[c * STEP:(c + 1) * STEP, u % 2].rearrange("p g t d -> p g (t d)"),
                                 rows[PART_U[c]]).then_inc(m_lw, 16)

            def store_u(u):
                for i in range(3):
                    sp.wait_ge((m_p1, m_p2, m_p3)[i], u + 1)
                    sp.dma_start(u_dram[u, i], uparts[u][:, i].rearrange("p t d -> p (t d)")).then_inc(m_ust[u], 16)

            sp.wait_ge(m_cst, 32)
            load_c(0, 0)
            store_u(0)
            load_u(0)
            for u in range(1, UNITS):
                store_u(u)
            for u in range(2, UNITS):
                sp.wait_ge(m_ust[u], 48)
            for q in range(1, 4):
                load_c(0, q)
            load_u(1)
            for u in range(2, UNITS):
                load_u(u)
                if u == 3:
                    for q in range(4):
                        load_c(1, q)
            sp.dma_start(q_wqk, io["a1_wqk"]).then_inc(q_w, 16)
            sp.dma_start(q_wv, io["a1_wv"]).then_inc(q_w, 16)
            sp.dma_start(q_wo, io["a1_wo"]).then_inc(q_w, 16)
            sp.dma_start(gw1[0], io["m1_w1"][0]).then_inc(g_w1[0], 16)
            sp.wait_ge(m_b, 8 * UNITS)
            for n, name in enumerate(("ln1_g", "ln1_b", "ln2_g", "ln2_b")):
                sp.dma_start(ln_gb[n], io[name].partition_broadcast(128)).then_inc(g_gb, 16)
            sp.dma_start(grw, io["m1_router"]).then_inc(g_gb, 16)
            for e in range(EXPERTS):
                if e >= 1:
                    if e >= 2:
                        sp.wait_ge(g_l1, 2 * (e - 1))
                    sp.dma_start(gw1[e % 2], io["m1_w1"][e]).then_inc(g_w1[e % 2], 16)
                if e >= 2:
                    sp.wait_ge(g_l2, e - 1)
                sp.dma_start(gw2[e % 2], io["m1_w2"][e]).then_inc(g_w2[e % 2], 16)
            sp.wait_ge(g_acc, 8 + TILES * EXPERTS)
            sp.dma_start(out.rearrange("(t p) d -> p t d", p=128), h[:]).then_inc(s_out, 16)
            sp.wait_ge(s_out, 16)

        @block.gpsimd
        def _(pool):
            pool.memset(neg_half[:], -0.5).then_inc(s_nh, 1)
            pool.wait_ge(s_nh, 1)

            def ln_pool(n):
                pool.wait_ge(s_mo, TILES * (n + 1))
                pool.tensor_scalar(rstd[:], moments[:, :, 1], LN_EPS, None, ALU.add).then_inc(s_rs, 1)
                pool.wait_ge(s_rs, 2 * n + 1)
                pool.tensor_tensor(rstd[:], rstd[:], neg_half[:], ALU.pow).then_inc(s_rs, 1)

            pool.iota(expert_ids[:], [[0, TILES], [1, EXPERTS]], channel_multiplier=0,
                      allow_small_or_imprecise_dtypes=True).then_inc(s_ids, 1)
            pool.memset(fwt[:, :, 0:1], 1.0).then_inc(s_ids, 1)
            ln_pool(0)

            def lower_b(raw, hi, done, count):
                pool.wait_ge(done, count)
                pool.tensor_tensor(hi, raw, hi.bitcast(F32), ALU.subtract).then_inc(done, 1)
                pool.wait_ge(done, count + 1)

            def moe0_lower_w1(e, p):
                pool.wait_ge(f_h1, e + 1)
                pool.tensor_tensor(fw1l[:, p], fw1[:, p, :, 0], fw1h[:, p, :, 0].bitcast(F32), ALU.subtract).then_inc(f_l1, 1)
                lower_b(fw1[64:128, p, :, 1], fw1h[64:128, p, :, 1], f_l1, 2 * e + 1)

            def moe0_lower_w2(e, p):
                pool.wait_ge(f_h2, e + 1)
                pool.tensor_tensor(fw2l[:, p], fw2[:, p, 0], fw2h[:, p, 0].bitcast(F32), ALU.subtract).then_inc(f_l2, 1)
                lower_b(fw2[64:128, p, 1], fw2h[64:128, p, 1], f_l2, 2 * e + 1)

            moe0_lower_w1(0, 0)
            moe0_lower_w2(0, 0)
            moe0_lower_w1(1, 1)
            ln_pool(1)
            with pool.Fori(0, EXPERTS // 2 - 1) as i:
                for p in range(2):
                    moe0_lower_w1(2 * i + p + 2, p)
                    moe0_lower_w2(2 * i + p + 1, 1 - p)
            moe0_lower_w1(EXPERTS, 0)
            moe0_lower_w2(EXPERTS - 1, 1)
            moe0_lower_w2(EXPERTS, 0)
            pool.wait_ge(f_y, 1 + EXPERTS)
            pool.memset(xpad, 0.0).then_inc(m_pad, 1)
            ln_pool(2)

            pool.wait_ge(m_dts, 2)
            pool.wait_ge(m_silu, UNITS)
            pool.tensor_tensor(du[:, 1], dts[:, 1], xc[:, 1], ALU.mult).then_inc(m_du, 1)
            pool.wait_ge(m_dts, 2)
            pool.memset(decay[:, :, :, :, 0:1].rearrange("p a b n o -> p (a b n) o"), 0.0).then_inc(m_zero, 1)

            for B in range(8 * UNITS):
                u, b = B // 8, B % 8
                hb = hbuf[(B // 2) % 3][:, b % 2].rearrange("p n t -> p (n t)")
                if b >= 6:
                    continue
                if b % 2 == 0:
                    pool.wait_ge(m_cld[b // 2], 16 * (u // 3 + 1))
                pool.wait_ge(m_scan, B + 1)
                pool.tensor_tensor(hb, hb, cb[:, b].rearrange("p n t -> p (n t)"), ALU.mult).then_inc(m_mul, 1)
            ln_pool(3)
            ln_pool(4)

            def lower_w1(e, p):
                pool.wait_ge(g_h1, e + 1)
                pool.tensor_tensor(gw1l[p], gw1[p][:, :, 0], gw1h[p][:, :, 0].bitcast(F32), ALU.subtract).then_inc(g_l1, 1)
                lower_b(gw1[p][64:128, :, 1], gw1h[p][64:128, :, 1], g_l1, 2 * e + 1)

            def lower_w2(e, p):
                pool.wait_ge(g_h2, e + 1)
                pool.tensor_tensor(gw2l[p], gw2[p], gw2h[p].bitcast(F32), ALU.subtract).then_inc(g_l2, 1)

            lower_w1(0, 0)
            lower_w2(0, 0)
            lower_w1(1, 1)
            ln_pool(5)
            for t in range(TILES):
                pool.wait_ge(s_x5, t + 1)
                pool.tensor_tensor(h[:, t, :], h[:, t, :], x5[:, t, :], ALU.add).then_inc(s_hx, 1)
            with pool.Fori(0, EXPERTS // 2 - 1) as i:
                for p in range(2):
                    lower_w1(2 * i + p + 2, p)
                    lower_w2(2 * i + p + 1, 1 - p)
            lower_w2(EXPERTS - 1, 1)

        @block.scalar
        def _(act):
            act.dma_start(ident[:], io["ident"]).then_inc(s_const, 16)
            act.dma_start(causal, io["causal"]).then_inc(s_const, 16)
            act.dma_start(tok_b, io["tok_b"].partition_broadcast(128)).then_inc(s_const, 16)

            def ln_act(n, bank):
                act.wait_ge(s_xt, TILES * (TURN[n] + 1))
                act.activation(xta[:], PS[:, bank, :], ACT.Copy).then_inc(s_xta, 1)

            ln_act(0, 6)
            for r in range(2):
                act.wait_ge(a_v, r + 1)
                act.activation(vtok[:, 2 * r, :].rearrange("p (a n) -> p a n", a=2),
                               PS[:, 4 * r:4 * r + 2, 0:384], ACT.Copy).then_inc(a_va, 1)

            def q_copy(j):
                act.wait_ge(a_proj, j + 1)
                if j >= 2:
                    act.wait_ge(a_s, j - 1)
                act.activation(qT[:, j % 2, :], PS[:, 0, :], ACT.Copy).then_inc(a_q, 1)

            def exps(j):
                act.wait_ge(a_sub, 4 * j + 4)
                v = prob[:, j % 2].rearrange("p t a k -> p (t a k)")
                act.activation(v, v, ACT.Exp, scale=0.125).then_inc(a_exp, 1)

            def probT_copy(j):
                act.wait_ge(a_pt, j + 1)
                act.activation(probT.rearrange("p t n -> p (t n)"), PS[:, 4, :], ACT.Copy).then_inc(a_ptc, 1)

            def even_copy(j):
                act.wait_ge(a_pv, j + 1)
                act.activation(attnT[:, j, :].rearrange("p (t a q) -> p a t q", a=2, q=64)[:, 0],
                               PS[:, 5, 0:256].rearrange("p (t q) -> p t q", q=64), ACT.Copy).then_inc(a_oe, 1)

            q_copy(0)
            q_copy(1)
            exps(0)
            for j in range(PAIRS):
                if j + 2 < PAIRS:
                    q_copy(j + 2)
                probT_copy(j)
                if j + 1 < PAIRS:
                    exps(j + 1)
                even_copy(j)

            ln_act(1, 6)
            act.sem_inc(f_relu, 2)

            def moe0_relu(e, p):
                act.wait_ge(f_hid, e + 1)
                act.wait_ge(f_hl, e + 1)
                act.activation(frelu[:, p], PS[:, 2 * p:2 * p + 2, :], ACT.Relu).then_inc(f_relu, 1)
                act.wait_ge(f_relu, e + 3)
                act.activation(frelu[:, p], frelu[:, p], ACT.Square).then_inc(f_sq, 1)

            moe0_relu(0, 0)
            act.wait_ge(f_lg, 1)
            act.activation(fscore.rearrange("p t e -> p (t e)"), PS[:, 6, 0:TILES * EXPERTS],
                           ACT.Sigmoid).then_inc(f_sig, 1)
            with act.Fori(0, EXPERTS // 2) as i:
                moe0_relu(2 * i + 1, 1)
                moe0_relu(2 * i + 2, 0)

            ln_act(2, 6)
            for c in range(CTILES):
                k = 2 * (c % 2)
                act.wait_ge(m_xz, c + 1)
                if c == 0:
                    act.wait_ge(m_pad, 1)
                act.activation(xpad[:, c, :, 3:67], PS[:, k, :].rearrange("p (b t) -> p b t", t=64),
                               ACT.Copy).then_inc(m_x, 1)
                act.activation(zgate[:, c], PS[:, k + 1, :], ACT.Silu).then_inc(m_z, 1)
            def silu(d):
                for c in range(CTILES):
                    act.wait_ge(m_cv, 12 * d + 9 + c + 1)
                    act.activation(xc[:, d, c], xc[:, d, c], ACT.Silu).then_inc(m_silu, 1)

            def xdbl_copy(d):
                act.wait_ge(m_xd, d + 1)
                act.activation(xdbl[0:44, d, :], PS[0:44, 4 + d, :], ACT.Copy).then_inc(m_xdc, 1)

            def softplus_exp(d):
                for c in range(CTILES):
                    act.wait_ge(m_dt, 3 * d + c + 1)
                    act.activation(softx[:, d, c], PS[:, (6, 7, 0)[c], :], ACT.Identity,
                                   bias=m_dtb[:, d, c:c + 1]).then_inc(m_se, 1)
                act.wait_ge(m_se, 5 * d + 3)
                act.activation(softe[:, d], softx[:, d], ACT.Abs).then_inc(m_se, 1)
                act.wait_ge(m_se, 5 * d + 4)
                act.activation(softe[:, d], softe[:, d], ACT.Exp, scale=-1.0).then_inc(m_se, 1)

            def bsel_copy(d):
                act.wait_ge(m_bsl, d + 1)
                act.activation(bsel[:, d].rearrange("p t g n -> p g t n"),
                               PS[:, 4 + d, :].rearrange("p (g t n) -> p g t n", g=8, n=STATE),
                               ACT.Copy).then_inc(m_bsc, 1)

            silu(0)
            xdbl_copy(0)
            silu(1)
            softplus_exp(0)
            act.activation(m_a.rearrange("p d c n -> p (d c n)"), m_a.rearrange("p d c n -> p (d c n)"),
                           ACT.Exp).then_inc(m_ea, 1)
            xdbl_copy(1)
            bsel_copy(0)
            softplus_exp(1)
            bsel_copy(1)
            for d in range(2):
                act.wait_ge(m_sw, d + 1)
                act.activation(dts[:, d], softw[d], ACT.Ln).then_inc(m_sl, 1)

            def part1(u):
                act.wait_ge(m_dut, u + 1)
                act.activation(uparts[u][:, 0].rearrange("p t d -> p (t d)"), PS[:, 2 + u % 2, :],
                               ACT.Copy).then_inc(m_p1, 1)

            def part2(u):
                act.wait_ge(m_r1, u + 1)
                act.activation(uparts[u][:, 1].rearrange("p t d -> p (t d)"), dr[:, u % 2],
                               ACT.Copy).then_inc(m_p2, 1)

            def decays(u, half, states=range(STATE)):
                if states[0] == 0 and u >= 1:
                    act.wait_ge(m_scan, 8 * (u - 1) + 4 * half + 4)
                for n in states:
                    i = act.activation(decay[:, half, :, n, 1:64],
                                       dts[:, u // 3, u % 3, 256 * half:256 * half + 256]
                                       .rearrange("p (b t) -> p b t", t=64)[:, :, 1:64],
                                       ACT.Exp, scale=m_a[:, u // 3, u % 3, n:n + 1])
                if states[-1] == STATE - 1:
                    i.then_inc(m_dec, 1)

            part1(0)
            part1(1)
            part2(0)
            part1(2)
            part2(1)
            act.wait_ge(m_zero, 1)
            act.wait_ge(m_na, 1)
            for u in range(2, UNITS):
                if u + 1 < UNITS:
                    part1(u + 1)
                decays(0, 0, range(4 * u - 8, 4 * u - 4))
                part2(u)
            decays(0, 1)
            for u in range(1, UNITS):
                for half in range(2):
                    decays(u, half)

            ln_act(4, 6)
            act.wait_ge(q_vd, 1)
            act.activation(q_v[:, 0:2, :], PS[:, 2:4, 0:384], ACT.Copy).then_inc(q_va, 1)

            def quad_q_copy(j):
                act.wait_ge(q_proj, j + 1)
                act.activation(q_qT[:, j % 2, :], PS[:, 0, :], ACT.Copy).then_inc(q_q, 1)

            def quad_exps(j):
                act.wait_ge(q_sub, 2 * j + 2)
                v = q_prob[:, j % 2].rearrange("p m t a k -> p (m t a k)")
                act.activation(v, v, ACT.Exp, scale=0.25).then_inc(q_exp, 1)

            def quad_probT_copy(j):
                act.wait_ge(q_pt, 1 + 2 * j)
                act.activation(q_probT[:, 0:2].rearrange("p m t n -> p (m t n)"), PS[:, 6, :],
                               ACT.Copy).then_inc(q_ptc[0], 1)

            def quad_even_copy(j):
                act.wait_ge(q_pv, j + 1)
                act.activation(q_attnT[:, j, :].rearrange("p (t a q) -> p a t q", a=2, q=64)[:, 0],
                               PS[:, 0, 0:256].rearrange("p (t q) -> p t q", q=64), ACT.Copy).then_inc(q_oe, 1)

            quad_q_copy(0)
            quad_q_copy(1)
            quad_exps(0)
            for j in range(QUADS):
                quad_probT_copy(j)
                if j + 1 < QUADS:
                    quad_exps(j + 1)
                quad_even_copy(j)
                if j + 2 < QUADS:
                    quad_q_copy(j + 2)
            ln_act(5, 6)
            def moe1_gelu(e, p, first=False):
                for m in range(3):
                    k = 2 * ((3 * p + m) % 2)
                    act.wait_ge(g_hid, 3 * e + m + 1)
                    if not first:
                        act.wait_ge(g_hl, 3 * (e - 1) + m + 1)
                    act.activation(gact[m], PS[:, k:k + 2, :], ACT.Gelu).then_inc(g_act, 1)

            moe1_gelu(0, 0, first=True)
            act.wait_ge(g_lg, 1)
            act.activation(glog.rearrange("p t e -> p (t e)"), PS[:, 6, 0:TILES * EXPERTS], ACT.Copy).then_inc(g_e, 1)
            moe1_gelu(1, 1)
            act.wait_ge(g_d, 1)
            act.activation(gpair[:, 1], gpair[:, 1], ACT.Exp).then_inc(g_e, 1)
            with act.Fori(1, EXPERTS // 2) as i:
                moe1_gelu(2 * i, 0)
                moe1_gelu(2 * i + 1, 1)

        @block.vector
        def _(dve):
            dve.wait_ge(s_const, 48)
            for t in range(TILES):
                dve.wait_ge(s_tok, t + 1)
                dve.tensor_tensor(h[:, t, :], PS[:, t, 0:DIM], tok_b, ALU.add).then_inc(s_h, 1)

            def ln_moments(n, src, src_sem, src_count, each=1):
                for t in range(TILES):
                    dve.wait_ge(src_sem, src_count + each * (t + 1))
                    dve.bn_stats(stats[:, t, :], src[:, t, :]).then_inc(s_st, 1)
                for t in range(TILES):
                    dve.wait_ge(s_st, TILES * n + t + 1)
                    dve.bn_aggr(moments[:, t, :], stats[:, t, :]).then_inc(s_mo, 1)
                dve.wait_ge(s_rs, 2 * n + 2)

            def upper_part(to, src):
                return dve.tensor_copy(to, src)

            def lower_part(to, src, hi):
                return dve.tensor_tensor(to, src, hi.bitcast(F32), ALU.subtract)

            def xtb_copy(n, bank):
                dve.wait_ge(s_xt, TILES * (TURN[n] + 1))
                dve.tensor_copy(xtb[:], PS[:, bank, :]).then_inc(s_xtb, 4)

            def split_x(n, bank):
                turn = TURN[n]
                dve.wait_ge(s_xt, TILES * (turn + 1))
                upper_part(xh[:, 1], PS[:, bank, :]).then_inc(s_xtb, 1)
                dve.wait_ge(s_xta, turn + 1)
                upper_part(xh[:, 0], xta[:]).then_inc(s_xtb, 1)
                dve.wait_ge(s_xtb, 4 * turn + 1)
                lower_part(xl[:, 1], PS[:, bank, :], xh[:, 1]).then_inc(s_xtb, 1)
                dve.wait_ge(s_xtb, 4 * turn + 2)
                lower_part(xl[:, 0], xta[:], xh[:, 0]).then_inc(s_xtb, 1)

            def ln_vector(n, src, src_sem, src_count, bank, split=False):
                ln_moments(n, src, src_sem, src_count)
                for t in range(TILES):
                    for to, cols in ((slice(0, DIM), slice(0, DIM)), (slice(DIM, 256), slice(128, DIM))):
                        dve.tensor_scalar(xn[:, t, to], src[:, t, cols], moments[:, t, 0:1], rstd[:, t:t + 1],
                                          ALU.subtract, ALU.mult).then_inc(s_xn, 1)
                (split_x if split else xtb_copy)(n, bank)

            def ln_plain(n, src, src_sem, src_count, to):
                ln_moments(n, src, src_sem, src_count)
                for t in range(TILES):
                    dve.tensor_scalar(to[:, t, 0:DIM], src[:, t, :], moments[:, t, 0:1], rstd[:, t:t + 1],
                                      ALU.subtract, ALU.mult).then_inc(s_xn, 2)

            def ln_affine(n, src, src_sem, src_count, each, bank, split=False):
                gamma, beta = ln_gb[2 * (n - 4)], ln_gb[2 * (n - 4) + 1]
                steps = s_aff[n - 4]
                dve.wait_ge(g_gb, 80)
                ln_moments(n, src, src_sem, src_count, each)
                for t in range(TILES):
                    dve.tensor_scalar(xn[:, t, 0:DIM], src[:, t, :], moments[:, t, 0:1], rstd[:, t:t + 1],
                                      ALU.subtract, ALU.mult).then_inc(steps, 1)
                dve.wait_ge(steps, TILES)
                dve.tensor_tensor(xn[:, :, 0:DIM], xn[:, :, 0:DIM],
                                  gamma.unsqueeze(1).to_broadcast([128, TILES, DIM]), ALU.mult).then_inc(steps, 1)
                dve.wait_ge(steps, TILES + 1)
                dve.tensor_tensor(xn[:, :, DIM:256], xn[:, :, 128:DIM],
                                  beta[:, 128:DIM].unsqueeze(1).to_broadcast([128, TILES, 64]),
                                  ALU.add).then_inc(steps, 1)
                dve.wait_ge(steps, TILES + 2)
                dve.tensor_tensor(xn[:, :, 0:DIM], xn[:, :, 0:DIM],
                                  beta.unsqueeze(1).to_broadcast([128, TILES, DIM]),
                                  ALU.add).then_inc(s_xn, 2 * TILES)
                (split_x if split else xtb_copy)(n, bank)

            ln_vector(0, h, s_h, 0, 7)
            for r in range(2):
                dve.wait_ge(a_v, r + 1)
                dve.tensor_copy(vtok[:, 2 * r + 1, :].rearrange("p (a n) -> p a n", a=2),
                                PS[:, 4 * r + 2:4 * r + 4, 0:384]).then_inc(a_vd, 1)

            def k_copy(j):
                dve.wait_ge(a_proj, j + 1)
                if j >= 2:
                    dve.wait_ge(a_s, j - 1)
                dve.tensor_copy(kT[:, j % 2, :], PS[:, 1, :]).then_inc(a_k, 1)

            def shift(j):
                b = j % 2
                dve.wait_ge(a_s, j + 1)
                if j >= 2:
                    dve.wait_ge(a_pt, j - 1)
                sc = prob[:, b]
                flat = sc.rearrange("p t a k -> p (t a) k")
                for a in range(2):
                    dve.tensor_tensor(sc[:, :, a], PS[:, 2 + a, 0:256].rearrange("p (t k) -> p t k", k=64),
                                      causal.unsqueeze(1).to_broadcast([128, 4, 64]),
                                      ALU.add).then_inc(a_sub, 1)
                dve.wait_ge(a_sub, 4 * j + 2)
                dve.tensor_reduce(rowmax[:, b, :], flat, AX.X, ALU.max).then_inc(a_sub, 1)
                dve.wait_ge(a_sub, 4 * j + 3)
                dve.tensor_tensor(flat, flat, rowmax[:, b, :].unsqueeze(2).to_broadcast([128, 8, 64]),
                                  ALU.subtract).then_inc(a_sub, 1)

            def normalise(j):
                b = j % 2
                flat = prob[:, b].rearrange("p t a k -> p (t a) k")
                dve.wait_ge(a_exp, j + 1)
                dve.tensor_reduce(rowsum[:, b, :], flat, AX.X, ALU.add).then_inc(a_p, 1)
                dve.wait_ge(a_p, 3 * j + 1)
                dve.reciprocal(rowsum[:, b, :], rowsum[:, b, :]).then_inc(a_p, 1)
                dve.wait_ge(a_p, 3 * j + 2)
                dve.tensor_tensor(flat, flat, rowsum[:, b, :].unsqueeze(2).to_broadcast([128, 8, 64]),
                                  ALU.mult).then_inc(a_p, 1)

            def odd_copy(j):
                dve.wait_ge(a_pv, j + 1)
                dve.tensor_copy(attnT[:, j, :].rearrange("p (t a q) -> p a t q", a=2, q=64)[:, 1],
                                PS[:, 6, 0:256].rearrange("p (t q) -> p t q", q=64)).then_inc(a_oo, 1)

            k_copy(0)
            k_copy(1)
            shift(0)

            def moe0_upper_w1(e, p, loads):
                dve.wait_ge(f_w1[p], 16 * loads)
                upper_part(fw1h[:, p], fw1[:, p]).then_inc(f_h1, 1)

            def moe0_upper_w2(e, p, loads, first=False):
                dve.wait_ge(f_w2[p], 16 * loads)
                if not first:
                    dve.wait_ge(f_y, e - 1)
                upper_part(fw2h[:, p], fw2[:, p]).then_inc(f_h2, 1)

            def split_router(raw, hi, lo, done):
                upper_part(hi, raw).then_inc(done, 1)
                dve.wait_ge(done, 1)
                lower_part(lo, raw[:, 0], hi[:, 0]).then_inc(done, 1)
                lower_part(hi[64:128, 1], raw[64:128, 1], hi[64:128, 1]).then_inc(done, 1)

            for j in range(PAIRS):
                normalise(j)
                if j + 2 < PAIRS:
                    k_copy(j + 2)
                if j + 1 < PAIRS:
                    shift(j + 1)
                odd_copy(j)
                if j == PAIRS - 2:
                    moe0_upper_w1(0, 0, 1)
                    moe0_upper_w2(0, 0, 1, first=True)
                    moe0_upper_w1(1, 1, 1)
                    dve.wait_ge(f_rw, 32)
                    split_router(frw, frwh, frwl, f_rs)
            for t in range(TILES):
                dve.wait_ge(a_o, t + 1)
                dve.tensor_tensor(h[:, t, :], h[:, t, :], PS[:, t, 0:DIM], ALU.add).then_inc(s_h, 1)

            ln_vector(1, h, s_h, 4, 7, split=True)
            dve.sem_inc(f_acc, 8)
            dve.sem_inc(f_hl, 2)

            def moe0_split_hidden(e, p):
                dve.wait_ge(f_sq, e + 1)
                upper_part(fhh[:, p], frelu[:, p]).then_inc(f_hh, 1)
                dve.wait_ge(f_hh, e + 1)
                lower_part(fhl[:, p], frelu[:, p], fhh[:, p]).then_inc(f_hl, 1)

            def moe0_add(e, p):
                dve.wait_ge(f_y, e + 1)
                for t in range(TILES):
                    dve.wait_ge(f_acc, TILES * e + t + 5)
                    dve.scalar_tensor_tensor(h[:, t, :], PS[:, 4 + 2 * p + t % 2, (t // 2) * DIM:(t // 2 + 1) * DIM],
                                             fwt[:, t, bass.ds(e, 1)], h[:, t, :],
                                             ALU.mult, ALU.add).then_inc(f_acc, 1)

            steps = [0]

            def routing_step(ins):
                steps[0] += 1
                ins.then_inc(f_rt, 1)
                dve.wait_ge(f_rt, steps[0])

            def moe0_step(e, p, w1_loads, w2_loads):
                moe0_upper_w2(e + 1, 1 - p, w2_loads)
                if w1_loads is not None:
                    dve.wait_ge(f_hid, e + 1)
                    moe0_upper_w1(e + 2, p, w1_loads)
                moe0_split_hidden(e + 1, 1 - p)

            moe0_split_hidden(0, 0)
            moe0_upper_w2(1, 1, 1, first=True)
            dve.wait_ge(f_hid, 1)
            moe0_upper_w1(2, 0, 2)
            dve.wait_ge(f_sig, 1)
            dve.wait_ge(f_rw, 32)
            dve.wait_ge(s_ids, 2)
            routing_step(dve.tensor_tensor(fpick, fscore, fbias.unsqueeze(1).to_broadcast([128, TILES, EXPERTS]),
                                           ALU.add))
            for t in range(TILES):
                routing_step(dve.max(ftop[:, t, :], fpick[:, t, :]))
                routing_step(dve.max_index(fidx[:, t, :], ftop[:, t, :], fpick[:, t, :]))
            routing_step(dve.tensor_copy(fidxf, fidx[:, :, 0:2]))
            for k in range(2):
                routing_step(dve.tensor_tensor(fhot[:, k], expert_ids[:],
                                               fidxf[:, :, k:k + 1].to_broadcast([128, TILES, EXPERTS]),
                                               ALU.is_equal))
            routing_step(dve.tensor_tensor(fhot[:, 0], fhot[:, 0], fhot[:, 1], ALU.add))
            routing_step(dve.tensor_tensor(fhot[:, 0], fhot[:, 0], fscore, ALU.mult))
            routing_step(dve.tensor_reduce(fsum, fhot[:, 0], AX.X, ALU.add))
            routing_step(dve.tensor_scalar(fsum, fsum, 1e-20, None, ALU.add))
            routing_step(dve.reciprocal(fsum, fsum))
            routing_step(dve.tensor_tensor(fwt[:, :, 1:1 + EXPERTS], fhot[:, 0],
                                           fsum.unsqueeze(2).to_broadcast([128, TILES, EXPERTS]), ALU.mult))
            moe0_split_hidden(1, 1)
            moe0_add(0, 0)
            with dve.Fori(0, EXPERTS // 2 - 1) as i:
                for q in range(2):
                    moe0_step(2 * i + 1 + q, 1 - q, i + 2 + q, i + 2)
                    moe0_add(2 * i + 1 + q, 1 - q)
            moe0_step(EXPERTS - 1, 1, None, EXPERTS // 2 + 1)
            moe0_add(EXPERTS - 1, 1)
            moe0_add(EXPERTS, 0)

            ln_vector(2, h, f_acc, 8 + TILES * EXPERTS, 7)
            dve.wait_ge(m_w, 160)
            for d in range(2):
                for k in range(TAPS):
                    for c in range(CTILES):
                        taps = xpad[:, c, :, k:k + 64] if d == 0 else xpad[:, c, :, 69 - k:5 - k:-1]
                        acc = xc[:, d, c].rearrange("p (b t) -> p b t", t=64)
                        if k == 0:
                            if d == 0:
                                dve.wait_ge(m_x, c + 1)
                            dve.tensor_scalar(acc, taps, m_conv[:, d, c, 0:1], m_convb[:, d, c:c + 1],
                                              ALU.mult, ALU.add).then_inc(m_cv, 1)
                        else:
                            dve.wait_ge(m_cv, 12 * d + 3 * (k - 1) + c + 1)
                            dve.scalar_tensor_tensor(acc, taps, m_conv[:, d, c, k:k + 1], acc,
                                                     ALU.mult, ALU.add).then_inc(m_cv, 1)

            bsteps = [0]

            def split_step(ins):
                bsteps[0] += 1
                ins.then_inc(m_bs, 1)
                dve.wait_ge(m_bs, bsteps[0])

            def split_b(d):
                dve.wait_ge(m_bt, d + 1)
                raw = bts[:, d]
                part = [bparts[:, d, i] for i in range(3)]
                split_step(dve.tensor_copy(raw, PS[:, 4 + d, 0:TILES * 44]
                                           .rearrange("p (t r) -> p t r", r=44)[:, :, RANK:RANK + STATE]))
                split_step(dve.tensor_copy(part[0], raw))
                split_step(dve.tensor_tensor(raw, raw, part[0], ALU.subtract))
                split_step(dve.tensor_copy(part[1], raw))
                split_step(dve.tensor_tensor(part[2], raw, part[1], ALU.subtract))

            def softplus_vector(d):
                dve.wait_ge(m_se, 5 * d + 5)
                dve.tensor_scalar(softw[d], softe[:, d], 1.0, None, ALU.add).then_inc(m_sw, 1)
                dve.wait_ge(m_sw, d + 1)
                dve.scalar_tensor_tensor(softe[:, d], softw[d], 1.0, softe[:, d],
                                         ALU.subtract, ALU.subtract).then_inc(m_sr, 1)
                dve.wait_ge(m_sr, d + 1)
                dve.scalar_tensor_tensor(softx[:, d], softx[:, d], 0.0, softe[:, d],
                                         ALU.max, ALU.subtract).then_inc(m_sm, 1)

            def dt_and_dtu(d):
                dve.wait_ge(m_sl, d + 1)
                dve.wait_ge(m_sm, d + 1)
                dve.tensor_tensor(dts[:, d], dts[:, d], softx[:, d], ALU.add).then_inc(m_dts, 1)
                if d == 0:
                    dve.wait_ge(m_dts, 1)
                    dve.wait_ge(m_silu, CTILES)
                    dve.tensor_tensor(du[:, 0], dts[:, 0], xc[:, 0], ALU.mult).then_inc(m_du, 1)

            def rest1(u):
                dve.wait_ge(m_p1, u + 1)
                if u >= 2:
                    dve.wait_ge(m_p3, u - 1)
                dve.tensor_tensor(dr[:, u % 2], PS[:, 2 + u % 2, :],
                                  uparts[u][:, 0].rearrange("p t d -> p (t d)"), ALU.subtract).then_inc(m_r1, 1)

            def part3(u):
                dve.wait_ge(m_p2, u + 1)
                dve.tensor_tensor(uparts[u][:, 2].rearrange("p t d -> p (t d)"), dr[:, u % 2],
                                  uparts[u][:, 1].rearrange("p t d -> p (t d)"), ALU.subtract).then_inc(m_p3, 1)

            def b_blocks(d, quarter):
                dve.wait_ge(m_bsc, d + 1)
                for t in range(4 * quarter, 4 * quarter + 4):
                    dve.tensor_scalar(bd[:, d, :, t, :], bsel[:, d].rearrange("p t g n -> p (t g) n"),
                                      m_mask[:, t:t + 1], None, ALU.mult).then_inc(m_bd, 1)

            split_b(0)
            softplus_vector(0)
            split_b(1)
            dve.wait_ge(m_ea, 1)
            dve.tensor_scalar(m_a.rearrange("p d c n -> p (d c n)"), m_a.rearrange("p d c n -> p (d c n)"),
                              -1.0, None, ALU.mult).then_inc(m_na, 1)
            softplus_vector(1)
            dt_and_dtu(0)
            dt_and_dtu(1)
            rest1(0)
            for u in range(UNITS):
                if u + 1 < UNITS:
                    rest1(u + 1)
                part3(u)
                if 1 <= u < 5:
                    b_blocks(0, u - 1)

            def take_y(u, half):
                d, c = u // 3, u % 3
                cols = slice(256 * half, 256 * half + 256)
                dve.wait_ge(m_y, 4 * u + 2 * half + 2)
                to = yf[:, c, cols] if d == 0 else yr[:, half]
                dve.scalar_tensor_tensor(to, xc[:, d, c, cols], m_d[:, d, c:c + 1],
                                         PS[:, 4 + half, 0:256], ALU.mult, ALU.add).then_inc(m_post, 1)
                if d == 1:
                    n = 2 * c + half + 1
                    dve.wait_ge(m_post, 2 * u + half + 1)
                    f = yf[:, c, cols].rearrange("p (b t) -> p b t", t=64)
                    dve.tensor_tensor(f, f, yr[:, half].rearrange("p (b t) -> p b t", t=64)[:, :, ::-1],
                                      ALU.add).then_inc(m_sum, 1)
                    dve.wait_ge(m_sum, n)
                    dve.tensor_tensor(zgate[:, c, cols], yf[:, c, cols], zgate[:, c, cols],
                                      ALU.mult).then_inc(m_g, 1)

            for B in range(8 * UNITS):
                u, b = B // 8, B % 8
                chunk = B // 2
                dve.wait_ge(m_b, B + 1)
                if b % 4 == 0:
                    dve.wait_ge(m_dec, 2 * u + b // 4 + 1)
                if b % 2 == 0 and chunk >= 3:
                    dve.wait_ge(m_y, chunk - 2)
                if B == 4:
                    dve.wait_ge(m_cst, 32)
                    dve.wait_ge(m_ust[0], 48)
                    dve.wait_ge(m_ust[1], 48)
                dve.tensor_tensor_scan(hbuf[chunk % 3][:, b % 2].rearrange("p n t -> p (n t)"),
                                       decay[:, b // 4, b % 4].rearrange("p n t -> p (n t)"),
                                       PS[:, 2 * (b % 2):2 * (b % 2) + 2, :].rearrange("p k x -> p (k x)"),
                                       0.0, ALU.mult, ALU.add).then_inc(m_scan, 1)
                if b == 7:
                    hb = hbuf[chunk % 3]
                    dve.wait_ge(m_cld[3], 16 * (u // 3 + 1))
                    for a in range(2):
                        dve.wait_ge(m_scan, B + a)
                        dve.tensor_tensor(hb[:, a], hb[:, a], cb[:, 6 + a], ALU.mult).then_inc(m_fold, 1)
                    dve.wait_ge(m_fold, 3 * u + 2)
                    dve.tensor_tensor(hb[:, :, 0:8], hb[:, :, 0:8], hb[:, :, 8:16], ALU.add).then_inc(m_fold, 1)
                if B in (9, 11, 13, 15):
                    b_blocks(1, (B - 9) // 2)
                if b % 4 == 0 and chunk >= 4:
                    half_no = (chunk - 4) // 2
                    take_y(half_no // 2, half_no % 2)
            take_y(UNITS - 1, 0)
            take_y(UNITS - 1, 1)
            for t in range(TILES):
                dve.wait_ge(m_o, t + 1)
                dve.tensor_tensor(h[:, t, :], h[:, t, :], PS[:, t, 0:DIM], ALU.add).then_inc(s_h, 1)

            ln_plain(3, h, s_h, 8, x4)
            ln_affine(4, x4, s_xn, 8 * 3, 2, 7)
            dve.wait_ge(q_vd, 2)
            dve.tensor_copy(q_v[:, 2:4, :], PS[:, 4:6, 0:384]).then_inc(q_vv, 1)

            def quad_k_copy(j):
                dve.wait_ge(q_proj, j + 1)
                dve.tensor_copy(q_kT[:, j % 2, :], PS[:, 1, :]).then_inc(q_k, 1)

            def quad_shift(j):
                b = j % 2
                dve.wait_ge(q_s, j + 1)
                sc = PS[:, 2:6, 0:256].rearrange("p m (x k) -> p m x k", k=64)
                mx = q_max[:, b].rearrange("p (m x) -> p m x", m=4)
                dve.tensor_reduce(mx, sc, AX.X, ALU.max).then_inc(q_sub, 1)
                dve.wait_ge(q_sub, 2 * j + 1)
                dve.tensor_tensor(q_prob[:, b].rearrange("p m t a k -> p m (t a) k"), sc,
                                  mx.unsqueeze(3).to_broadcast([128, 4, 4, 64]), ALU.subtract).then_inc(q_sub, 1)

            def quad_normalise(j):
                b = j % 2
                flat = q_prob[:, b].rearrange("p m t a k -> p (m t a) k")
                dve.wait_ge(q_exp, j + 1)
                dve.tensor_reduce(q_sum[:, b], flat, AX.X, ALU.add).then_inc(q_p, 1)
                dve.wait_ge(q_p, 3 * j + 1)
                dve.reciprocal(q_sum[:, b], q_sum[:, b]).then_inc(q_p, 1)
                dve.wait_ge(q_p, 3 * j + 2)
                dve.tensor_tensor(flat, flat, q_sum[:, b].unsqueeze(2).to_broadcast([128, 16, 64]),
                                  ALU.mult).then_inc(q_p, 1)

            def quad_probT_copy_b(j):
                dve.wait_ge(q_pt, 2 + 2 * j)
                dve.tensor_copy(q_probT[:, 2:4].rearrange("p m t n -> p (m t n)"), PS[:, 7, :]).then_inc(q_ptc[1], 1)

            def quad_odd_copy(j):
                dve.wait_ge(q_pv, j + 1)
                dve.tensor_copy(q_attnT[:, j, :].rearrange("p (t a q) -> p a t q", a=2, q=64)[:, 1],
                                PS[:, 1, 0:256].rearrange("p (t q) -> p t q", q=64)).then_inc(q_oo, 1)

            quad_k_copy(0)
            quad_k_copy(1)

            def upper_w1(e, p, loads):
                dve.wait_ge(g_w1[p], 16 * loads)
                upper_part(gw1h[p], gw1[p]).then_inc(g_h1, 1)

            def upper_w2(e, p, loads, first=False):
                dve.wait_ge(g_w2[p], 16 * loads)
                if not first:
                    dve.wait_ge(g_y, e - 1)
                upper_part(gw2h[p], gw2[p]).then_inc(g_h2, 1)

            quad_shift(0)
            for j in range(QUADS):
                quad_normalise(j)
                quad_probT_copy_b(j)
                if j + 1 < QUADS:
                    quad_shift(j + 1)
                quad_odd_copy(j)
                if j == 0:
                    upper_w1(0, 0, 1)
                    upper_w2(0, 0, 1, first=True)
                    upper_w1(1, 1, 1)
                    dve.wait_ge(g_gb, 80)
                    split_router(grw, grwh, grwl, g_rs)
                if j + 2 < QUADS:
                    quad_k_copy(j + 2)
            for t in range(TILES):
                dve.wait_ge(q_o, t + 1)
                dve.tensor_tensor(x5[:, t, :], x4[:, t, :], PS[:, t, 0:DIM], ALU.add).then_inc(s_x5, 1)
            ln_affine(5, x5, s_x5, 0, 1, 7, split=True)
            dve.sem_inc(g_acc, 8)

            def moe1_add(e, p):
                dve.wait_ge(g_y, e + 1)
                for t in range(TILES):
                    dve.wait_ge(g_acc, TILES * e + t + 5)
                    dve.scalar_tensor_tensor(h[:, t, :], PS[:, 4 + 2 * p + t % 2, (t // 2) * DIM:(t // 2 + 1) * DIM],
                                             gwt[:, t, bass.ds(e, 1)], h[:, t, :],
                                             ALU.mult, ALU.add).then_inc(g_acc, 1)

            def split_hidden(e, p):
                for m in range(3):
                    pair = slice(2 * m, 2 * m + 2)
                    dve.wait_ge(g_act, 3 * e + m + 1)
                    upper_part(ghh[p][:, pair], gact[m]).then_inc(g_hh, 1)
                    dve.wait_ge(g_hh, 3 * e + m + 1)
                    lower_part(ghl[p][:, pair], gact[m], ghh[p][:, pair]).then_inc(g_hl, 1)

            split_hidden(0, 0)
            dve.wait_ge(g_hid, 3)
            upper_w1(2, 0, 2)
            split_hidden(1, 1)
            upper_w2(1, 1, 1, first=True)
            steps1 = [0]

            def routing1_step(ins):
                steps1[0] += 1
                ins.then_inc(g_rt, 1)
                dve.wait_ge(g_rt, steps1[0])

            dve.wait_ge(g_e, 1)
            for t in range(TILES):
                routing1_step(dve.max(gtop[:, t, :], glog[:, t, :]))
                routing1_step(dve.max_index(gidx[:, t, :], gtop[:, t, :], glog[:, t, :]))
            dve.tensor_tensor(gpair[:, 1], gtop[:, :, 1], gtop[:, :, 0], ALU.subtract).then_inc(g_d, 1)
            routing1_step(dve.tensor_copy(gidxf, gidx[:, :, 0:2]))
            dve.wait_ge(g_e, 2)
            routing1_step(dve.tensor_scalar(gpair[:, 0], gpair[:, 1], 1.0, None, ALU.add))
            routing1_step(dve.reciprocal(gpair[:, 0], gpair[:, 0]))
            routing1_step(dve.tensor_tensor(gpair[:, 1], gpair[:, 1], gpair[:, 0], ALU.mult))
            for k in range(2):
                routing1_step(dve.tensor_tensor(ghot[:, k], expert_ids[:],
                                                gidxf[:, :, k:k + 1].to_broadcast([128, TILES, EXPERTS]),
                                                ALU.is_equal))
                routing1_step(dve.tensor_tensor(ghot[:, k], ghot[:, k],
                                                gpair[:, k].unsqueeze(2).to_broadcast([128, TILES, EXPERTS]),
                                                ALU.mult))
            routing1_step(dve.tensor_tensor(gwt, ghot[:, 0], ghot[:, 1], ALU.add))
            dve.wait_ge(s_hx, TILES)

            moe1_add(0, 0)

            def moe1_step(e, p, w1_loads, w2_loads):
                if w1_loads is not None:
                    dve.wait_ge(g_hid, 3 * e + 3)
                    upper_w1(e + 2, p, w1_loads)
                split_hidden(e + 1, 1 - p)
                upper_w2(e + 1, 1 - p, w2_loads)
                moe1_add(e, p)

            with dve.Fori(0, EXPERTS // 2 - 2) as i:
                for q in range(2):
                    moe1_step(2 * i + 1 + q, 1 - q, i + 2 + q, i + 2)
            moe1_step(EXPERTS - 3, 1, EXPERTS // 2, EXPERTS // 2)
            moe1_step(EXPERTS - 2, 0, None, EXPERTS // 2)
            moe1_add(EXPERTS - 1, 1)

        @block.tensor
        def _(pe):
            pe.wait_ge(s_tokw, 16)
            for k in range(PATCH_K):
                pe.wait_ge(s_patch[k], 16)
                for t in range(TILES):
                    mm = pe.matmul(PS[:, t, 0:DIM], patches[:, k, t * 128:t * 128 + 128], tok_w[:, k, :],
                                   start=(k == 0), stop=(k == PATCH_K - 1))
                    if k == PATCH_K - 1:
                        mm.then_inc(s_tok, 1)
            pe.wait_ge(s_const, 48)

            def keep_warm(products, bank=6, moving=xta[:]):
                for _ in range(products):
                    pe.matmul(PS[:, bank, :], ident[:], moving, start=True, stop=True)

            def ln_tensor(n, bank_a, bank_b):
                for t in range(TILES):
                    cols = slice(t * 128, t * 128 + 128)
                    pe.wait_ge(s_xn, 8 * n + 2 * t + 2)
                    pe.transpose(PS[:, bank_a, cols], xn[:, t, 0:128], ident[:])
                    pe.transpose(PS[:, bank_b, cols], xn[:, t, 128:256], ident[:]).then_inc(s_xt, 1)

            keep_warm(7, moving=patches[:, 0])
            ln_tensor(0, 6, 7)
            pe.wait_ge(s_w0, 48)
            pe.wait_ge(s_xta, 1)
            pe.wait_ge(s_xtb, 4)
            pe.wait_ge(s_h, 4)
            for r in range(2):
                for half in range(2):
                    ncol = slice(half * 384, half * 384 + 384)
                    banks = [PS[:, 4 * r + half, 0:384], PS[:, 4 * r + 2 + half, 0:384]]
                    for i, t in enumerate((2 * r, 2 * r + 1)):
                        pe.matmul(banks[i], xta[:, t * 128:t * 128 + 128], wv[:, 0, ncol], start=True, stop=False)
                    for i, t in enumerate((2 * r, 2 * r + 1)):
                        rows = slice(64 * i, 64 * i + 64)
                        mm = pe.matmul(banks[i], xtb[rows, t * 128:t * 128 + 128], wv[rows, 1, ncol],
                                       start=False, stop=True)
                mm.then_inc(a_v, 1)

            def project(j):
                if j >= 1:
                    pe.wait_ge(a_q, j)
                    pe.wait_ge(a_k, j)
                else:
                    pe.wait_ge(a_va, 1)
                    pe.wait_ge(a_vd, 1)
                for i in range(2):
                    pe.matmul(PS[:, i, :], wqk[:, j, i, :], xta[:], start=True, stop=False)
                for i in range(2):
                    rows = slice(64 * i, 64 * i + 64)
                    mm = pe.matmul(PS[:, i, :], wqk[rows, j, 2, :], xtb[rows, :], start=False, stop=True)
                mm.then_inc(a_proj, 1)

            def scores(j):
                b = j % 2
                pe.wait_ge(a_q, j + 1)
                pe.wait_ge(a_k, j + 1)
                if j >= 1:
                    pe.wait_ge(a_sub, 4 * (j - 1) + 2)
                for swap in range(2):
                    for t in range(TILES):
                        for i in ((0, 1), (1, 0))[swap]:
                            a = (i + swap) % 2
                            rows = slice(64 * i, 64 * i + 64)
                            img = 2 * t + a
                            cols = slice(img * 64, img * 64 + 64)
                            mm = pe.matmul(PS[rows, 2 + a, t * 64:t * 64 + 64], qT[rows, b, cols],
                                           kT[rows, b, cols], start=True, stop=True)
                mm.then_inc(a_s, 1)

            def transpose_probs(j):
                pe.wait_ge(a_p, 3 * j + 3)
                if j >= 1:
                    pe.wait_ge(a_ptc, j)
                for t in range(TILES):
                    mm = pe.transpose(PS[:, 4, t * 128:t * 128 + 128], prob[:, j % 2, t].rearrange("p a k -> p (a k)"), ident[:])
                mm.then_inc(a_pt, 1)

            def weigh(j):
                pe.wait_ge(a_ptc, j + 1)
                if j >= 1:
                    pe.wait_ge(a_oe, j)
                    pe.wait_ge(a_oo, j)
                for i in range(2):
                    for t in range(TILES):
                        for a in range(2):
                            rows = slice(64 * a, 64 * a + 64)
                            outp = slice(64 * i, 64 * i + 64)
                            mm = pe.matmul(PS[outp, 5 + a, t * 64:t * 64 + 64],
                                           vtok[rows, t, (2 * j + i) * 64:(2 * j + i) * 64 + 64],
                                           probT[rows, t, i * 64:i * 64 + 64], start=True, stop=True)
                mm.then_inc(a_pv, 1)

            project(0)
            pe.wait_ge(a_va, 2)
            pe.wait_ge(a_vd, 2)
            project(1)
            scores(0)
            for j in range(PAIRS):
                if j + 2 < PAIRS:
                    project(j + 2)
                transpose_probs(j)
                if j + 1 < PAIRS:
                    scores(j + 1)
                weigh(j)
            pe.wait_ge(a_oe, PAIRS)
            pe.wait_ge(a_oo, PAIRS)
            for t in range(TILES):
                for j in range(PAIRS):
                    mm = pe.matmul(PS[:, t, 0:DIM], attnT[:, j, t * 128:t * 128 + 128], wo[:, j, :],
                                   start=(j == 0), stop=(j == PAIRS - 1))
                mm.then_inc(a_o, 1)

            def split_product(to, pairs):
                for k, (stationary, moving) in enumerate(pairs):
                    mm = pe.matmul(to, stationary, moving, start=(k == 0),
                                   stop=(k == len(pairs) - 1))
                return mm

            keep_warm(7)
            ln_tensor(1, 6, 7)
            pe.wait_ge(s_xta, 2)
            pe.wait_ge(s_xtb, 8)

            def router_logits(wh, wl):
                for t in range(TILES):
                    cols = slice(t * 128, t * 128 + 128)
                    mm = split_product(PS[:, 6, t * EXPERTS:(t + 1) * EXPERTS], (
                        (xh[:, 0, cols], wh[:, 0]), (xl[:, 0, cols], wh[:, 0]), (xh[:, 0, cols], wl),
                        (xh[:, 1, cols], wh[:, 1]), (xl[:, 1, cols], wh[:, 1])))
                return mm

            def moe0_up(e, p):
                pe.wait_ge(f_l1, 2 * e + 2)
                pe.wait_ge(f_relu, e + 1)
                for i in range(2):
                    mm = split_product(PS[:, 2 * p + i, :], (
                        (fw1h[:, p, i, 0], xh[:, 0]), (fw1h[:, p, i, 0], xl[:, 0]), (fw1l[:, p, i], xh[:, 0]),
                        (fw1h[:, p, i, 1], xh[:, 1]), (fw1h[:, p, i, 1], xl[:, 1])))
                mm.then_inc(f_hid, 1)

            def moe0_down(e, p):
                pe.wait_ge(f_l2, 2 * e + 2)
                pe.wait_ge(f_hl, e + 3)
                pe.wait_ge(f_acc, TILES * e + 4)
                for t in range(TILES):
                    cols = slice(t * 128, t * 128 + 128)
                    mm = split_product(PS[:, 4 + 2 * p + t % 2, (t // 2) * DIM:(t // 2 + 1) * DIM], (
                        (fhh[:, p, 0, cols], fw2h[:, p, 0]), (fhh[:, p, 0, cols], fw2l[:, p]),
                        (fhl[:, p, 0, cols], fw2h[:, p, 0]),
                        (fhh[:, p, 1, cols], fw2h[:, p, 1]), (fhl[:, p, 1, cols], fw2h[:, p, 1])))
                mm.then_inc(f_y, 1)

            moe0_up(0, 0)
            pe.wait_ge(f_rs, 3)
            router_logits(frwh, frwl).then_inc(f_lg, 1)
            pe.wait_ge(f_sig, 1)
            with pe.Fori(0, EXPERTS // 2) as i:
                for p in range(2):
                    moe0_up(2 * i + p + 1, 1 - p)
                    moe0_down(2 * i + p, p)
            moe0_down(EXPERTS, 0)

            keep_warm(7, bank=0)
            ln_tensor(2, 6, 7)
            pe.wait_ge(m_w, 160)
            pe.wait_ge(s_xta, 3)
            pe.wait_ge(s_xtb, 12)
            for c in range(CTILES):
                k = 2 * (c % 2)
                if c >= 2:
                    pe.wait_ge(m_x, c - 1)
                    pe.wait_ge(m_z, c - 1)
                for i in range(2):
                    pe.matmul(PS[:, k + i, :], m_in[:, c, i, :], xta[:], start=True, stop=False)
                for i in range(2):
                    rows = slice(64 * i, 64 * i + 64)
                    mm = pe.matmul(PS[:, k + i, :], m_in[rows, c, 2, :], xtb[rows, :], start=False, stop=True)
                mm.then_inc(m_xz, 1)

            def x_dbl(d):
                for c in range(CTILES):
                    pe.wait_ge(m_silu, 3 * d + c + 1)
                    mm = pe.matmul(PS[0:44, 4 + d, :], m_xp[:, d, c, :], xc[:, d, c], start=(c == 0),
                                   stop=(c == CTILES - 1))
                mm.then_inc(m_xd, 1)
                pe.wait_ge(m_xdc, d + 1)
                for t in range(TILES):
                    mm = pe.transpose(PS[:, 4 + d, t * 44:t * 44 + 44], xdbl[0:44, d, t * 128:t * 128 + 128],
                                      ident[0:44, 0:44])
                mm.then_inc(m_bt, 1)

            def raw_dt(d):
                if d == 1:
                    pe.wait_ge(m_se, 3)
                for c in range(CTILES):
                    pe.matmul(PS[:, (6, 7, 0)[c], :], m_dtw[0:RANK, d, c * 128:c * 128 + 128], xdbl[0:RANK, d, :],
                              start=True, stop=True).then_inc(m_dt, 1)

            def select_b(d):
                pe.wait_ge(m_bs, 5 * d + 5)
                pe.wait_ge(m_sell, 16)
                for g in range(8):
                    for j in range(3):
                        mm = pe.matmul(PS[:, 4 + d, g * 64:g * 64 + 64], m_sel[:, g, j, :],
                                       bparts[:, d, j].rearrange("p t n -> p (t n)"), start=(j == 0), stop=(j == 2))
                mm.then_inc(m_bsl, 1)

            def transpose_dtu(u):
                pe.wait_ge(m_du, u // 3 + 1)
                if u >= 2:
                    pe.wait_ge(m_r1, u - 1)
                for t in range(TILES):
                    mm = pe.transpose(PS[:, 2 + u % 2, t * 128:t * 128 + 128], du[:, u // 3, u % 3, t * 128:t * 128 + 128],
                                      ident[:])
                mm.then_inc(m_dut, 1)

            x_dbl(0)
            raw_dt(0)
            select_b(0)
            x_dbl(1)
            raw_dt(1)
            select_b(1)
            pe.wait_ge(m_z, CTILES)
            for u in range(UNITS):
                transpose_dtu(u)

            def form_inputs(B):
                u, b = B // 8, B % 8
                if b == 0:
                    pe.wait_ge(m_lw, 16 * COMBOS * (u + 1))
                    pe.wait_ge(m_bd, STEP * (u // 3 + 1))
                if B >= 2:
                    pe.wait_ge(m_scan, B - 1)
                for s in range(4):
                    for nh in range(2):
                        to = PS[:, 2 * (b % 2) + nh, :].rearrange("p (n t) -> p t n", t=64)
                        mm = pe.matmul(to[:, s * STEP:(s + 1) * STEP, :],
                                       lw[:, u % 2, (b % 2) * 4 + s, b // 2, :],
                                       bd[:, u // 3, b * 4 + s, :, nh * 8:nh * 8 + 8], start=True, stop=True)
                mm.then_inc(m_b, 1)

            def sum_states(v):
                u, q = v // 4, v % 4
                pe.wait_ge(m_mul, by_pool(v))
                if q == 3:
                    pe.wait_ge(m_fold, 3 * u + 3)
                if q % 2 == 0 and u >= 1:
                    pe.wait_ge(m_post, 2 * (u - 1) + q // 2 + 1)
                to = PS[:, 4 + q // 2, (q % 2) * 128:(q % 2) * 128 + 128]
                states = STATE // 2 if q == 3 else STATE
                for n in range(states):
                    mm = pe.matmul(to, ident[:], hbuf[v % 3][:, :, n, :], start=(n == 0), stop=(n == states - 1))
                mm.then_inc(m_y, 1)

            pe.wait_ge(m_r1, UNITS)
            pe.wait_ge(m_bsc, 2)
            pe.wait_ge(m_se, 8)
            for B in range(4):
                form_inputs(B)
            for v in range(4 * UNITS):
                if v + 2 < 4 * UNITS:
                    form_inputs(2 * v + 4)
                    form_inputs(2 * v + 5)
                sum_states(v)
            pe.wait_ge(m_scan, 8 * UNITS)
            pe.wait_ge(m_g, 2 * CTILES)
            for t in range(TILES):
                for c in range(CTILES):
                    mm = pe.matmul(PS[:, t, 0:DIM], zgate[:, c, t * 128:t * 128 + 128], m_out[:, c, :],
                                   start=(c == 0), stop=(c == CTILES - 1))
                mm.then_inc(m_o, 1)

            keep_warm(7)
            ln_tensor(4, 6, 7)
            pe.wait_ge(q_w, 48)
            pe.wait_ge(s_xta, 4)
            pe.wait_ge(s_xtb, 16)
            for r in range(2):
                banks = [PS[:, 2 + 2 * r + i, 0:384] for i in range(2)]
                for i in range(2):
                    t = 2 * r + i
                    pe.matmul(banks[i], xta[:, t * 128:t * 128 + 128], q_wv[:, 0, :], start=True, stop=False)
                for i in range(2):
                    t = 2 * r + i
                    rows = slice(64 * i, 64 * i + 64)
                    mm = pe.matmul(banks[i], xtb[rows, t * 128:t * 128 + 128], q_wv[rows, 1, :],
                                   start=False, stop=True)
                mm.then_inc(q_vd, 1)

            def quad_project(j):
                if j >= 1:
                    pe.wait_ge(q_q, j)
                    pe.wait_ge(q_k, j)
                if j >= 2:
                    pe.wait_ge(q_oe, j - 1)
                    pe.wait_ge(q_oo, j - 1)
                for i in range(2):
                    pe.matmul(PS[:, i, :], q_wqk[:, j, i, :], xta[:], start=True, stop=False)
                for i in range(2):
                    rows = slice(64 * i, 64 * i + 64)
                    mm = pe.matmul(PS[:, i, :], q_wqk[rows, j, 2, :], xtb[rows, :], start=False, stop=True)
                mm.then_inc(q_proj, 1)

            def quad_scores(j):
                b = j % 2
                pe.wait_ge(q_q, j + 1)
                pe.wait_ge(q_k, j + 1)
                if j >= 1:
                    pe.wait_ge(q_sub, 2 * j)
                for swap in range(2):
                    for t2 in range(2):
                        for a in range(2):
                            for hd in ((0, 1, 2, 3), (1, 0, 3, 2))[swap]:
                                side, hp = hd % 2, hd // 2
                                par = (side + swap) % 2
                                img = 2 * (2 * t2 + par) + a
                                rows = slice(32 * hd, 32 * hd + 32)
                                cols = slice(img * 64, img * 64 + 64)
                                x = (t2 * 2 + a) * 64
                                mm = pe.matmul(PS[64 * side:64 * side + 64, 2 + 2 * hp + par, x:x + 64],
                                               q_qT[rows, b, cols], q_kT[rows, b, cols], start=True, stop=True,
                                               tile_position=(32 * hd, 64 * side))
                mm.then_inc(q_s, 1)

            def quad_transpose_probs(j):
                pe.wait_ge(q_p, 3 * j + 3)
                if j >= 1:
                    pe.wait_ge(q_ptc[0], j)
                    pe.wait_ge(q_ptc[1], j)
                for m in range(4):
                    for t2 in range(2):
                        x = ((m % 2) * 2 + t2) * 128
                        mm = pe.transpose(PS[:, 6 + m // 2, x:x + 128],
                                          q_prob[:, j % 2, m, t2].rearrange("p a k -> p (a k)"), ident[:])
                    if m % 2:
                        mm.then_inc(q_pt, 1)

            def quad_weigh(j):
                pe.wait_ge(q_ptc[0], j + 1)
                pe.wait_ge(q_ptc[1], j + 1)
                pe.wait_ge(q_q, min(j + 2, QUADS))
                pe.wait_ge(q_k, min(j + 2, QUADS))
                if j >= 1:
                    pe.wait_ge(q_oe, j)
                    pe.wait_ge(q_oo, j)
                for hd in range(4):
                    side, hp = hd % 2, hd // 2
                    for t in range(TILES):
                        for a in range(2):
                            rows = slice(64 * a, 64 * a + 64)
                            hcol = (4 * j + hd) * 32
                            mm = pe.matmul(PS[32 * hd:32 * hd + 32, a, t * 64:t * 64 + 64],
                                           q_v[rows, t, hcol:hcol + 32],
                                           q_probT[rows, 2 * hp + t % 2, t // 2, side * 64:side * 64 + 64],
                                           start=True, stop=True, tile_position=(64 * a, 32 * hd))
                mm.then_inc(q_pv, 1)

            quad_project(0)
            pe.wait_ge(q_va, 1)
            pe.wait_ge(q_vv, 1)
            quad_project(1)
            quad_scores(0)
            for j in range(QUADS):
                quad_transpose_probs(j)
                if j + 1 < QUADS:
                    quad_scores(j + 1)
                quad_weigh(j)
                if j + 2 < QUADS:
                    quad_project(j + 2)
            pe.wait_ge(q_oe, QUADS)
            pe.wait_ge(q_oo, QUADS)
            for t in range(TILES):
                for j in range(QUADS):
                    mm = pe.matmul(PS[:, t, 0:DIM], q_attnT[:, j, t * 128:t * 128 + 128], q_wo[:, j, :],
                                   start=(j == 0), stop=(j == QUADS - 1))
                mm.then_inc(q_o, 1)

            keep_warm(7)
            ln_tensor(5, 6, 7)
            pe.wait_ge(g_gb, 80)
            pe.wait_ge(s_xta, 5)
            pe.wait_ge(s_xtb, 20)

            def moe1_up(e, p, first=False):
                pe.wait_ge(g_l1, 2 * e + 2)
                for m in range(3):
                    k = 2 * ((3 * p + m) % 2)
                    if not first or m == 2:
                        pe.wait_ge(g_act, 3 * e + m - 1)
                    for i in range(2):
                        c = 2 * m + i
                        mm = split_product(PS[:, k + i, :], (
                            (gw1h[p][:, c, 0], xh[:, 0]), (gw1h[p][:, c, 0], xl[:, 0]), (gw1l[p][:, c], xh[:, 0]),
                            (gw1h[p][:, c, 1], xh[:, 1]), (gw1h[p][:, c, 1], xl[:, 1])))
                    mm.then_inc(g_hid, 1)

            def moe1_down(e, p):
                pe.wait_ge(g_l2, e + 1)
                pe.wait_ge(g_hl, 3 * e + 3)
                pe.wait_ge(g_acc, TILES * e + 4)
                for t in range(TILES):
                    cols = slice(t * 128, t * 128 + 128)
                    mm = split_product(PS[:, 4 + 2 * p + t % 2, (t // 2) * DIM:(t // 2 + 1) * DIM],
                                       [q for k in range(HCHUNKS) for q in (
                                           (ghh[p][:, k, cols], gw2h[p][:, k]), (ghh[p][:, k, cols], gw2l[p][:, k]),
                                           (ghl[p][:, k, cols], gw2h[p][:, k]))])
                mm.then_inc(g_y, 1)

            moe1_up(0, 0, first=True)
            pe.wait_ge(g_rs, 3)
            router_logits(grwh, grwl).then_inc(g_lg, 1)
            pe.wait_ge(g_e, 1)
            with pe.Fori(0, EXPERTS // 2 - 1) as i:
                for p in range(2):
                    moe1_up(2 * i + p + 1, 1 - p)
                    moe1_down(2 * i + p, p)
            moe1_up(EXPERTS - 1, 1)
            moe1_down(EXPERTS - 2, 0)
            moe1_down(EXPERTS - 1, 1)


def lay_out(i):
    import numpy as np
    f = lambda a: np.ascontiguousarray(a)
    chunked = lambda a: f(a.reshape(-1, 128, a.shape[-1]).transpose(1, 0, 2))
    twice = lambda a: np.concatenate([a, a], 0)

    x = i["x"].reshape(8, 3, 8, 16, 8, 16)
    a = {"ident": np.eye(128, dtype=np.float32)}
    a["patches"] = chunked(x.transpose(1, 3, 5, 0, 2, 4).reshape(768, 512))
    a["tok_w"] = chunked(i["L0_tok_W"].reshape(192, 16, 16, 3).transpose(3, 1, 2, 0).reshape(768, 192))
    a["tok_b"] = f(i["L0_tok_b"])
    q = np.arange(128)[:, None] % 64
    a["causal"] = np.where(np.arange(64)[None, :] > q, np.float32(MASKED), np.float32(0)).astype(np.float32)

    pair = lambda w: w.reshape(6, 2, 192, 64).transpose(2, 0, 1, 3).reshape(192, 6, 128)
    wq, wk = pair(i["L0_attn_W_Q"]), pair(i["L0_attn_W_K"])
    a["a0_wqk"] = f(np.stack([wq[:128], wk[:128], np.concatenate([wq[128:], wk[128:]], 0)], 2))
    wv = i["L0_attn_W_V"].transpose(1, 0, 2).reshape(192, 768)
    a["a0_wv"] = f(np.stack([wv[:128], twice(wv[128:])], 1))
    a["a0_wo"] = chunked(i["L0_attn_W_O"])

    moe0_1 = lambda w: np.stack([np.stack([m[:128], twice(m[128:])], 1)
                                 for m in (w[:, :128], np.concatenate([w[:, 128:]] * 2, 1))], 1)
    moe0_2 = lambda w: np.stack([w[:128], twice(w[128:])], 1)
    a["m0_w1"] = f(np.stack([moe0_1(w) for w in [i["L0_ffn_w_fc_sh"], *i["L0_ffn_w1"]]], 0))
    a["m0_w2"] = f(np.stack([moe0_2(w) for w in [i["L0_ffn_w_proj_sh"], *i["L0_ffn_w2"]]], 0))
    a["m0_router"] = f(moe0_2(i["L0_ffn_router_w"].T))
    a["m0_bias"] = f(i["L0_ffn_balance_bias"])

    w = i["L1_attn_in_proj_w"].T
    wx, wz = w[:, :384].reshape(192, 3, 128), w[:, 384:].reshape(192, 3, 128)
    a["m_in"] = f(np.stack([wx[:128], wz[:128], np.concatenate([wx[128:], wz[128:]], 0)], 2))
    both = lambda name: np.stack([i["L1_attn_" + name], i["L1_attn_" + name + "_b"]], 0)
    per_channel = lambda v: f(v.reshape(2, 3, 128, -1).transpose(2, 0, 1, 3))
    a["m_xp"] = per_channel(both("x_proj_w").transpose(0, 2, 1))
    a["m_dtw"] = f(np.stack([i["L1_attn_dt_proj_w"], i["L1_attn_dt_proj_w_b"]], 0).transpose(2, 0, 1))
    a["m_out"] = chunked(i["L1_attn_out_proj_w"].T)
    a["m_conv"] = per_channel(both("conv1d_w"))
    a["m_convb"] = per_channel(both("conv1d_bias"))[..., 0]
    a["m_dtb"] = per_channel(both("dt_proj_bias"))[..., 0]
    a["m_a"] = per_channel(both("A_log"))
    a["m_d"] = per_channel(both("D"))[..., 0]
    row = np.arange(128)
    a["m_mask"] = (row[:, None] % STEP == np.arange(STEP)[None, :]).astype(np.float32)
    sel = np.zeros((128, 8, 3, 128), np.uint16)
    for c in range(COMBOS):
        for g in range(8):
            for t in range(STEP):
                sel[g * STEP + t, g, PART_B[c], c * STEP + t] = 1
    a["m_sel"] = sel * np.uint16(0x3F80)

    w = i["L1_ffn_Wqkv"].reshape(192, 3, 12, 16)
    w = np.concatenate([w, np.zeros_like(w)], 3).reshape(192, 3, 384)
    wq, wk, wv = w[:, 0].reshape(192, 3, 128), w[:, 1].reshape(192, 3, 128), w[:, 2]
    a["a1_wqk"] = f(np.stack([wq[:128], wk[:128], np.concatenate([wq[128:], wk[128:]], 0)], 2))
    a["a1_wv"] = f(np.stack([wv[:128], twice(wv[128:])], 1))
    w = i["L1_ffn_Wproj"].reshape(12, 16, 192)
    a["a1_wo"] = chunked(np.concatenate([w, np.zeros_like(w)], 1).reshape(384, 192))
    w = i["L1_ffn_W1"].reshape(8, 192, 6, 128)
    a["m1_w1"] = f(np.stack([w[:, :128], np.concatenate([w[:, 128:], w[:, 128:]], 1)], 3))
    a["m1_w2"] = f(i["L1_ffn_W2"].reshape(8, 6, 128, 192).transpose(0, 2, 1, 3))
    a["m1_router"] = f(moe0_2(i["L1_ffn_Wrouter"]))
    for n in ("ln1_g", "ln1_b", "ln2_g", "ln2_b"):
        a[n] = f(i["L1_ffn_" + n])
    return a


def kernel(**inputs):
    import numpy as np
    import concourse.bacc as bacc
    from concourse.bass_utils import run_bass_kernel_spmd

    arrays = lay_out({k: np.asarray(v) for k, v in inputs.items()})
    nc = bacc.Bacc("TRN2", target_bir_lowering=False, num_devices=1)
    io = {n: nc.dram_tensor(f"in_{n}", a.shape, mybir.dt.from_np(a.dtype), kind="ExternalInput").ap()
          for n, a in arrays.items()}
    out = nc.dram_tensor("out", (TOKENS, DIM), mybir.dt.float32, kind="ExternalOutput").ap()
    build_tower(nc, io, out)
    got = run_bass_kernel_spmd(nc, [{f"in_{n}": a for n, a in arrays.items()}], core_ids=[0])
    return got.results[0]["out"].reshape(BATCH, TOKENS_PER_IMAGE, DIM)
```

```python
import concourse.bass as bass
from concourse import mybir
from contextlib import ExitStack

BATCH, TOKENS_PER_IMAGE, DIM = 8, 64, 192
TOKENS = BATCH * TOKENS_PER_IMAGE
TILES = TOKENS // 128
PATCH_K = 768 // 128
HEADS = 12
PAIRS = HEADS // 2
LN_EPS = 1e-5
EXPERTS = 8
INNER, STATE, RANK, TAPS = 384, 16, 12, 4
CTILES = INNER // 128
UNITS = 2 * CTILES
STEP = 16
COMBOS = 8
PART_U = [c % 3 for c in range(COMBOS)]
PART_B = [c // 3 for c in range(COMBOS)]
MASKED = -1.0e30
FIRST_PAIRS, OTHER_PAIRS = slice(0, 2), slice(2, 6)


def build_tower(nc, io, out):
    F32 = mybir.dt.float32
    F32R = mybir.dt.float32r
    BF16 = mybir.dt.bfloat16
    ALU = mybir.AluOpType
    ACT = mybir.ActivationFunctionType
    AX = mybir.AxisListType

    c_dram = nc.dram_tensor("c_scratch", (2, BATCH, STATE, 64), F32, kind="Internal").ap()
    u_dram = nc.dram_tensor("u_scratch", (UNITS, 3, 128, 512), BF16, kind="Internal").ap()

    ctx = ExitStack()
    with ctx:
        def sb(name, shape, dt=F32):
            return ctx.enter_context(nc.sbuf_tensor(name, shape, dt))

        def sem(name):
            return ctx.enter_context(nc.semaphore(name))

        PS = ctx.enter_context(nc.psum_tensor("PS", [128, 8, 512], F32))

        ident = sb("ident", [128, 128])
        h = sb("h", [128, TILES, DIM])
        xn = sb("xn", [128, TILES, 256])
        stats = sb("stats", [128, TILES, 6])
        moments = sb("moments", [128, TILES, 2])
        rstd = sb("rstd", [128, TILES])
        neg_half = sb("neg_half", [128, 1])

        expert_ids = sb("expert_ids", [128, TILES, EXPERTS])

        ARENA = 49900
        arena_at = -(-nc.sbuf_base // 32) * 32
        arena = sb("arena", [128, ARENA])

        def carve(at, *shape, dt=F32):
            n = 1
            for s in shape:
                n *= s
            cols = n // 2 if dt == BF16 else n
            if dt == F32R:
                at[0] = -(-at[0] // 8) * 8
            assert at[0] + cols <= at[1], (at, shape)
            if dt == F32R:
                v = nc.alloc_sbuf_tensor_at(f"parts_at_{at[0]}", [128, cols], F32R, offset=arena_at + 4 * at[0])[:]
            else:
                v = arena[:, at[0]:at[0] + cols]
            at[0] += cols
            if dt == BF16:
                v = v.bitcast(dt)
            names = "abcde"[:len(shape)]
            if len(shape) > 1:
                v = v.rearrange(f"p ({' '.join(names)}) -> p {' '.join(names)}",
                                **{names[i]: shape[i] for i in range(1, len(shape))})
            return v

        SPLIT_X = 25128
        at = [SPLIT_X, SPLIT_X + 4 * TOKENS]
        xh = carve(at, 2, TOKENS, dt=F32R)
        xl = carve(at, 2, TOKENS, dt=F32R)

        at = [0, ARENA]
        patches = carve(at, PATCH_K, TOKENS)
        tok_w = carve(at, PATCH_K, DIM)
        tok_b = carve(at, DIM)
        wqk = carve(at, PAIRS, 2, 2, 128)
        wv = carve(at, 2, HEADS * 64)
        wqkl = carve(at, PAIRS, 2, 128, dt=F32R)
        wvh = carve(at, 2, HEADS * 64, dt=F32R)
        wvl = carve(at, HEADS * 64, dt=F32R)
        wo = carve(at, PAIRS, DIM)
        causal = carve(at, 64)
        vtok = carve(at, TILES, HEADS * 64)
        qT = carve(at, 2, TOKENS)
        kT = carve(at, 2, TOKENS)
        prob = carve(at, 2, TILES, 2, 64)
        rowmax = carve(at, 2, 8)
        rowsum = carve(at, 2, 8)
        probT = carve(at, TILES, 128)
        attnT = carve(at, PAIRS, TOKENS)

        frw = carve(at, 2, EXPERTS)
        fbias = carve(at, EXPERTS)
        fscore = carve(at, TILES, EXPERTS)
        fpick = carve(at, TILES, EXPERTS)
        ftop = carve(at, TILES, 8)
        fidx = carve(at, TILES, 8).bitcast(mybir.dt.uint32)
        fidxf = carve(at, TILES, 2)
        fhot = carve(at, 2, TILES, EXPERTS)
        fsum = carve(at, TILES)
        fwt = carve(at, TILES, 1 + EXPERTS)

        at = [SPLIT_X + 4 * TOKENS, 29896 + 8192]
        fw1 = carve(at, 2, 2, 2, 128)
        fw1h = carve(at, 2, 2, 2, 128, dt=F32R)
        fw1l = carve(at, 2, 2, 128, dt=F32R)
        fw2 = carve(at, 2, 2, DIM)
        fw2h = carve(at, 2, 2, DIM, dt=F32R)
        fw2l = carve(at, 2, DIM, dt=F32R)
        frwh = carve(at, 2, EXPERTS, dt=F32R)
        frwl = carve(at, EXPERTS, dt=F32R)
        wqkh = carve([at[0], at[1]], PAIRS, 2, 2, 128, dt=F32R)
        frelu = carve(at, 2, 2, TOKENS)
        fhh = carve(at, 2, 2, TOKENS, dt=F32R)
        fhl = carve(at, 2, 2, TOKENS, dt=F32R)

        at = [29896, ARENA]
        fresh = at[0]
        decay = carve(at, 2, 4, STATE, 64)
        mark = at[0]
        at = [fresh, mark]
        xpad = carve(at, CTILES, BATCH, 70)
        softx = carve(at, 2, CTILES, TOKENS)
        softe = carve(at, 2, CTILES, TOKENS)
        at = [mark, ARENA]
        m_in = carve(at, CTILES, 2, 2, 128)
        m_xp = carve(at, 2, CTILES, 44)
        m_dtw = carve(at, 2, INNER)
        m_out = carve(at, CTILES, DIM)
        m_conv = carve(at, 2, CTILES, TAPS)
        m_convb = carve(at, 2, CTILES)
        m_dtb = carve(at, 2, CTILES)
        m_a = carve(at, 2, CTILES, STATE)
        m_d = carve(at, 2, CTILES)
        m_mask = carve(at, STEP)
        zgate = carve(at, CTILES, TOKENS)
        xc = carve(at, 2, CTILES, TOKENS)
        dts = carve(at, 2, CTILES, TOKENS)
        bts = carve(at, 2, TILES, STATE)
        at = [0, fresh]
        hbuf = [carve(at, 2, STATE, 64) for _ in range(2)]
        mark = at[0]
        at = [0, mark]
        m_inh = carve([0, mark], CTILES, 2, 2, 128, dt=F32R)
        m_inl = carve([CTILES * 512, mark], CTILES, 2, 128, dt=F32R)
        du = carve(at, 2, CTILES, TOKENS)
        dr = carve(at, 2, TOKENS)
        at = [mark, fresh]
        bd = carve(at, 2, 32, STEP, STATE, dt=BF16)
        lw = carve(at, 2, 8, TILES, 128, dt=BF16)
        cb = carve(at, BATCH, STATE, 64)
        softw = [cb[:, 4 + 2 * d:6 + 2 * d].rearrange("p b n t -> p (b n t)")[:, 0:CTILES * TOKENS]
                 .rearrange("p (c t) -> p c t", c=CTILES) for d in range(2)]
        m_sel = carve([at[0], at[1]], 8, 3, 128, dt=BF16)
        yf = carve(at, CTILES, TOKENS)
        third = at[0]
        xdbl = carve(at, 2, TOKENS)
        uparts = [carve(at, 3, TILES, 128, dt=BF16) for _ in range(2)]
        hbuf.append(carve([third, at[0]], 2, STATE, 64))
        for lent in (lw[:, 1].rearrange("p g t d -> p (g t d)"),
                     cb[:, 2:4].rearrange("p b n t -> p (b n t)").bitcast(BF16)):
            for k in range(2):
                uparts.append(lent[:, k * 1536:(k + 1) * 1536].rearrange("p (i t d) -> p i t d", i=3, t=TILES))
        bparts = carve(at, 2, 3, TILES, STATE, dt=BF16)
        bsel = carve(at, 2, TILES, 8, STATE, dt=BF16)
        yr = carve(at, 2, 256)

        QUADS = HEADS // 4
        HCHUNKS = 6
        at = [4096, 8192]
        q_wqk = carve(at, QUADS, 2, 2, 128)
        q_wv = carve(at, 2, HEADS * 32)
        gw1_0 = carve(at, HCHUNKS, 2, 128)
        at = [8192, 16384]
        gw1 = [gw1_0, carve(at, HCHUNKS, 2, 128)]
        gw2 = [carve(at, HCHUNKS, DIM) for _ in range(2)]
        gw1h = [carve(at, HCHUNKS, 2, 128, dt=F32R) for _ in range(2)]
        ln_gb = [carve(at, DIM) for _ in range(4)]
        grw = carve(at, 2, EXPERTS)
        grwh = carve(at, 2, EXPERTS, dt=F32R)
        grwl = carve(at, EXPERTS, dt=F32R)
        at = [0, 4096]
        q_wqkh = carve(at, QUADS, 2, 2, 128, dt=F32R)
        q_wqkl = carve(at, QUADS, 2, 128, dt=F32R)
        q_wvh = carve(at, 2, HEADS * 32, dt=F32R)
        q_wvl = carve(at, HEADS * 32, dt=F32R)
        q_wo = carve(at, QUADS, DIM)
        at = [16384, SPLIT_X]
        q_v = carve(at, TILES, HEADS * 32)
        q_qT = carve(at, 2, TOKENS)
        q_kT = carve(at, 2, TOKENS)
        q_prob = carve(at, 2, 4, 2, 2, 64)
        q_probT = carve(at, 4, 2, 128)
        q_attnT = carve(at, QUADS, TOKENS)
        q_max = carve(at, 2, 16)
        q_sum = carve(at, 2, 16)
        gtop = carve(at, TILES, 8)
        gidx = carve(at, TILES, 8).bitcast(mybir.dt.uint32)
        gidxf = carve(at, TILES, 2)
        glog = carve(at, TILES, EXPERTS)
        ghot = carve(at, 2, TILES, EXPERTS)
        gpair = carve(at, 2, TILES)
        gwt = carve(at, TILES, EXPERTS)
        at = [fresh, fresh + 8192]
        x4 = carve(at, TILES, DIM)
        x5 = carve(at, TILES, DIM)
        scaled = carve(at, TILES, DIM)
        gw2p = [carve(at, HCHUNKS, 2, DIM, dt=F32R)]
        gw1l = [carve(at, HCHUNKS, 128, dt=F32R) for _ in range(2)]
        at = [fresh + 8192, ARENA]
        gw2p.append(carve(at, HCHUNKS, 2, DIM, dt=F32R))
        ghh = [carve(at, HCHUNKS, TOKENS, dt=F32R) for _ in range(2)]
        at = [16384, SPLIT_X]
        ghl = [carve(at, HCHUNKS, TOKENS, dt=F32R)]
        ghl.append(carve(at, HCHUNKS, TOKENS, dt=F32R))
        at = [SPLIT_X + 4 * TOKENS, 29896]
        gact_a = carve(at, 4, TOKENS)
        at = [29896 + 8192 + 2 * HCHUNKS * DIM + 2 * HCHUNKS * TOKENS, ARENA]
        gact_b = carve(at, 2, TOKENS)
        gact = [gact_a[:, 0:2], gact_a[:, 2:4], gact_b]

        s_const = sem("const_loaded")
        s_tokw = sem("tok_weights_loaded")
        s_patch = [sem(f"patches_loaded{k}") for k in range(PATCH_K)]
        s_tok = sem("tok_done")
        s_h = sem("h_written")
        s_zero = sem("warm_up_zeros_set")
        s_nh = sem("neg_half_set")
        s_wv = sem("attn0_wv_loaded")
        s_wqk = sem("attn0_wqk_loaded")
        s_wo = sem("attn0_wo_loaded")
        p_up = sem("projection_upper_done")
        p_lo = sem("projection_lower_done")
        s_out = sem("out_stored")
        s_mo = sem("ln_stats_moments")
        s_rs = sem("ln_rstd")
        s_xn = sem("ln_normed")
        s_xt = sem("ln_transposed")
        s_xta = sem("ln_xta")
        s_xtb = sem("ln_xtb")
        TURN = [0, 1, 2, None, 3, 4]

        a_v = sem("attn0_v_done")
        a_va = sem("attn0_v_copied_by_scalar")
        a_vd = sem("attn0_v_copied_by_vector")
        a_proj = sem("attn0_qk_done")
        a_q = sem("attn0_q_copied")
        a_k = sem("attn0_k_copied")
        a_s = sem("attn0_scores_done")
        a_sub = sem("attn0_masked_max_shifted")
        a_exp = sem("attn0_exp_done")
        a_p = sem("attn0_sum_recip_probs")
        a_pt = sem("attn0_probs_transposed")
        a_ptc = sem("attn0_probsT_copied")
        a_pv = sem("attn0_pv_done")
        a_oe = sem("attn0_even_copied")
        a_oo = sem("attn0_odd_copied")
        a_o = sem("attn0_out_done")

        f_w1 = [sem(f"moe0_w1_loaded{n}") for n in range(2)]
        f_w2 = [sem(f"moe0_w2_loaded{n}") for n in range(2)]
        f_rw = sem("moe0_router_loaded")
        f_rs = sem("moe0_router_split_steps")
        f_lg = sem("moe0_logits_done")
        f_sig = sem("moe0_sigmoid_done")
        f_rt = sem("moe0_routing_steps")
        f_hid = sem("moe0_hidden_done")
        f_relu = sem("moe0_relu_done")
        f_sq = sem("moe0_hidden_squared")
        f_h1 = sem("moe0_w1_upper_done")
        f_l1 = sem("moe0_w1_lower_done")
        f_h2 = sem("moe0_w2_upper_done")
        f_l2 = sem("moe0_w2_lower_done")
        f_hl = sem("moe0_hidden_lower_done")
        f_y = sem("moe0_y_done")
        f_acc = sem("moe0_y_added")
        s_ids = sem("expert_ids_made")

        q_w = sem("attn1_weights_loaded")
        q_wol = sem("attn1_wo_loaded")
        q_vd = sem("attn1_v_done")
        q_va = sem("attn1_v_copied_by_scalar")
        q_vv = sem("attn1_v_copied_by_vector")
        q_proj = sem("attn1_qk_done")
        q_q = sem("attn1_q_copied")
        q_k = sem("attn1_k_copied")
        q_s = sem("attn1_scores_done")
        q_sub = sem("attn1_max_shifted")
        q_exp = sem("attn1_exp_done")
        q_p = sem("attn1_sum_recip_probs")
        q_pt = sem("attn1_probs_transposed")
        q_ptc = [sem(f"attn1_probsT_copied{n}") for n in range(2)]
        q_pv = sem("attn1_pv_done")
        q_oe = sem("attn1_even_copied")
        q_oo = sem("attn1_odd_copied")
        q_o = sem("attn1_out_done")
        s_x5 = sem("x5_written")
        s_hx = sem("x5_added_to_h")
        s_aff = [sem(f"ln{n}_affine_steps") for n in range(4, 6)]
        g_w1 = [sem(f"moe1_w1_loaded{n}") for n in range(2)]
        g_w2 = [sem(f"moe1_w2_loaded{n}") for n in range(2)]
        g_gb = sem("norm_gains_loaded")
        g_rs = sem("moe1_router_split_steps")
        g_lg = sem("moe1_logits_done")
        g_rt = sem("moe1_routing_steps")
        g_d = sem("moe1_top_difference")
        g_e = sem("moe1_logits_copied_top_exp")
        g_hid = sem("moe1_hidden_done")
        g_act = sem("moe1_gelu_done")
        g_h1 = sem("moe1_w1_upper_done")
        g_l1 = sem("moe1_w1_lower_done")
        g_h2 = sem("moe1_w2_upper_done")
        g_l2 = sem("moe1_w2_lower_done")
        s_hh = sem("hidden_upper_done")
        g_hl = sem("moe1_hidden_lower_done")
        g_y = sem("moe1_y_done")
        g_acc = sem("moe1_y_added")

        m_w = sem("ssm_weights_loaded")
        m_sell = sem("ssm_selector_loaded")
        m_pad = sem("ssm_pads_zeroed")
        m_xz = sem("ssm_xz_done")
        m_x = sem("ssm_x_copied")
        m_z = sem("ssm_z_gated")
        m_cv = sem("ssm_conv_taps_by_vector")
        m_cp = sem("ssm_conv_taps_by_pool")
        m_silu = sem("ssm_conv_silu")
        m_xd = sem("ssm_xdbl_done")
        m_xdc = sem("ssm_xdbl_copied")
        m_cst = sem("ssm_c_stored")
        m_cld = [sem(f"ssm_c_loaded{q}") for q in range(4)]
        m_bt = sem("ssm_b_transposed")
        m_bs = sem("ssm_b_split_steps")
        m_bsl = sem("ssm_b_selected")
        m_bsc = sem("ssm_b_selected_copied")
        m_bd = sem("ssm_b_blocks")
        m_dt = sem("ssm_dt_raw_done")
        m_se = sem("ssm_softplus_x_abs_exp")
        m_sw = sem("ssm_softplus_w_rest_less")
        m_sl = sem("ssm_softplus_ln")
        m_dts = sem("ssm_dt_ready")
        m_du = sem("ssm_dtu_ready")
        m_dut = sem("ssm_dtu_transposed")
        m_p1 = sem("ssm_dtu_part1")
        m_r1 = sem("ssm_dtu_rest")
        m_p2 = sem("ssm_dtu_part2")
        m_p3 = sem("ssm_dtu_part3")
        m_ust = [sem(f"ssm_dtu_stored{u}") for u in range(UNITS)]
        m_lw = sem("ssm_dtu_loaded")
        m_ea = sem("ssm_a_exp")
        m_na = sem("ssm_a_negated")
        m_zero = sem("ssm_decay_starts_zeroed")
        m_dec = sem("ssm_decay_ready")
        m_b = sem("ssm_inputs_formed")
        m_scan = sem("ssm_scanned")
        m_mul = sem("ssm_times_c_by_pool")
        m_fold = sem("ssm_times_c_and_folded")

        def by_pool(chunk):
            return 2 * (chunk + 1 - (chunk + 1) // 4)
        m_y = sem("ssm_y_summed")
        m_post = sem("ssm_y_taken")
        m_yr = sem("ssm_yr_made")
        m_sum = sem("ssm_directions_added")
        m_g = sem("ssm_gated")
        m_o = sem("ssm_out_done")

        def conv_taps(d, c, k):
            return xpad[:, c, :, k:k + 64] if d == 0 else xpad[:, c, :, 69 - k:5 - k:-1]

        def moe0_upper_w1(eng, upper, e, p, loads):
            eng.wait_ge(f_w1[p], 16 * loads)
            upper(fw1h[:, p], fw1[:, p]).then_inc(f_h1, 1)

        def moe0_upper_w2(eng, upper, e, p, loads, first=False):
            eng.wait_ge(f_w2[p], 16 * loads)
            if not first:
                eng.wait_ge(f_y, e - 1)
            upper(fw2h[:, p], fw2[:, p]).then_inc(f_h2, 1)

        ADD_ORDER = [(t0 + t, piece) for t0 in range(0, TILES, 2) for piece in range(2) for t in range(2)]

        block = ctx.enter_context(nc.Block())

        @block.sync
        def _(sp):
            sp.dma_start(tok_w, io["tok_w"]).then_inc(s_tokw, 16)
            for k in range(PATCH_K):
                sp.dma_start(patches[:, k, :], io["patches"][:, k, :]).then_inc(s_patch[k], 16)
            sp.dma_start(wv, io["a0_wv"]).then_inc(s_wv, 16)
            sp.dma_start(wqk, io["a0_wqk"]).then_inc(s_wqk, 16)
            sp.dma_start(wo, io["a0_wo"]).then_inc(s_wo, 16)
            sp.dma_start(frw, io["m0_router"]).then_inc(f_rw, 16)
            sp.dma_start(fbias, io["m0_bias"].partition_broadcast(128)).then_inc(f_rw, 16)
            for e in range(1 + EXPERTS):
                if e >= 2:
                    sp.wait_ge(f_l1, 2 * (e - 1))
                sp.dma_start(fw1[:, e % 2], io["m0_w1"][e]).then_inc(f_w1[e % 2], 16)
                if e >= 2:
                    sp.wait_ge(f_l2, 2 * (e - 1))
                sp.dma_start(fw2[:, e % 2], io["m0_w2"][e]).then_inc(f_w2[e % 2], 16)
            for n, (to, name) in enumerate(((m_in, "m_in"), (m_xp, "m_xp"), (m_dtw[0:RANK], "m_dtw"), (m_out, "m_out"),
                                            (m_conv, "m_conv"), (m_convb, "m_convb"), (m_dtb, "m_dtb"),
                                            (m_a, "m_a"), (m_d, "m_d"), (m_mask, "m_mask"))):
                sp.dma_start(to, io[name]).then_inc(m_w, 16)
            sp.wait_ge(m_xz, CTILES)
            sp.dma_start(m_sel.bitcast(mybir.dt.uint16), io["m_sel"]).then_inc(m_sell, 16)
            for d in range(2):
                sp.wait_ge(m_xdc, d + 1)
                sp.dma_start(c_dram[d].rearrange("b n t -> n b t"),
                             xdbl[RANK + STATE:44, d, :].rearrange("n (b t) -> n b t", t=64)).then_inc(m_cst, 16)

            def load_c(d, q):
                if d == 1:
                    sp.wait_ge(m_mul, by_pool(4 * (CTILES - 1) + q))
                    sp.wait_ge(m_fold, 3 * (CTILES - 1 + q // 3))
                sp.dma_start(cb[:, 2 * q:2 * q + 2].rearrange("p b n t -> p (b n t)"),
                             c_dram[d, 2 * q:2 * q + 2].rearrange("b n t -> (b n t)").partition_broadcast(128)
                             ).then_inc(m_cld[q], 16)

            def load_u(u):
                if u >= 2:
                    sp.wait_ge(m_b, 8 * (u - 1))
                if u >= 1:
                    sp.wait_ge(m_lw, 16 * COMBOS * u)
                sp.wait_ge(m_ust[u], 48)
                rows = u_dram[u].rearrange("i (g t) x -> i t g x", t=STEP)
                for c in range(COMBOS):
                    sp.dma_start(lw[c * STEP:(c + 1) * STEP, u % 2].rearrange("p g t d -> p g (t d)"),
                                 rows[PART_U[c]]).then_inc(m_lw, 16)

            def store_u(u):
                for i in range(3):
                    sp.wait_ge((m_p1, m_p2, m_p3)[i], u + 1)
                    sp.dma_start(u_dram[u, i], uparts[u][:, i].rearrange("p t d -> p (t d)")).then_inc(m_ust[u], 16)

            sp.wait_ge(m_cst, 32)
            load_c(0, 0)
            store_u(0)
            load_u(0)
            for u in range(1, UNITS):
                store_u(u)
            for u in range(2, UNITS):
                sp.wait_ge(m_ust[u], 48)
            for q in range(1, 4):
                load_c(0, q)
            load_u(1)
            for u in range(2, UNITS):
                load_u(u)
                if u == 3:
                    for q in range(4):
                        load_c(1, q)
            sp.dma_start(q_wqk, io["a1_wqk"]).then_inc(q_w, 16)
            sp.dma_start(q_wv, io["a1_wv"]).then_inc(q_w, 16)
            sp.dma_start(gw1[0], io["m1_w1"][0]).then_inc(g_w1[0], 16)
            sp.wait_ge(m_b, 8 * UNITS)
            for n, name in enumerate(("ln1_g", "ln1_b", "ln2_g", "ln2_b")):
                sp.dma_start(ln_gb[n], io[name].partition_broadcast(128)).then_inc(g_gb, 16)
            sp.dma_start(grw, io["m1_router"]).then_inc(g_gb, 16)
            sp.wait_ge(m_y, 4 * UNITS)
            sp.dma_start(q_wo, io["a1_wo"]).then_inc(q_wol, 16)
            for e in range(EXPERTS):
                if e >= 1:
                    if e >= 2:
                        sp.wait_ge(g_l1, 2 * (e - 1))
                    sp.dma_start(gw1[e % 2], io["m1_w1"][e]).then_inc(g_w1[e % 2], 16)
                if e >= 2:
                    sp.wait_ge(g_l2, e - 1)
                sp.dma_start(gw2[e % 2], io["m1_w2"][e]).then_inc(g_w2[e % 2], 16)
            out_tiles = out.rearrange("(t p) d -> p t d", p=128)
            sp.wait_ge(g_acc, 2 * TILES * EXPERTS + 4)
            sp.dma_start(out_tiles[:, 0:2], h[:, 0:2]).then_inc(s_out, 16)
            sp.wait_ge(g_acc, 2 * TILES * EXPERTS + 8)
            sp.dma_start(out_tiles[:, 2:4], h[:, 2:4]).then_inc(s_out, 16)
            sp.wait_ge(s_out, 32)

        @block.gpsimd
        def _(pool):
            pool.memset(xn[:, 0, 0:128], 0.0).then_inc(s_zero, 1)
            pool.memset(neg_half[:], -0.5).then_inc(s_nh, 1)
            pool.wait_ge(s_nh, 1)

            def ln_pool(n):
                for t in range(TILES):
                    step = 2 * (TILES * n + t)
                    pool.wait_ge(s_mo, step + 2)
                    pool.tensor_scalar(rstd[:, t:t + 1], moments[:, t, 1:2], LN_EPS, None, ALU.add).then_inc(s_rs, 1)
                    pool.wait_ge(s_rs, step + 1)
                    pool.tensor_tensor(rstd[:, t:t + 1], rstd[:, t:t + 1], neg_half[:, 0:1], ALU.pow).then_inc(s_rs, 1)

            pool.iota(expert_ids[:], [[0, TILES], [1, EXPERTS]], channel_multiplier=0,
                      allow_small_or_imprecise_dtypes=True).then_inc(s_ids, 1)
            pool.memset(fwt[:, :, 0:1], 1.0).then_inc(s_ids, 1)
            def lower_b(raw, hi, done, count):
                pool.wait_ge(done, count)
                pool.tensor_tensor(hi, raw, hi.bitcast(F32), ALU.subtract).then_inc(done, 1)
                pool.wait_ge(done, count + 1)

            def projection_lower(k, raw, hi, lo):
                pool.wait_ge(p_up, k + 1)
                pool.tensor_tensor(lo, raw[0], hi[0].bitcast(F32), ALU.subtract).then_inc(p_lo, 1)
                lower_b(raw[1][64:128], hi[1][64:128], p_lo, 2 * k + 1)

            ln_pool(0)
            for k, pairs in ((1, FIRST_PAIRS), (2, OTHER_PAIRS)):
                projection_lower(k, (wqk[:, pairs, :, 0], wqk[:, pairs, :, 1]),
                                 (wqkh[:, pairs, :, 0], wqkh[:, pairs, :, 1]), wqkl[:, pairs])

            def moe0_lower_w1(e, p):
                pool.wait_ge(f_h1, e + 1)
                pool.tensor_tensor(fw1l[:, p], fw1[:, p, :, 0], fw1h[:, p, :, 0].bitcast(F32), ALU.subtract).then_inc(f_l1, 1)
                lower_b(fw1[64:128, p, :, 1], fw1h[64:128, p, :, 1], f_l1, 2 * e + 1)

            def moe0_lower_w2(e, p):
                pool.wait_ge(f_h2, e + 1)
                pool.tensor_tensor(fw2l[:, p], fw2[:, p, 0], fw2h[:, p, 0].bitcast(F32), ALU.subtract).then_inc(f_l2, 1)
                lower_b(fw2[64:128, p, 1], fw2h[64:128, p, 1], f_l2, 2 * e + 1)

            moe0_lower_w1(0, 0)
            moe0_lower_w2(0, 0)
            moe0_lower_w1(1, 1)
            ln_pool(1)
            with pool.Fori(0, EXPERTS // 2 - 1) as i:
                for p in range(2):
                    moe0_lower_w1(2 * i + p + 2, p)
                    moe0_lower_w2(2 * i + p + 1, 1 - p)
            moe0_lower_w1(EXPERTS, 0)
            moe0_lower_w2(EXPERTS - 1, 1)
            moe0_lower_w2(EXPERTS, 0)
            projection_lower(3, (m_in[:, :, :, 0], m_in[:, :, :, 1]), (m_inh[:, :, :, 0], m_inh[:, :, :, 1]), m_inl)
            pool.wait_ge(f_y, 1 + EXPERTS)
            pool.memset(xpad, 0.0).then_inc(m_pad, 1)
            ln_pool(2)

            pool.wait_ge(m_w, 160)
            pool.wait_ge(m_x, CTILES)
            acc = xc[:, 1, CTILES - 1].rearrange("p (b t) -> p b t", t=64)
            term = softe[:, 1, 0].rearrange("p (b t) -> p b t", t=64)
            weights = m_conv[:, 1, CTILES - 1]
            pool.tensor_scalar(acc, conv_taps(1, CTILES - 1, 0), weights[:, 0:1], m_convb[:, 1, CTILES - 1:CTILES],
                               ALU.mult, ALU.add).then_inc(m_cp, 1)
            for k in range(1, TAPS):
                pool.wait_ge(m_cp, 2 * k - 1)
                pool.tensor_scalar(term, conv_taps(1, CTILES - 1, k), weights[:, k:k + 1], None,
                                   ALU.mult).then_inc(m_cp, 1)
                pool.wait_ge(m_cp, 2 * k)
                pool.tensor_tensor(acc, acc, term, ALU.add).then_inc(m_cp, 1)
            pool.wait_ge(m_dts, 2)
            pool.wait_ge(m_silu, UNITS)
            pool.tensor_tensor(du[:, 1], dts[:, 1], xc[:, 1], ALU.mult).then_inc(m_du, 1)
            pool.wait_ge(m_dts, 2)
            pool.memset(decay[:, :, :, :, 0:1].rearrange("p a b n o -> p (a b n) o"), 0.0).then_inc(m_zero, 1)

            for B in range(8 * UNITS):
                u, b = B // 8, B % 8
                hb = hbuf[(B // 2) % 3][:, b % 2].rearrange("p n t -> p (n t)")
                if b >= 6:
                    continue
                if b % 2 == 0:
                    pool.wait_ge(m_cld[b // 2], 16 * (u // 3 + 1))
                pool.wait_ge(m_scan, B + 1)
                pool.tensor_tensor(hb, hb, cb[:, b].rearrange("p n t -> p (n t)"), ALU.mult).then_inc(m_mul, 1)
            projection_lower(4, (q_wv[:, 0], q_wv[:, 1]), (q_wvh[:, 0], q_wvh[:, 1]), q_wvl)
            projection_lower(5, (q_wqk[:, :, :, 0], q_wqk[:, :, :, 1]), (q_wqkh[:, :, :, 0], q_wqkh[:, :, :, 1]), q_wqkl)
            ln_pool(3)
            ln_pool(4)

            def lower_w1(e, p):
                pool.wait_ge(g_h1, e + 1)
                pool.tensor_tensor(gw1l[p], gw1[p][:, :, 0], gw1h[p][:, :, 0].bitcast(F32), ALU.subtract).then_inc(g_l1, 1)
                lower_b(gw1[p][64:128, :, 1], gw1h[p][64:128, :, 1], g_l1, 2 * e + 1)

            def lower_w2(e, p):
                pool.wait_ge(g_h2, e + 1)
                pool.tensor_tensor(gw2p[p][:, :, 1], gw2[p], gw2p[p][:, :, 0].bitcast(F32), ALU.subtract).then_inc(g_l2, 1)

            lower_w1(0, 0)
            lower_w2(0, 0)
            lower_w1(1, 1)
            ln_pool(5)
            for t in range(TILES):
                pool.wait_ge(s_x5, t + 1)
                pool.tensor_tensor(h[:, t, :], h[:, t, :], x5[:, t, :], ALU.add).then_inc(s_hx, 1)
            with pool.Fori(0, EXPERTS // 2 - 1) as i:
                for p in range(2):
                    lower_w1(2 * i + p + 2, p)
                    lower_w2(2 * i + p + 1, 1 - p)
            lower_w2(EXPERTS - 1, 1)

        @block.scalar
        def _(act):
            act.dma_start(ident[:], io["ident"]).then_inc(s_const, 16)
            act.dma_start(causal, io["causal"]).then_inc(s_const, 16)
            act.dma_start(tok_b, io["tok_b"].partition_broadcast(128)).then_inc(s_const, 16)

            def ln_act(n, bank):
                act.wait_ge(s_xt, TILES * (TURN[n] + 1))
                act.activation(xh[:, 0], PS[:, bank, :], ACT.Copy).then_inc(s_xta, 1)

            act.wait_ge(s_wv, 16)
            act.activation(wvh, wv, ACT.Copy).then_inc(p_up, 1)
            act.wait_ge(s_wqk, 16)
            for pairs in (FIRST_PAIRS, OTHER_PAIRS):
                act.activation(wqkh[:, pairs], wqk[:, pairs], ACT.Copy).then_inc(p_up, 1)
            ln_act(0, 6)
            for r in range(2):
                act.wait_ge(a_v, r + 1)
                act.activation(vtok[:, 2 * r, :].rearrange("p (a n) -> p a n", a=2),
                               PS[:, 4 * r:4 * r + 2, 0:384], ACT.Copy).then_inc(a_va, 1)

            def q_copy(j):
                act.wait_ge(a_proj, j + 1)
                if j >= 2:
                    act.wait_ge(a_s, j - 1)
                act.activation(qT[:, j % 2, :], PS[:, 0, :], ACT.Copy).then_inc(a_q, 1)

            def exps(j):
                act.wait_ge(a_sub, 4 * j + 4)
                v = prob[:, j % 2].rearrange("p t a k -> p (t a k)")
                act.activation(v, v, ACT.Exp, scale=0.125).then_inc(a_exp, 1)

            def probT_copy(j):
                act.wait_ge(a_pt, j + 1)
                act.activation(probT.rearrange("p t n -> p (t n)"), PS[:, 4, :], ACT.Copy).then_inc(a_ptc, 1)

            def even_copy(j):
                act.wait_ge(a_pv, j + 1)
                act.activation(attnT[:, j, :].rearrange("p (t a q) -> p a t q", a=2, q=64)[:, 0],
                               PS[:, 5, 0:256].rearrange("p (t q) -> p t q", q=64), ACT.Copy).then_inc(a_oe, 1)

            q_copy(0)
            q_copy(1)
            exps(0)
            for j in range(PAIRS):
                if j + 2 < PAIRS:
                    q_copy(j + 2)
                probT_copy(j)
                if j + 1 < PAIRS:
                    exps(j + 1)
                even_copy(j)

            ln_act(1, 6)
            act.sem_inc(f_relu, 2)

            def moe0_relu(e, p):
                act.wait_ge(f_hid, e + 1)
                act.wait_ge(f_hl, e + 1)
                act.activation(frelu[:, p], PS[:, 2 * p:2 * p + 2, :], ACT.Relu).then_inc(f_relu, 1)
                act.wait_ge(f_relu, e + 3)
                act.activation(frelu[:, p], frelu[:, p], ACT.Square).then_inc(f_sq, 1)

            moe0_relu(0, 0)
            act.wait_ge(f_lg, 1)
            act.activation(fscore.rearrange("p t e -> p (t e)"), PS[:, 6, 0:TILES * EXPERTS],
                           ACT.Sigmoid).then_inc(f_sig, 1)

            def upper_by_act(to, src):
                return act.activation(to, src, ACT.Copy)

            def moe0_step(e, p, w1_loads, w2_loads, first=False):
                moe0_upper_w2(act, upper_by_act, e + 1, 1 - p, w2_loads, first)
                if w1_loads is not None:
                    act.wait_ge(f_hid, e + 1)
                    moe0_upper_w1(act, upper_by_act, e + 2, p, w1_loads)
                moe0_relu(e + 1, 1 - p)

            moe0_step(0, 0, 2, 1, first=True)
            with act.Fori(0, EXPERTS // 2 - 1) as i:
                for q in range(2):
                    moe0_step(2 * i + 1 + q, 1 - q, i + 2 + q, i + 2)
            moe0_step(EXPERTS - 1, 1, None, EXPERTS // 2 + 1)

            act.wait_ge(m_w, 160)
            act.activation(m_inh, m_in, ACT.Copy).then_inc(p_up, 1)
            ln_act(2, 6)
            for c in range(CTILES):
                k = 2 * (c % 2)
                act.wait_ge(m_xz, c + 1)
                if c == 0:
                    act.wait_ge(m_pad, 1)
                act.activation(xpad[:, c, :, 3:67], PS[:, k, :].rearrange("p (b t) -> p b t", t=64),
                               ACT.Copy).then_inc(m_x, 1)
                act.activation(zgate[:, c], PS[:, k + 1, :], ACT.Silu).then_inc(m_z, 1)
            def silu(d):
                for c in range(CTILES):
                    if CTILES * d + c < UNITS - 1:
                        act.wait_ge(m_cv, TAPS * (CTILES * d + c + 1))
                    else:
                        act.wait_ge(m_cp, 2 * TAPS - 1)
                    act.activation(xc[:, d, c], xc[:, d, c], ACT.Silu).then_inc(m_silu, 1)

            def xdbl_copy(d):
                act.wait_ge(m_xd, d + 1)
                act.activation(xdbl[0:44, d, :], PS[0:44, 4 + d, :], ACT.Copy).then_inc(m_xdc, 1)

            def softplus_exp(d):
                for c in range(CTILES):
                    act.wait_ge(m_dt, 3 * d + c + 1)
                    act.activation(softx[:, d, c], PS[:, (6, 7, 0)[c], :], ACT.Identity,
                                   bias=m_dtb[:, d, c:c + 1]).then_inc(m_se, 1)
                act.wait_ge(m_se, 5 * d + 3)
                act.activation(softe[:, d], softx[:, d], ACT.Abs).then_inc(m_se, 1)
                act.wait_ge(m_se, 5 * d + 4)
                act.activation(softe[:, d], softe[:, d], ACT.Exp, scale=-1.0).then_inc(m_se, 1)

            def bsel_copy(d):
                act.wait_ge(m_bsl, d + 1)
                act.activation(bsel[:, d].rearrange("p t g n -> p g t n"),
                               PS[:, 4 + d, :].rearrange("p (g t n) -> p g t n", g=8, n=STATE),
                               ACT.Copy).then_inc(m_bsc, 1)

            def softplus_ln(d):
                act.wait_ge(m_sw, 3 * d + 1)
                act.activation(dts[:, d], softw[d], ACT.Ln).then_inc(m_sl, 1)

            silu(0)
            xdbl_copy(0)
            silu(1)
            softplus_exp(0)
            act.activation(m_a.rearrange("p d c n -> p (d c n)"), m_a.rearrange("p d c n -> p (d c n)"),
                           ACT.Exp).then_inc(m_ea, 1)
            xdbl_copy(1)
            softplus_ln(0)
            bsel_copy(0)
            softplus_exp(1)
            softplus_ln(1)
            bsel_copy(1)

            def part1(u):
                act.wait_ge(m_dut, u + 1)
                act.activation(uparts[u][:, 0].rearrange("p t d -> p (t d)"), PS[:, 2 + u % 2, :],
                               ACT.Copy).then_inc(m_p1, 1)

            def part2(u):
                act.wait_ge(m_r1, u + 1)
                act.activation(uparts[u][:, 1].rearrange("p t d -> p (t d)"), dr[:, u % 2],
                               ACT.Copy).then_inc(m_p2, 1)

            def decays(u, half, states=range(STATE)):
                if states[0] == 0 and u >= 1:
                    act.wait_ge(m_scan, 8 * (u - 1) + 4 * half + 4)
                for n in states:
                    i = act.activation(decay[:, half, :, n, 1:64],
                                       dts[:, u // 3, u % 3, 256 * half:256 * half + 256]
                                       .rearrange("p (b t) -> p b t", t=64)[:, :, 1:64],
                                       ACT.Exp, scale=m_a[:, u // 3, u % 3, n:n + 1])
                if states[-1] == STATE - 1:
                    i.then_inc(m_dec, 1)

            part1(0)
            part1(1)
            part2(0)
            part1(2)
            part2(1)
            act.wait_ge(m_zero, 1)
            act.wait_ge(m_na, 1)
            for u in range(2, UNITS):
                if u + 1 < UNITS:
                    part1(u + 1)
                decays(0, 0, range(4 * u - 8, 4 * u - 4))
                part2(u)
            decays(0, 1)
            for u in range(1, UNITS):
                for half in range(2):
                    decays(u, half)

            act.wait_ge(m_y, 4 * UNITS)
            act.wait_ge(q_w, 32)
            act.activation(q_wvh, q_wv, ACT.Copy).then_inc(p_up, 1)
            act.activation(q_wqkh, q_wqk, ACT.Copy).then_inc(p_up, 1)
            ln_act(4, 6)
            act.wait_ge(q_vd, 1)
            act.activation(q_v[:, 0:2, :], PS[:, 2:4, 0:384], ACT.Copy).then_inc(q_va, 1)

            def quad_q_copy(j):
                act.wait_ge(q_proj, j + 1)
                act.activation(q_qT[:, j % 2, :], PS[:, 0, :], ACT.Copy).then_inc(q_q, 1)

            def quad_exps(j):
                act.wait_ge(q_sub, 2 * j + 2)
                v = q_prob[:, j % 2].rearrange("p m t a k -> p (m t a k)")
                act.activation(v, v, ACT.Exp, scale=0.25).then_inc(q_exp, 1)

            def quad_probT_copy(j):
                act.wait_ge(q_pt, 1 + 2 * j)
                act.activation(q_probT[:, 0:2].rearrange("p m t n -> p (m t n)"), PS[:, 6, :],
                               ACT.Copy).then_inc(q_ptc[0], 1)

            def quad_even_copy(j):
                act.wait_ge(q_pv, j + 1)
                act.activation(q_attnT[:, j, :].rearrange("p (t a q) -> p a t q", a=2, q=64)[:, 0],
                               PS[:, 0, 0:256].rearrange("p (t q) -> p t q", q=64), ACT.Copy).then_inc(q_oe, 1)

            quad_q_copy(0)
            quad_q_copy(1)
            quad_exps(0)
            for j in range(QUADS):
                quad_probT_copy(j)
                if j + 1 < QUADS:
                    quad_exps(j + 1)
                quad_even_copy(j)
                if j + 2 < QUADS:
                    quad_q_copy(j + 2)
            ln_act(5, 6)
            def moe1_gelu(e, p, first=False):
                for m in range(3):
                    k = 2 * ((3 * p + m) % 2)
                    act.wait_ge(g_hid, 3 * e + m + 1)
                    if not first:
                        act.wait_ge(g_hl, 3 * (e - 1) + m + 1)
                    act.activation(gact[m], PS[:, k:k + 2, :], ACT.Gelu).then_inc(g_act, 1)

            moe1_gelu(0, 0, first=True)
            act.wait_ge(g_lg, 1)
            act.activation(glog.rearrange("p t e -> p (t e)"), PS[:, 6, 0:TILES * EXPERTS], ACT.Copy).then_inc(g_e, 1)
            moe1_gelu(1, 1)
            act.wait_ge(g_d, 1)
            act.activation(gpair[:, 1], gpair[:, 1], ACT.Exp).then_inc(g_e, 1)
            with act.Fori(1, EXPERTS // 2) as i:
                moe1_gelu(2 * i, 0)
                moe1_gelu(2 * i + 1, 1)

        @block.vector
        def _(dve):

            def add_patch_bias(t):
                dve.wait_ge(s_tok, t + 1)
                if t == 0:
                    dve.wait_ge(s_const, 48)
                dve.tensor_tensor(h[:, t, :], PS[:, t, 0:DIM], tok_b, ALU.add).then_inc(s_h, 1)

            def add_to_h(ready):
                def produce(t):
                    dve.wait_ge(ready, t + 1)
                    dve.tensor_tensor(h[:, t, :], h[:, t, :], PS[:, t, 0:DIM], ALU.add).then_inc(s_h, 1)
                return produce

            def ln_tiles(n, src, src_sem, src_count, each, normalise, produce):
                for t in range(TILES + 1):
                    if t < TILES:
                        if produce:
                            produce(t)
                        dve.wait_ge(src_sem, src_count + each * (t + 1))
                        dve.bn_stats(stats[:, t, :], src[:, t, :]).then_inc(s_mo, 1)
                        dve.wait_ge(s_mo, 2 * (TILES * n + t) + 1)
                        dve.bn_aggr(moments[:, t, :], stats[:, t, :]).then_inc(s_mo, 1)
                    if t >= 1:
                        dve.wait_ge(s_rs, 2 * (TILES * n + t))
                        normalise(t - 1)

            def upper_part(to, src):
                return dve.tensor_copy(to, src)

            def lower_part(to, src, hi):
                return dve.tensor_tensor(to, src, hi.bitcast(F32), ALU.subtract)

            def split_x(n, bank):
                turn = TURN[n]
                dve.wait_ge(s_xt, TILES * (turn + 1))
                upper_part(xh[:, 1], PS[:, bank, :]).then_inc(s_xtb, 1)
                dve.wait_ge(s_xta, turn + 1)
                lower_part(xl[:, 0], PS[:, bank - 1, :], xh[:, 0]).then_inc(s_xtb, 1)
                dve.wait_ge(s_xtb, 3 * turn + 1)
                lower_part(xl[:, 1], PS[:, bank, :], xh[:, 1]).then_inc(s_xtb, 1)

            def ln_vector(n, src, src_sem, src_count, bank, produce=None):
                def normalise(t):
                    for to, cols in ((slice(0, DIM), slice(0, DIM)), (slice(DIM, 256), slice(128, DIM))):
                        dve.tensor_scalar(xn[:, t, to], src[:, t, cols], moments[:, t, 0:1], rstd[:, t:t + 1],
                                          ALU.subtract, ALU.mult).then_inc(s_xn, 1)

                ln_tiles(n, src, src_sem, src_count, 1, normalise, produce)
                split_x(n, bank)

            def ln_plain(n, src, src_sem, src_count, to, produce):
                def normalise(t):
                    dve.tensor_scalar(to[:, t, 0:DIM], src[:, t, :], moments[:, t, 0:1], rstd[:, t:t + 1],
                                      ALU.subtract, ALU.mult).then_inc(s_xn, 2)

                ln_tiles(n, src, src_sem, src_count, 1, normalise, produce)

            def ln_affine(n, src, src_sem, src_count, each, bank, produce=None):
                gamma, beta = ln_gb[2 * (n - 4)], ln_gb[2 * (n - 4) + 1]
                steps = s_aff[n - 4]
                dve.wait_ge(g_gb, 80)

                def normalise(t):
                    dve.scalar_tensor_tensor(scaled[:, t], src[:, t, :], moments[:, t, 0:1], gamma,
                                             ALU.subtract, ALU.mult).then_inc(steps, 1)
                    dve.wait_ge(steps, t + 1)
                    for to, cols in ((slice(0, DIM), slice(0, DIM)), (slice(DIM, 256), slice(128, DIM))):
                        dve.scalar_tensor_tensor(xn[:, t, to], scaled[:, t, cols], rstd[:, t:t + 1], beta[:, cols],
                                                 ALU.mult, ALU.add).then_inc(s_xn, 1)

                ln_tiles(n, src, src_sem, src_count, each, normalise, produce)
                split_x(n, bank)

            dve.wait_ge(p_up, 1)
            lower_part(wvl, wv[:, 0], wvh[:, 0]).then_inc(p_lo, 1)
            lower_part(wvh[64:128, 1], wv[64:128, 1], wvh[64:128, 1]).then_inc(p_lo, 1)
            ln_vector(0, h, s_h, 0, 7, add_patch_bias)
            for r in range(2):
                dve.wait_ge(a_v, r + 1)
                dve.tensor_copy(vtok[:, 2 * r + 1, :].rearrange("p (a n) -> p a n", a=2),
                                PS[:, 4 * r + 2:4 * r + 4, 0:384]).then_inc(a_vd, 1)

            def k_copy(j):
                dve.wait_ge(a_proj, j + 1)
                if j >= 2:
                    dve.wait_ge(a_s, j - 1)
                dve.tensor_copy(kT[:, j % 2, :], PS[:, 1, :]).then_inc(a_k, 1)

            def shift(j):
                b = j % 2
                dve.wait_ge(a_s, j + 1)
                if j >= 2:
                    dve.wait_ge(a_pt, j - 1)
                sc = prob[:, b]
                flat = sc.rearrange("p t a k -> p (t a) k")
                for a in range(2):
                    dve.tensor_tensor(sc[:, :, a], PS[:, 2 + a, 0:256].rearrange("p (t k) -> p t k", k=64),
                                      causal.unsqueeze(1).to_broadcast([128, 4, 64]),
                                      ALU.add).then_inc(a_sub, 1)
                dve.wait_ge(a_sub, 4 * j + 2)
                dve.tensor_reduce(rowmax[:, b, :], flat, AX.X, ALU.max).then_inc(a_sub, 1)
                dve.wait_ge(a_sub, 4 * j + 3)
                dve.tensor_tensor(flat, flat, rowmax[:, b, :].unsqueeze(2).to_broadcast([128, 8, 64]),
                                  ALU.subtract).then_inc(a_sub, 1)

            def normalise(j):
                b = j % 2
                flat = prob[:, b].rearrange("p t a k -> p (t a) k")
                dve.wait_ge(a_exp, j + 1)
                dve.tensor_reduce(rowsum[:, b, :], flat, AX.X, ALU.add).then_inc(a_p, 1)
                dve.wait_ge(a_p, 3 * j + 1)
                dve.reciprocal(rowsum[:, b, :], rowsum[:, b, :]).then_inc(a_p, 1)
                dve.wait_ge(a_p, 3 * j + 2)
                dve.tensor_tensor(flat, flat, rowsum[:, b, :].unsqueeze(2).to_broadcast([128, 8, 64]),
                                  ALU.mult).then_inc(a_p, 1)

            def odd_copy(j):
                dve.wait_ge(a_pv, j + 1)
                dve.tensor_copy(attnT[:, j, :].rearrange("p (t a q) -> p a t q", a=2, q=64)[:, 1],
                                PS[:, 6, 0:256].rearrange("p (t q) -> p t q", q=64)).then_inc(a_oo, 1)

            k_copy(0)
            k_copy(1)
            shift(0)

            def split_router(raw, hi, lo, done):
                upper_part(hi, raw).then_inc(done, 1)
                dve.wait_ge(done, 1)
                lower_part(lo, raw[:, 0], hi[:, 0]).then_inc(done, 1)
                lower_part(hi[64:128, 1], raw[64:128, 1], hi[64:128, 1]).then_inc(done, 1)

            for j in range(PAIRS):
                normalise(j)
                if j + 2 < PAIRS:
                    k_copy(j + 2)
                if j + 1 < PAIRS:
                    shift(j + 1)
                odd_copy(j)
                if j == PAIRS - 2:
                    moe0_upper_w1(dve, upper_part, 0, 0, 1)
                    moe0_upper_w2(dve, upper_part, 0, 0, 1, first=True)
                    moe0_upper_w1(dve, upper_part, 1, 1, 1)
                    dve.wait_ge(f_rw, 32)
                    split_router(frw, frwh, frwl, f_rs)

            ln_vector(1, h, s_h, 4, 7, add_to_h(a_o))
            dve.sem_inc(f_acc, 8)
            dve.sem_inc(f_hl, 2)

            def moe0_split_hidden(e, p):
                dve.wait_ge(f_sq, e + 1)
                upper_part(fhh[:, p], frelu[:, p]).then_inc(s_hh, 1)
                dve.wait_ge(s_hh, e + 1)
                lower_part(fhl[:, p], frelu[:, p], fhh[:, p]).then_inc(f_hl, 1)

            def moe0_add(e, p):
                dve.wait_ge(f_y, e + 1)
                for t in range(TILES):
                    dve.wait_ge(f_acc, TILES * e + t + 5)
                    dve.scalar_tensor_tensor(h[:, t, :], PS[:, 4 + 2 * p + t % 2, (t // 2) * DIM:(t // 2 + 1) * DIM],
                                             fwt[:, t, bass.ds(e, 1)], h[:, t, :],
                                             ALU.mult, ALU.add).then_inc(f_acc, 1)

            steps = [0]

            def routing_step(ins):
                steps[0] += 1
                ins.then_inc(f_rt, 1)
                dve.wait_ge(f_rt, steps[0])

            moe0_split_hidden(0, 0)
            dve.wait_ge(f_sig, 1)
            dve.wait_ge(f_rw, 32)
            dve.wait_ge(s_ids, 2)
            routing_step(dve.tensor_tensor(fpick, fscore, fbias.unsqueeze(1).to_broadcast([128, TILES, EXPERTS]),
                                           ALU.add))
            for t in range(TILES):
                routing_step(dve.max(ftop[:, t, :], fpick[:, t, :]))
                routing_step(dve.max_index(fidx[:, t, :], ftop[:, t, :], fpick[:, t, :]))
            routing_step(dve.tensor_copy(fidxf, fidx[:, :, 0:2]))
            for k in range(2):
                routing_step(dve.tensor_tensor(fhot[:, k], expert_ids[:],
                                               fidxf[:, :, k:k + 1].to_broadcast([128, TILES, EXPERTS]),
                                               ALU.is_equal))
            routing_step(dve.tensor_tensor(fhot[:, 0], fhot[:, 0], fhot[:, 1], ALU.add))
            routing_step(dve.tensor_tensor(fhot[:, 0], fhot[:, 0], fscore, ALU.mult))
            routing_step(dve.tensor_reduce(fsum, fhot[:, 0], AX.X, ALU.add))
            routing_step(dve.tensor_scalar(fsum, fsum, 1e-20, None, ALU.add))
            routing_step(dve.reciprocal(fsum, fsum))
            routing_step(dve.tensor_tensor(fwt[:, :, 1:1 + EXPERTS], fhot[:, 0],
                                           fsum.unsqueeze(2).to_broadcast([128, TILES, EXPERTS]), ALU.mult))
            moe0_split_hidden(1, 1)
            moe0_add(0, 0)
            with dve.Fori(0, EXPERTS // 2 - 1) as i:
                for q in range(2):
                    moe0_split_hidden(2 * i + 2 + q, q)
                    moe0_add(2 * i + 1 + q, 1 - q)
            moe0_split_hidden(EXPERTS, 0)
            moe0_add(EXPERTS - 1, 1)
            moe0_add(EXPERTS, 0)

            ln_vector(2, h, f_acc, 8 + TILES * EXPERTS, 7)
            dve.wait_ge(m_w, 160)
            for n in range(UNITS - 1):
                d, c = n // CTILES, n % CTILES
                acc = xc[:, d, c].rearrange("p (b t) -> p b t", t=64)
                if d == 0:
                    dve.wait_ge(m_x, c + 1)
                dve.tensor_scalar(acc, conv_taps(d, c, 0), m_conv[:, d, c, 0:1], m_convb[:, d, c:c + 1],
                                  ALU.mult, ALU.add).then_inc(m_cv, 1)
                for k in range(1, TAPS):
                    dve.wait_ge(m_cv, TAPS * n + k)
                    dve.scalar_tensor_tensor(acc, conv_taps(d, c, k), m_conv[:, d, c, k:k + 1], acc,
                                             ALU.mult, ALU.add).then_inc(m_cv, 1)

            bsteps = [0]

            def split_step(ins):
                bsteps[0] += 1
                ins.then_inc(m_bs, 1)
                dve.wait_ge(m_bs, bsteps[0])

            def split_b(d):
                dve.wait_ge(m_bt, d + 1)
                raw = bts[:, d]
                part = [bparts[:, d, i] for i in range(3)]
                split_step(dve.tensor_copy(raw, PS[:, 4 + d, 0:TILES * 44]
                                           .rearrange("p (t r) -> p t r", r=44)[:, :, RANK:RANK + STATE]))
                split_step(dve.tensor_copy(part[0], raw))
                split_step(dve.tensor_tensor(raw, raw, part[0], ALU.subtract))
                split_step(dve.tensor_copy(part[1], raw))
                split_step(dve.tensor_tensor(part[2], raw, part[1], ALU.subtract))

            def softplus_vector(d):
                dve.wait_ge(m_se, 5 * d + 5)
                dve.tensor_scalar(softw[d], softe[:, d], 1.0, None, ALU.add).then_inc(m_sw, 1)
                dve.wait_ge(m_sw, 3 * d + 1)
                dve.scalar_tensor_tensor(softe[:, d], softw[d], 1.0, softe[:, d],
                                         ALU.subtract, ALU.subtract).then_inc(m_sw, 1)
                dve.wait_ge(m_sw, 3 * d + 2)
                dve.scalar_tensor_tensor(softx[:, d], softx[:, d], 0.0, softe[:, d],
                                         ALU.max, ALU.subtract).then_inc(m_sw, 1)

            def dt_and_dtu(d):
                dve.wait_ge(m_sl, d + 1)
                dve.wait_ge(m_sw, 3 * d + 3)
                dve.tensor_tensor(dts[:, d], dts[:, d], softx[:, d], ALU.add).then_inc(m_dts, 1)
                if d == 0:
                    dve.wait_ge(m_dts, 1)
                    dve.wait_ge(m_silu, CTILES)
                    dve.tensor_tensor(du[:, 0], dts[:, 0], xc[:, 0], ALU.mult).then_inc(m_du, 1)

            def rest1(u):
                dve.wait_ge(m_p1, u + 1)
                if u >= 2:
                    dve.wait_ge(m_p3, u - 1)
                dve.tensor_tensor(dr[:, u % 2], PS[:, 2 + u % 2, :],
                                  uparts[u][:, 0].rearrange("p t d -> p (t d)"), ALU.subtract).then_inc(m_r1, 1)

            def b_blocks(d, quarter):
                dve.wait_ge(m_bsc, d + 1)
                for t in range(4 * quarter, 4 * quarter + 4):
                    dve.tensor_scalar(bd[:, d, :, t, :], bsel[:, d].rearrange("p t g n -> p (t g) n"),
                                      m_mask[:, t:t + 1], None, ALU.mult).then_inc(m_bd, 1)

            def part3(u):
                dve.wait_ge(m_p2, u + 1)
                dve.tensor_tensor(uparts[u][:, 2].rearrange("p t d -> p (t d)"), dr[:, u % 2],
                                  uparts[u][:, 1].rearrange("p t d -> p (t d)"), ALU.subtract).then_inc(m_p3, 1)

            split_b(0)
            softplus_vector(0)
            dt_and_dtu(0)
            dve.wait_ge(m_ea, 1)
            dve.tensor_scalar(m_a.rearrange("p d c n -> p (d c n)"), m_a.rearrange("p d c n -> p (d c n)"),
                              -1.0, None, ALU.mult).then_inc(m_na, 1)
            split_b(1)
            b_blocks(0, 0)
            b_blocks(0, 1)
            softplus_vector(1)
            dt_and_dtu(1)
            rest1(0)
            for u in range(UNITS):
                if u + 1 < UNITS:
                    rest1(u + 1)
                part3(u)
                if u in (1, 2):
                    b_blocks(0, u + 1)

            def take_y(u, half):
                d, c = u // 3, u % 3
                cols = slice(256 * half, 256 * half + 256)
                dve.wait_ge(m_y, 4 * u + 2 * half + 2)
                to = yf[:, c, cols] if d == 0 else yr[:, half]
                dve.scalar_tensor_tensor(to, xc[:, d, c, cols], m_d[:, d, c:c + 1],
                                         PS[:, 4 + half, 0:256], ALU.mult, ALU.add).then_inc(m_post, 1)
                if d == 1:
                    n = 2 * c + half + 1
                    dve.wait_ge(m_post, 2 * u + half + 1)
                    f = yf[:, c, cols].rearrange("p (b t) -> p b t", t=64)
                    dve.tensor_tensor(f, f, yr[:, half].rearrange("p (b t) -> p b t", t=64)[:, :, ::-1],
                                      ALU.add).then_inc(m_sum, 1)
                    dve.wait_ge(m_sum, n)
                    dve.tensor_tensor(zgate[:, c, cols], yf[:, c, cols], zgate[:, c, cols],
                                      ALU.mult).then_inc(m_g, 1)

            for B in range(8 * UNITS):
                u, b = B // 8, B % 8
                chunk = B // 2
                dve.wait_ge(m_b, B + 1)
                if b % 4 == 0:
                    dve.wait_ge(m_dec, 2 * u + b // 4 + 1)
                if b % 2 == 0 and chunk >= 3:
                    dve.wait_ge(m_y, chunk - 2)
                if B == 4:
                    dve.wait_ge(m_cst, 32)
                    dve.wait_ge(m_ust[0], 48)
                    dve.wait_ge(m_ust[1], 48)
                dve.tensor_tensor_scan(hbuf[chunk % 3][:, b % 2].rearrange("p n t -> p (n t)"),
                                       decay[:, b // 4, b % 4].rearrange("p n t -> p (n t)"),
                                       PS[:, 2 * (b % 2):2 * (b % 2) + 2, :].rearrange("p k x -> p (k x)"),
                                       0.0, ALU.mult, ALU.add).then_inc(m_scan, 1)
                if b == 7:
                    hb = hbuf[chunk % 3]
                    dve.wait_ge(m_cld[3], 16 * (u // 3 + 1))
                    for a in range(2):
                        dve.wait_ge(m_scan, B + a)
                        dve.tensor_tensor(hb[:, a], hb[:, a], cb[:, 6 + a], ALU.mult).then_inc(m_fold, 1)
                    dve.wait_ge(m_fold, 3 * u + 2)
                    dve.tensor_tensor(hb[:, :, 0:8], hb[:, :, 0:8], hb[:, :, 8:16], ALU.add).then_inc(m_fold, 1)
                if B in (9, 11, 13, 15):
                    b_blocks(1, (B - 9) // 2)
                if b % 4 == 0 and chunk >= 4:
                    half_no = (chunk - 4) // 2
                    take_y(half_no // 2, half_no % 2)
            take_y(UNITS - 1, 0)
            take_y(UNITS - 1, 1)

            ln_plain(3, h, s_h, 8, x4, add_to_h(m_o))
            ln_affine(4, x4, s_xn, 8 * 3, 2, 7)
            dve.wait_ge(q_vd, 2)
            dve.tensor_copy(q_v[:, 2:4, :], PS[:, 4:6, 0:384]).then_inc(q_vv, 1)

            def quad_k_copy(j):
                dve.wait_ge(q_proj, j + 1)
                dve.tensor_copy(q_kT[:, j % 2, :], PS[:, 1, :]).then_inc(q_k, 1)

            def quad_shift(j):
                b = j % 2
                dve.wait_ge(q_s, j + 1)
                sc = PS[:, 2:6, 0:256].rearrange("p m (x k) -> p m x k", k=64)
                mx = q_max[:, b].rearrange("p (m x) -> p m x", m=4)
                dve.tensor_reduce(mx, sc, AX.X, ALU.max).then_inc(q_sub, 1)
                dve.wait_ge(q_sub, 2 * j + 1)
                dve.tensor_tensor(q_prob[:, b].rearrange("p m t a k -> p m (t a) k"), sc,
                                  mx.unsqueeze(3).to_broadcast([128, 4, 4, 64]), ALU.subtract).then_inc(q_sub, 1)

            def quad_normalise(j):
                b = j % 2
                flat = q_prob[:, b].rearrange("p m t a k -> p (m t a) k")
                dve.wait_ge(q_exp, j + 1)
                dve.tensor_reduce(q_sum[:, b], flat, AX.X, ALU.add).then_inc(q_p, 1)
                dve.wait_ge(q_p, 3 * j + 1)
                dve.reciprocal(q_sum[:, b], q_sum[:, b]).then_inc(q_p, 1)
                dve.wait_ge(q_p, 3 * j + 2)
                dve.tensor_tensor(flat, flat, q_sum[:, b].unsqueeze(2).to_broadcast([128, 16, 64]),
                                  ALU.mult).then_inc(q_p, 1)

            def quad_probT_copy_b(j):
                dve.wait_ge(q_pt, 2 + 2 * j)
                dve.tensor_copy(q_probT[:, 2:4].rearrange("p m t n -> p (m t n)"), PS[:, 7, :]).then_inc(q_ptc[1], 1)

            def quad_odd_copy(j):
                dve.wait_ge(q_pv, j + 1)
                dve.tensor_copy(q_attnT[:, j, :].rearrange("p (t a q) -> p a t q", a=2, q=64)[:, 1],
                                PS[:, 1, 0:256].rearrange("p (t q) -> p t q", q=64)).then_inc(q_oo, 1)

            quad_k_copy(0)
            quad_k_copy(1)

            def upper_w1(e, p, loads):
                dve.wait_ge(g_w1[p], 16 * loads)
                upper_part(gw1h[p], gw1[p]).then_inc(g_h1, 1)

            def upper_w2(e, p, loads, first=False):
                dve.wait_ge(g_w2[p], 16 * loads)
                if not first:
                    dve.wait_ge(g_y, TILES * (e - 1))
                upper_part(gw2p[p][:, :, 0], gw2[p]).then_inc(g_h2, 1)

            quad_shift(0)
            for j in range(QUADS):
                quad_normalise(j)
                quad_probT_copy_b(j)
                if j + 1 < QUADS:
                    quad_shift(j + 1)
                quad_odd_copy(j)
                if j == 0:
                    upper_w1(0, 0, 1)
                    upper_w2(0, 0, 1, first=True)
                    upper_w1(1, 1, 1)
                    dve.wait_ge(g_gb, 80)
                    split_router(grw, grwh, grwl, g_rs)
                if j + 2 < QUADS:
                    quad_k_copy(j + 2)

            def make_x5(t):
                dve.wait_ge(q_o, t + 1)
                dve.tensor_tensor(x5[:, t, :], x4[:, t, :], PS[:, t, 0:DIM], ALU.add).then_inc(s_x5, 1)

            ln_affine(5, x5, s_x5, 0, 1, 7, make_x5)
            dve.sem_inc(g_acc, 8)

            def moe1_add(e, p):
                for n, (t, piece) in enumerate(ADD_ORDER):
                    if piece == 0:
                        dve.wait_ge(g_y, TILES * e + t + 1)
                    dve.wait_ge(g_acc, 2 * TILES * e + 7 + n)
                    dve.scalar_tensor_tensor(h[:, t, :], PS[:, 4 + t, piece * DIM:(piece + 1) * DIM],
                                             gwt[:, t, bass.ds(e, 1)], h[:, t, :],
                                             ALU.mult, ALU.add).then_inc(g_acc, 1)

            def split_hidden(e, p):
                for m in range(3):
                    pair = slice(2 * m, 2 * m + 2)
                    dve.wait_ge(g_act, 3 * e + m + 1)
                    upper_part(ghh[p][:, pair], gact[m]).then_inc(s_hh, 1)
                    dve.wait_ge(s_hh, 1 + EXPERTS + 3 * e + m + 1)
                    lower_part(ghl[p][:, pair], gact[m], ghh[p][:, pair]).then_inc(g_hl, 1)

            split_hidden(0, 0)
            dve.wait_ge(g_hid, 3)
            upper_w1(2, 0, 2)
            split_hidden(1, 1)
            upper_w2(1, 1, 1, first=True)
            steps1 = [0]

            def routing1_step(ins):
                steps1[0] += 1
                ins.then_inc(g_rt, 1)
                dve.wait_ge(g_rt, steps1[0])

            dve.wait_ge(g_e, 1)
            for t in range(TILES):
                routing1_step(dve.max(gtop[:, t, :], glog[:, t, :]))
                routing1_step(dve.max_index(gidx[:, t, :], gtop[:, t, :], glog[:, t, :]))
            dve.tensor_tensor(gpair[:, 1], gtop[:, :, 1], gtop[:, :, 0], ALU.subtract).then_inc(g_d, 1)
            routing1_step(dve.tensor_copy(gidxf, gidx[:, :, 0:2]))
            dve.wait_ge(g_e, 2)
            routing1_step(dve.tensor_scalar(gpair[:, 0], gpair[:, 1], 1.0, None, ALU.add))
            routing1_step(dve.reciprocal(gpair[:, 0], gpair[:, 0]))
            routing1_step(dve.tensor_tensor(gpair[:, 1], gpair[:, 1], gpair[:, 0], ALU.mult))
            for k in range(2):
                routing1_step(dve.tensor_tensor(ghot[:, k], expert_ids[:],
                                                gidxf[:, :, k:k + 1].to_broadcast([128, TILES, EXPERTS]),
                                                ALU.is_equal))
                routing1_step(dve.tensor_tensor(ghot[:, k], ghot[:, k],
                                                gpair[:, k].unsqueeze(2).to_broadcast([128, TILES, EXPERTS]),
                                                ALU.mult))
            routing1_step(dve.tensor_tensor(gwt, ghot[:, 0], ghot[:, 1], ALU.add))
            dve.wait_ge(s_hx, TILES)

            moe1_add(0, 0)

            def moe1_step(e, p, w1_loads, w2_loads):
                if w1_loads is not None:
                    dve.wait_ge(g_hid, 3 * e + 3)
                    upper_w1(e + 2, p, w1_loads)
                split_hidden(e + 1, 1 - p)
                upper_w2(e + 1, 1 - p, w2_loads)
                moe1_add(e, p)

            with dve.Fori(0, EXPERTS // 2 - 2) as i:
                for q in range(2):
                    moe1_step(2 * i + 1 + q, 1 - q, i + 2 + q, i + 2)
            moe1_step(EXPERTS - 3, 1, EXPERTS // 2, EXPERTS // 2)
            moe1_step(EXPERTS - 2, 0, None, EXPERTS // 2)
            moe1_add(EXPERTS - 1, 1)

        @block.tensor
        def _(pe):
            def keep_warm(products, bank=6, operand=ident[:]):
                for _ in range(products):
                    pe.matmul(PS[:, bank, 0:128], operand, operand, start=True, stop=True)

            pe.wait_ge(s_zero, 1)
            keep_warm(8, operand=xn[:, 0, 0:128])
            pe.wait_ge(s_tokw, 16)
            for k in range(PATCH_K):
                pe.wait_ge(s_patch[k], 16)
                for t in range(TILES):
                    mm = pe.matmul(PS[:, t, 0:DIM], patches[:, k, t * 128:t * 128 + 128], tok_w[:, k, :],
                                   start=(k == 0), stop=(k == PATCH_K - 1))
                    if k == PATCH_K - 1:
                        mm.then_inc(s_tok, 1)
            pe.wait_ge(s_const, 48)

            def split_product(to, pairs):
                for k, (stationary, moving) in enumerate(pairs):
                    mm = pe.matmul(to, stationary, moving, start=(k == 0),
                                   stop=(k == len(pairs) - 1))
                return mm

            def x_stationary(to, t, wh, wl):
                cols = slice(t * 128, t * 128 + 128)
                return split_product(to, ((xh[:, 0, cols], wh[:, 0]), (xl[:, 0, cols], wh[:, 0]), (xh[:, 0, cols], wl),
                                          (xh[:, 1, cols], wh[:, 1]), (xl[:, 1, cols], wh[:, 1])))

            def x_moving(to, wh, wl):
                return split_product(to, ((wh[:, 0], xh[:, 0]), (wh[:, 0], xl[:, 0]), (wl, xh[:, 0]),
                                          (wh[:, 1], xh[:, 1]), (wh[:, 1], xl[:, 1])))

            def ln_tensor(n, bank_a, bank_b):
                for t in range(TILES):
                    cols = slice(t * 128, t * 128 + 128)
                    pe.wait_ge(s_xn, 8 * n + 2 * t + 2)
                    pe.transpose(PS[:, bank_a, cols], xn[:, t, 0:128], ident[:])
                    pe.transpose(PS[:, bank_b, cols], xn[:, t, 128:256], ident[:]).then_inc(s_xt, 1)

            keep_warm(20)
            ln_tensor(0, 6, 7)
            keep_warm(12, bank=5)
            pe.wait_ge(p_lo, 2)
            pe.wait_ge(s_xta, 1)
            pe.wait_ge(s_xtb, 3)
            pe.wait_ge(s_h, 4)
            for r in range(2):
                for half in range(2):
                    ncol = slice(half * 384, half * 384 + 384)
                    for i in range(2):
                        mm = x_stationary(PS[:, 4 * r + 2 * i + half, 0:384], 2 * r + i, wvh[:, :, ncol], wvl[:, ncol])
                mm.then_inc(a_v, 1)

            def project(j):
                if j >= 1:
                    pe.wait_ge(a_q, j)
                    pe.wait_ge(a_k, j)
                else:
                    pe.wait_ge(a_va, 1)
                    pe.wait_ge(a_vd, 1)
                pe.wait_ge(p_lo, 4 if j < 2 else 6)
                for i in range(2):
                    mm = x_moving(PS[:, i, :], wqkh[:, j, i], wqkl[:, j, i])
                mm.then_inc(a_proj, 1)

            def scores(j):
                b = j % 2
                pe.wait_ge(a_q, j + 1)
                pe.wait_ge(a_k, j + 1)
                if j >= 1:
                    pe.wait_ge(a_sub, 4 * (j - 1) + 2)
                for swap in range(2):
                    for t in range(TILES):
                        for i in ((0, 1), (1, 0))[swap]:
                            a = (i + swap) % 2
                            rows = slice(64 * i, 64 * i + 64)
                            img = 2 * t + a
                            cols = slice(img * 64, img * 64 + 64)
                            mm = pe.matmul(PS[rows, 2 + a, t * 64:t * 64 + 64], qT[rows, b, cols],
                                           kT[rows, b, cols], start=True, stop=True)
                mm.then_inc(a_s, 1)

            def transpose_probs(j):
                keep_warm(7, bank=7)
                pe.wait_ge(a_p, 3 * j + 3)
                if j >= 1:
                    pe.wait_ge(a_ptc, j)
                for t in range(TILES):
                    mm = pe.transpose(PS[:, 4, t * 128:t * 128 + 128], prob[:, j % 2, t].rearrange("p a k -> p (a k)"), ident[:])
                mm.then_inc(a_pt, 1)

            def weigh(j):
                pe.wait_ge(a_ptc, j + 1)
                if j >= 1:
                    pe.wait_ge(a_oe, j)
                    pe.wait_ge(a_oo, j)
                for i in range(2):
                    for t in range(TILES):
                        for a in range(2):
                            rows = slice(64 * a, 64 * a + 64)
                            outp = slice(64 * i, 64 * i + 64)
                            mm = pe.matmul(PS[outp, 5 + a, t * 64:t * 64 + 64],
                                           vtok[rows, t, (2 * j + i) * 64:(2 * j + i) * 64 + 64],
                                           probT[rows, t, i * 64:i * 64 + 64], start=True, stop=True)
                mm.then_inc(a_pv, 1)

            project(0)
            pe.wait_ge(a_va, 2)
            pe.wait_ge(a_vd, 2)
            project(1)
            scores(0)
            for j in range(PAIRS):
                if j + 2 < PAIRS:
                    project(j + 2)
                transpose_probs(j)
                if j + 1 < PAIRS:
                    scores(j + 1)
                weigh(j)
            pe.wait_ge(a_oe, PAIRS)
            pe.wait_ge(a_oo, PAIRS)
            pe.wait_ge(s_wo, 16)
            for t in range(TILES):
                for j in range(PAIRS):
                    mm = pe.matmul(PS[:, t, 0:DIM], attnT[:, j, t * 128:t * 128 + 128], wo[:, j, :],
                                   start=(j == 0), stop=(j == PAIRS - 1))
                mm.then_inc(a_o, 1)

            keep_warm(14)
            ln_tensor(1, 6, 7)
            keep_warm(12, bank=5)
            pe.wait_ge(s_xta, 2)
            pe.wait_ge(s_xtb, 6)

            def router_logits(wh, wl):
                for t in range(TILES):
                    mm = x_stationary(PS[:, 6, t * EXPERTS:(t + 1) * EXPERTS], t, wh, wl)
                return mm

            def moe0_up(e, p):
                pe.wait_ge(f_l1, 2 * e + 2)
                pe.wait_ge(f_relu, e + 1)
                for i in range(2):
                    mm = x_moving(PS[:, 2 * p + i, :], fw1h[:, p, i], fw1l[:, p, i])
                mm.then_inc(f_hid, 1)

            def moe0_down(e, p):
                pe.wait_ge(f_l2, 2 * e + 2)
                pe.wait_ge(f_hl, e + 3)
                pe.wait_ge(f_acc, TILES * e + 4)
                for t in range(TILES):
                    cols = slice(t * 128, t * 128 + 128)
                    mm = split_product(PS[:, 4 + 2 * p + t % 2, (t // 2) * DIM:(t // 2 + 1) * DIM], (
                        (fhh[:, p, 0, cols], fw2h[:, p, 0]), (fhh[:, p, 0, cols], fw2l[:, p]),
                        (fhl[:, p, 0, cols], fw2h[:, p, 0]),
                        (fhh[:, p, 1, cols], fw2h[:, p, 1]), (fhl[:, p, 1, cols], fw2h[:, p, 1])))
                mm.then_inc(f_y, 1)

            moe0_up(0, 0)
            pe.wait_ge(f_rs, 3)
            router_logits(frwh, frwl).then_inc(f_lg, 1)
            pe.wait_ge(f_sig, 1)
            with pe.Fori(0, EXPERTS // 2) as i:
                for p in range(2):
                    moe0_up(2 * i + p + 1, 1 - p)
                    moe0_down(2 * i + p, p)
            moe0_down(EXPERTS, 0)

            keep_warm(18, bank=0)
            ln_tensor(2, 6, 7)
            keep_warm(6, bank=0)
            pe.wait_ge(m_w, 160)
            pe.wait_ge(p_lo, 8)
            pe.wait_ge(s_xta, 3)
            pe.wait_ge(s_xtb, 9)
            for c in range(CTILES):
                k = 2 * (c % 2)
                if c >= 2:
                    pe.wait_ge(m_x, c - 1)
                    pe.wait_ge(m_z, c - 1)
                for i in range(2):
                    mm = x_moving(PS[:, k + i, :], m_inh[:, c, i], m_inl[:, c, i])
                mm.then_inc(m_xz, 1)

            def x_dbl(d):
                for c in range(CTILES):
                    pe.wait_ge(m_silu, 3 * d + c + 1)
                    mm = pe.matmul(PS[0:44, 4 + d, :], m_xp[:, d, c, :], xc[:, d, c], start=(c == 0),
                                   stop=(c == CTILES - 1))
                mm.then_inc(m_xd, 1)
                pe.wait_ge(m_xdc, d + 1)
                for t in range(TILES):
                    mm = pe.transpose(PS[:, 4 + d, t * 44:t * 44 + 44], xdbl[0:44, d, t * 128:t * 128 + 128],
                                      ident[0:44, 0:44])
                mm.then_inc(m_bt, 1)

            def raw_dt(d):
                if d == 1:
                    pe.wait_ge(m_se, 3)
                for c in range(CTILES):
                    pe.matmul(PS[:, (6, 7, 0)[c], :], m_dtw[0:RANK, d, c * 128:c * 128 + 128], xdbl[0:RANK, d, :],
                              start=True, stop=True).then_inc(m_dt, 1)

            def select_b(d):
                pe.wait_ge(m_bs, 5 * d + 5)
                pe.wait_ge(m_sell, 16)
                for g in range(8):
                    for j in range(3):
                        mm = pe.matmul(PS[:, 4 + d, g * 64:g * 64 + 64], m_sel[:, g, j, :],
                                       bparts[:, d, j].rearrange("p t n -> p (t n)"), start=(j == 0), stop=(j == 2))
                mm.then_inc(m_bsl, 1)

            def transpose_dtu(u):
                pe.wait_ge(m_du, u // 3 + 1)
                if u >= 2:
                    pe.wait_ge(m_r1, u - 1)
                for t in range(TILES):
                    mm = pe.transpose(PS[:, 2 + u % 2, t * 128:t * 128 + 128], du[:, u // 3, u % 3, t * 128:t * 128 + 128],
                                      ident[:])
                mm.then_inc(m_dut, 1)

            x_dbl(0)
            raw_dt(0)
            x_dbl(1)
            raw_dt(1)
            select_b(0)
            select_b(1)
            pe.wait_ge(m_z, CTILES)
            for u in range(UNITS):
                transpose_dtu(u)

            def form_inputs(B):
                u, b = B // 8, B % 8
                if b == 0:
                    pe.wait_ge(m_lw, 16 * COMBOS * (u + 1))
                    pe.wait_ge(m_bd, STEP * (u // 3 + 1))
                if B >= 2:
                    pe.wait_ge(m_scan, B - 1)
                for s in range(4):
                    for nh in range(2):
                        to = PS[:, 2 * (b % 2) + nh, :].rearrange("p (n t) -> p t n", t=64)
                        mm = pe.matmul(to[:, s * STEP:(s + 1) * STEP, :],
                                       lw[:, u % 2, (b % 2) * 4 + s, b // 2, :],
                                       bd[:, u // 3, b * 4 + s, :, nh * 8:nh * 8 + 8], start=True, stop=True)
                mm.then_inc(m_b, 1)

            def sum_states(v):
                u, q = v // 4, v % 4
                pe.wait_ge(m_mul, by_pool(v))
                if q == 3:
                    pe.wait_ge(m_fold, 3 * u + 3)
                if q % 2 == 0 and u >= 1:
                    pe.wait_ge(m_post, 2 * (u - 1) + q // 2 + 1)
                to = PS[:, 4 + q // 2, (q % 2) * 128:(q % 2) * 128 + 128]
                states = STATE // 2 if q == 3 else STATE
                for n in range(states):
                    mm = pe.matmul(to, ident[:], hbuf[v % 3][:, :, n, :], start=(n == 0), stop=(n == states - 1))
                mm.then_inc(m_y, 1)

            pe.wait_ge(m_r1, UNITS)
            pe.wait_ge(m_bsc, 2)
            pe.wait_ge(m_se, 8)
            for B in range(4):
                form_inputs(B)
            for v in range(4 * UNITS):
                if v + 2 < 4 * UNITS:
                    form_inputs(2 * v + 4)
                    form_inputs(2 * v + 5)
                sum_states(v)
            pe.wait_ge(m_scan, 8 * UNITS)
            pe.wait_ge(m_g, 2 * CTILES)
            for t in range(TILES):
                for c in range(CTILES):
                    mm = pe.matmul(PS[:, t, 0:DIM], zgate[:, c, t * 128:t * 128 + 128], m_out[:, c, :],
                                   start=(c == 0), stop=(c == CTILES - 1))
                mm.then_inc(m_o, 1)

            keep_warm(20)
            ln_tensor(4, 6, 7)
            keep_warm(12, bank=5)
            pe.wait_ge(p_lo, 12)
            pe.wait_ge(s_xta, 4)
            pe.wait_ge(s_xtb, 12)
            for t in range(TILES):
                mm = x_stationary(PS[:, 2 + t, 0:384], t, q_wvh, q_wvl)
                if t % 2:
                    mm.then_inc(q_vd, 1)

            def quad_project(j):
                if j >= 1:
                    pe.wait_ge(q_q, j)
                    pe.wait_ge(q_k, j)
                if j >= 2:
                    pe.wait_ge(q_oe, j - 1)
                    pe.wait_ge(q_oo, j - 1)
                for i in range(2):
                    mm = x_moving(PS[:, i, :], q_wqkh[:, j, i], q_wqkl[:, j, i])
                mm.then_inc(q_proj, 1)

            def quad_scores(j):
                b = j % 2
                pe.wait_ge(q_q, j + 1)
                pe.wait_ge(q_k, j + 1)
                if j >= 1:
                    pe.wait_ge(q_sub, 2 * j)
                for swap in range(2):
                    for t2 in range(2):
                        for a in range(2):
                            for hd in ((0, 1, 2, 3), (1, 0, 3, 2))[swap]:
                                side, hp = hd % 2, hd // 2
                                par = (side + swap) % 2
                                img = 2 * (2 * t2 + par) + a
                                rows = slice(32 * hd, 32 * hd + 32)
                                cols = slice(img * 64, img * 64 + 64)
                                x = (t2 * 2 + a) * 64
                                mm = pe.matmul(PS[64 * side:64 * side + 64, 2 + 2 * hp + par, x:x + 64],
                                               q_qT[rows, b, cols], q_kT[rows, b, cols], start=True, stop=True,
                                               tile_position=(32 * hd, 64 * side))
                mm.then_inc(q_s, 1)

            def quad_transpose_probs(j):
                if j >= 1:
                    pe.wait_ge(q_ptc[0], j)
                    pe.wait_ge(q_ptc[1], j)
                keep_warm(14, bank=7)
                pe.wait_ge(q_p, 3 * j + 3)
                for m in range(4):
                    for t2 in range(2):
                        x = ((m % 2) * 2 + t2) * 128
                        mm = pe.transpose(PS[:, 6 + m // 2, x:x + 128],
                                          q_prob[:, j % 2, m, t2].rearrange("p a k -> p (a k)"), ident[:])
                    if m % 2:
                        mm.then_inc(q_pt, 1)

            def quad_weigh(j):
                pe.wait_ge(q_ptc[0], j + 1)
                pe.wait_ge(q_ptc[1], j + 1)
                pe.wait_ge(q_q, min(j + 2, QUADS))
                pe.wait_ge(q_k, min(j + 2, QUADS))
                if j >= 1:
                    pe.wait_ge(q_oe, j)
                    pe.wait_ge(q_oo, j)
                for hd in range(4):
                    side, hp = hd % 2, hd // 2
                    for t in range(TILES):
                        for a in range(2):
                            rows = slice(64 * a, 64 * a + 64)
                            hcol = (4 * j + hd) * 32
                            mm = pe.matmul(PS[32 * hd:32 * hd + 32, a, t * 64:t * 64 + 64],
                                           q_v[rows, t, hcol:hcol + 32],
                                           q_probT[rows, 2 * hp + t % 2, t // 2, side * 64:side * 64 + 64],
                                           start=True, stop=True, tile_position=(64 * a, 32 * hd))
                mm.then_inc(q_pv, 1)

            quad_project(0)
            pe.wait_ge(q_va, 1)
            pe.wait_ge(q_vv, 1)
            quad_project(1)
            quad_scores(0)
            for j in range(QUADS):
                quad_transpose_probs(j)
                if j + 1 < QUADS:
                    quad_scores(j + 1)
                quad_weigh(j)
                if j + 2 < QUADS:
                    quad_project(j + 2)
            pe.wait_ge(q_oe, QUADS)
            pe.wait_ge(q_oo, QUADS)
            pe.wait_ge(q_wol, 16)
            for t in range(TILES):
                for j in range(QUADS):
                    mm = pe.matmul(PS[:, t, 0:DIM], q_attnT[:, j, t * 128:t * 128 + 128], q_wo[:, j, :],
                                   start=(j == 0), stop=(j == QUADS - 1))
                mm.then_inc(q_o, 1)

            keep_warm(14)
            ln_tensor(5, 6, 7)
            keep_warm(6, bank=5)
            pe.wait_ge(g_gb, 80)
            pe.wait_ge(s_xta, 5)
            pe.wait_ge(s_xtb, 15)

            def moe1_up(e, p, first=False):
                pe.wait_ge(g_l1, 2 * e + 2)
                for m in range(3):
                    k = 2 * ((3 * p + m) % 2)
                    if not first or m == 2:
                        pe.wait_ge(g_act, 3 * e + m - 1)
                    for i in range(2):
                        c = 2 * m + i
                        mm = x_moving(PS[:, k + i, :], gw1h[p][:, c], gw1l[p][:, c])
                    mm.then_inc(g_hid, 1)

            def moe1_down(e, p):
                pe.wait_ge(g_l2, e + 1)
                pe.wait_ge(g_hl, 3 * e + 3)
                for t in range(TILES):
                    pe.wait_ge(g_acc, 2 * TILES * e + ADD_ORDER.index((t, 1)) + 1)
                    cols = slice(t * 128, t * 128 + 128)
                    for k in range(HCHUNKS):
                        last = k == HCHUNKS - 1

                        def upper_hidden():
                            return pe.matmul(PS[:, 4 + t, 0:2 * DIM], ghh[p][:, k, cols],
                                             gw2p[p][:, k].rearrange("p a n -> p (a n)"), start=(k == 0), stop=last)

                        if k == 0:
                            upper_hidden()
                        pe.matmul(PS[:, 4 + t, 0:DIM], ghl[p][:, k, cols], gw2p[p][:, k, 0], start=False, stop=False)
                        if k > 0:
                            mm = upper_hidden()
                    mm.then_inc(g_y, 1)

            moe1_up(0, 0, first=True)
            pe.wait_ge(g_rs, 3)
            router_logits(grwh, grwl).then_inc(g_lg, 1)
            pe.wait_ge(g_e, 1)
            with pe.Fori(0, EXPERTS // 2 - 1) as i:
                for p in range(2):
                    moe1_up(2 * i + p + 1, 1 - p)
                    moe1_down(2 * i + p, p)
            moe1_up(EXPERTS - 1, 1)
            moe1_down(EXPERTS - 2, 0)
            moe1_down(EXPERTS - 1, 1)


def lay_out(i):
    import numpy as np
    f = lambda a: np.ascontiguousarray(a)
    chunked = lambda a: f(a.reshape(-1, 128, a.shape[-1]).transpose(1, 0, 2))
    twice = lambda a: np.concatenate([a, a], 0)

    two_by_two = lambda v, w: f(np.stack([np.stack([m[:128], twice(m[128:])], 2) for m in (v, w)], 2))

    x = i["x"].reshape(8, 3, 8, 16, 8, 16)
    a = {"ident": np.eye(128, dtype=np.float32)}
    a["patches"] = chunked(x.transpose(1, 3, 5, 0, 2, 4).reshape(768, 512))
    a["tok_w"] = chunked(i["L0_tok_W"].reshape(192, 16, 16, 3).transpose(3, 1, 2, 0).reshape(768, 192))
    a["tok_b"] = f(i["L0_tok_b"])
    q = np.arange(128)[:, None] % 64
    a["causal"] = np.where(np.arange(64)[None, :] > q, np.float32(MASKED), np.float32(0)).astype(np.float32)

    pair = lambda w: w.reshape(6, 2, 192, 64).transpose(2, 0, 1, 3).reshape(192, 6, 128)
    wq, wk = pair(i["L0_attn_W_Q"]), pair(i["L0_attn_W_K"])
    a["a0_wqk"] = two_by_two(wq, wk)
    wv = i["L0_attn_W_V"].transpose(1, 0, 2).reshape(192, 768)
    a["a0_wv"] = f(np.stack([wv[:128], twice(wv[128:])], 1))
    a["a0_wo"] = chunked(i["L0_attn_W_O"])

    moe0_1 = lambda w: np.stack([np.stack([m[:128], twice(m[128:])], 1)
                                 for m in (w[:, :128], np.concatenate([w[:, 128:]] * 2, 1))], 1)
    moe0_2 = lambda w: np.stack([w[:128], twice(w[128:])], 1)
    a["m0_w1"] = f(np.stack([moe0_1(w) for w in [i["L0_ffn_w_fc_sh"], *i["L0_ffn_w1"]]], 0))
    a["m0_w2"] = f(np.stack([moe0_2(w) for w in [i["L0_ffn_w_proj_sh"], *i["L0_ffn_w2"]]], 0))
    a["m0_router"] = f(moe0_2(i["L0_ffn_router_w"].T))
    a["m0_bias"] = f(i["L0_ffn_balance_bias"])

    w = i["L1_attn_in_proj_w"].T
    wx, wz = w[:, :384].reshape(192, 3, 128), w[:, 384:].reshape(192, 3, 128)
    a["m_in"] = two_by_two(wx, wz)
    both = lambda name: np.stack([i["L1_attn_" + name], i["L1_attn_" + name + "_b"]], 0)
    per_channel = lambda v: f(v.reshape(2, 3, 128, -1).transpose(2, 0, 1, 3))
    a["m_xp"] = per_channel(both("x_proj_w").transpose(0, 2, 1))
    a["m_dtw"] = f(np.stack([i["L1_attn_dt_proj_w"], i["L1_attn_dt_proj_w_b"]], 0).transpose(2, 0, 1))
    a["m_out"] = chunked(i["L1_attn_out_proj_w"].T)
    a["m_conv"] = per_channel(both("conv1d_w"))
    a["m_convb"] = per_channel(both("conv1d_bias"))[..., 0]
    a["m_dtb"] = per_channel(both("dt_proj_bias"))[..., 0]
    a["m_a"] = per_channel(both("A_log"))
    a["m_d"] = per_channel(both("D"))[..., 0]
    row = np.arange(128)
    a["m_mask"] = (row[:, None] % STEP == np.arange(STEP)[None, :]).astype(np.float32)
    sel = np.zeros((128, 8, 3, 128), np.uint16)
    for c in range(COMBOS):
        for g in range(8):
            for t in range(STEP):
                sel[g * STEP + t, g, PART_B[c], c * STEP + t] = 1
    a["m_sel"] = sel * np.uint16(0x3F80)

    w = i["L1_ffn_Wqkv"].reshape(192, 3, 12, 16)
    w = np.concatenate([w, np.zeros_like(w)], 3).reshape(192, 3, 384)
    wq, wk, wv = w[:, 0].reshape(192, 3, 128), w[:, 1].reshape(192, 3, 128), w[:, 2]
    a["a1_wqk"] = two_by_two(wq, wk)
    a["a1_wv"] = f(np.stack([wv[:128], twice(wv[128:])], 1))
    w = i["L1_ffn_Wproj"].reshape(12, 16, 192)
    a["a1_wo"] = chunked(np.concatenate([w, np.zeros_like(w)], 1).reshape(384, 192))
    w = i["L1_ffn_W1"].reshape(8, 192, 6, 128)
    a["m1_w1"] = f(np.stack([w[:, :128], np.concatenate([w[:, 128:], w[:, 128:]], 1)], 3))
    a["m1_w2"] = f(i["L1_ffn_W2"].reshape(8, 6, 128, 192).transpose(0, 2, 1, 3))
    a["m1_router"] = f(moe0_2(i["L1_ffn_Wrouter"]))
    for n in ("ln1_g", "ln1_b", "ln2_g", "ln2_b"):
        a[n] = f(i["L1_ffn_" + n])
    return a


def kernel(**inputs):
    import numpy as np
    import concourse.bacc as bacc
    from concourse.bass_utils import run_bass_kernel_spmd

    arrays = lay_out({k: np.asarray(v) for k, v in inputs.items()})
    nc = bacc.Bacc("TRN2", target_bir_lowering=False, num_devices=1)
    io = {n: nc.dram_tensor(f"in_{n}", a.shape, mybir.dt.from_np(a.dtype), kind="ExternalInput").ap()
          for n, a in arrays.items()}
    out = nc.dram_tensor("out", (TOKENS, DIM), mybir.dt.float32, kind="ExternalOutput").ap()
    build_tower(nc, io, out)
    got = run_bass_kernel_spmd(nc, [{f"in_{n}": a for n, a in arrays.items()}], core_ids=[0])
    return got.results[0]["out"].reshape(BATCH, TOKENS_PER_IMAGE, DIM)
```
